# Optimizing a Trainium2 kernel written in Bass

```python
import numpy as np
import jax
import jax.numpy as jnp

def _softmax(x, axis=-1):
    return jax.nn.softmax(x, axis=axis)

def _gelu(x):
    return jax.nn.gelu(x, approximate=True)

def _silu(x):
    return jax.nn.silu(x)

def _sigmoid(x):
    return jax.nn.sigmoid(x)

def _layernorm(x, axis=-1, eps=1e-05):
    m = jnp.mean(x, axis=axis, keepdims=True)
    v = jnp.var(x, axis=axis, keepdims=True)
    return (x - m) / jnp.sqrt(v + eps)

def _scatter_add(tgt, idx, src, axis=0):
    return tgt.at[idx].add(src)

def _segment_sum(src, seg, n):
    return jax.ops.segment_sum(src, seg, n)
kernel_name = 'mk_gps_d1_gnn_r8_fa51bb'

def setup_inputs(seed: int=0):
    np.random.seed(seed)
    _w = jnp.asarray

    def _rec_inputs():
        import jax
        import jax.numpy as jnp
        _gk = jax.random.key(seed)
        x = -8.776e-05 + 1 * jax.random.normal(jax.random.fold_in(_gk, 1), (1250, 512), jnp.float32)
        src = jax.random.randint(jax.random.fold_in(_gk, 2), (40000,), 0, 1250, jnp.int32)
        dst = jax.random.randint(jax.random.fold_in(_gk, 3), (40000,), 0, 1250, jnp.int32)
        _o = jnp.argsort(dst, stable=True)
        src = src[_o]
        dst = dst[_o]
        edge_type_4 = jax.random.randint(jax.random.fold_in(_gk, 12), (40000,), 0, 4, jnp.int32)
        return (x, src, dst, edge_type_4)
    x, src, dst, edge_type_4 = _rec_inputs()

    def _L0_gnn_setup():
        import jax, jax.numpy as jnp
        import numpy as np
        N = 1250
        E = 20000
        DIM = 512
        R = 4
        EPS = 1e-05

        def layer_norm(h, w, b):
            mu = jnp.mean(h, axis=-1, keepdims=True)
            var = jnp.mean((h - mu) ** 2, axis=-1, keepdims=True)
            return (h - mu) * jax.lax.rsqrt(var + EPS) * w + b
        key = jax.random.key(seed)
        ks = jax.random.split(key, 12)
        s = 0.02
        inp = {'x': jax.random.normal(ks[0], (N, DIM), dtype=jnp.float32), 'edge_index': jax.random.randint(ks[1], (2, E), 0, N, dtype=jnp.int64), 'edge_type': jax.random.randint(ks[2], (E,), 0, R, dtype=jnp.int64), 'self_W': jax.random.normal(ks[3], (DIM, DIM), dtype=jnp.float32) * s, 'self_b': jnp.zeros((DIM,), dtype=jnp.float32), 'rel_W': jax.random.normal(ks[4], (R, DIM, DIM), dtype=jnp.float32) * s, 'rel_b': jnp.zeros((R, DIM), dtype=jnp.float32), 'ln1_w': jnp.ones((DIM,), dtype=jnp.float32), 'ln1_b': jnp.zeros((DIM,), dtype=jnp.float32), 'W1': jax.random.normal(ks[5], (DIM, 2 * DIM), dtype=jnp.float32) * s, 'b1': jnp.zeros((2 * DIM,), dtype=jnp.float32), 'W2': jax.random.normal(ks[6], (2 * DIM, DIM), dtype=jnp.float32) * s, 'b2': jnp.zeros((DIM,), dtype=jnp.float32), 'ln2_w': jnp.ones((DIM,), dtype=jnp.float32), 'ln2_b': jnp.zeros((DIM,), dtype=jnp.float32)}
        return inp
    _L0_gnn_all = _L0_gnn_setup()
    _L0_gnn_in = {k: v for k, v in _L0_gnn_all.items() if k in ('self_W', 'self_b', 'rel_W', 'rel_b', 'ln1_w', 'ln1_b', 'W1', 'b1', 'W2', 'b2', 'ln2_w', 'ln2_b')}
    del _L0_gnn_all

    def _L0_mix_setup():
        import jax, jax.numpy as jnp
        import numpy as np
        DIM, HEADS, DIM_HEAD = (512, 8, 64)
        key = jax.random.key(seed)
        ks = jax.random.split(key, 9)
        B, T = (4, 512)
        s = 1.0 / np.sqrt(DIM)
        x = jax.random.normal(ks[0], (B, T, DIM), dtype=jnp.float32)
        Wq = jax.random.uniform(ks[1], (DIM, DIM), jnp.float32, -s, s)
        Wk = jax.random.uniform(ks[2], (DIM, DIM), jnp.float32, -s, s)
        Wv = jax.random.uniform(ks[3], (DIM, DIM), jnp.float32, -s, s)
        Wp = jax.random.uniform(ks[4], (DIM, DIM), jnp.float32, -s, s)
        bq = jax.random.uniform(ks[5], (DIM,), jnp.float32, -s, s)
        bk = jax.random.uniform(ks[6], (DIM,), jnp.float32, -s, s)
        bv = jax.random.uniform(ks[7], (DIM,), jnp.float32, -s, s)
        bp = jax.random.uniform(ks[8], (DIM,), jnp.float32, -s, s)
        return {'x': x, 'Wq': Wq, 'bq': bq, 'Wk': Wk, 'bk': bk, 'Wv': Wv, 'bv': bv, 'Wp': Wp, 'bp': bp}
    _L0_mix_all = _L0_mix_setup()
    _L0_mix_in = {k: v for k, v in _L0_mix_all.items() if k in ('Wq', 'bq', 'Wk', 'bk', 'Wv', 'bv', 'Wp', 'bp')}
    del _L0_mix_all

    def _L0_ffn_setup():
        import jax, jax.numpy as jnp
        import numpy as np
        DIM = 512
        FFN_DIM = 1408
        GROUP = 128
        EPS = 1e-05

        def _quantize_weight(w, group_size):
            o, i = w.shape
            wg = w.reshape(o, i // group_size, group_size)
            scale = jnp.mean(jnp.abs(wg), axis=-1, keepdims=True) + EPS
            wq = jnp.clip(jnp.round(wg / scale), -1.0, 1.0) * scale
            return wq.reshape(o, i)

        def _bitlinear(x, w, group_size=GROUP):
            wq = w + jax.lax.stop_gradient(_quantize_weight(w, group_size) - w)
            return jnp.einsum('bsd,fd->bsf', x, wq)
        key = jax.random.key(seed)
        k_x, k_g, k_u, k_d = jax.random.split(key, 4)
        x = jax.random.normal(k_x, (8, 512, DIM), dtype=jnp.float32)
        sd_in = 1.0 / np.sqrt(DIM)
        sd_ffn = 1.0 / np.sqrt(FFN_DIM)
        w_gate = jax.random.normal(k_g, (FFN_DIM, DIM), dtype=jnp.float32) * sd_in
        w_up = jax.random.normal(k_u, (FFN_DIM, DIM), dtype=jnp.float32) * sd_in
        w_down = jax.random.normal(k_d, (DIM, FFN_DIM), dtype=jnp.float32) * sd_ffn
        return {'x': x, 'w_gate': w_gate, 'w_up': w_up, 'w_down': w_down}
    _L0_ffn_all = _L0_ffn_setup()
    _L0_ffn_in = {k: v for k, v in _L0_ffn_all.items() if k in ('w_gate', 'w_up', 'w_down')}
    del _L0_ffn_all
    return {'x': x, 'src': src, 'dst': dst, 'edge_type_4': edge_type_4, 'L0_gnn_self_W': _L0_gnn_in['self_W'], 'L0_gnn_self_b': _L0_gnn_in['self_b'], 'L0_gnn_rel_W': _L0_gnn_in['rel_W'], 'L0_gnn_rel_b': _L0_gnn_in['rel_b'], 'L0_gnn_ln1_w': _L0_gnn_in['ln1_w'], 'L0_gnn_ln1_b': _L0_gnn_in['ln1_b'], 'L0_gnn_W1': _L0_gnn_in['W1'], 'L0_gnn_b1': _L0_gnn_in['b1'], 'L0_gnn_W2': _L0_gnn_in['W2'], 'L0_gnn_b2': _L0_gnn_in['b2'], 'L0_gnn_ln2_w': _L0_gnn_in['ln2_w'], 'L0_gnn_ln2_b': _L0_gnn_in['ln2_b'], 'L0_mix_Wq': _L0_mix_in['Wq'], 'L0_mix_bq': _L0_mix_in['bq'], 'L0_mix_Wk': _L0_mix_in['Wk'], 'L0_mix_bk': _L0_mix_in['bk'], 'L0_mix_Wv': _L0_mix_in['Wv'], 'L0_mix_bv': _L0_mix_in['bv'], 'L0_mix_Wp': _L0_mix_in['Wp'], 'L0_mix_bp': _L0_mix_in['bp'], 'L0_ffn_w_gate': _L0_ffn_in['w_gate'], 'L0_ffn_w_up': _L0_ffn_in['w_up'], 'L0_ffn_w_down': _L0_ffn_in['w_down']}

def reference(x, src, dst, edge_type_4, L0_gnn_self_W, L0_gnn_self_b, L0_gnn_rel_W, L0_gnn_rel_b, L0_gnn_ln1_w, L0_gnn_ln1_b, L0_gnn_W1, L0_gnn_b1, L0_gnn_W2, L0_gnn_b2, L0_gnn_ln2_w, L0_gnn_ln2_b, L0_mix_Wq, L0_mix_bq, L0_mix_Wk, L0_mix_bk, L0_mix_Wv, L0_mix_bv, L0_mix_Wp, L0_mix_bp, L0_ffn_w_gate, L0_ffn_w_up, L0_ffn_w_down):
    import jax
    import jax.numpy as jnp

    def _L0_gnn_ref(x, edge_index, edge_type, self_W, self_b, rel_W, rel_b, ln1_w, ln1_b, W1, b1, W2, b2, ln2_w, ln2_b):
        import jax, jax.numpy as jnp
        import numpy as np
        N = 1250
        E = 20000
        DIM = 512
        R = 4
        EPS = 1e-05

        def layer_norm(h, w, b):
            mu = jnp.mean(h, axis=-1, keepdims=True)
            var = jnp.mean((h - mu) ** 2, axis=-1, keepdims=True)
            return (h - mu) * jax.lax.rsqrt(var + EPS) * w + b
        n = x.shape[0]
        src, dst = (edge_index[0], edge_index[1])
        h_all = jnp.einsum('nd,rdf->nrf', x, rel_W) + rel_b
        msg = h_all[src, edge_type]
        agg = jax.ops.segment_sum(msg, dst, num_segments=n)
        deg = jax.ops.segment_sum(jnp.ones_like(dst, dtype=x.dtype), dst, num_segments=n)
        agg = agg / jnp.maximum(deg, 1.0)[:, None]
        h = x @ self_W + self_b + agg
        x1 = layer_norm(x + h, ln1_w, ln1_b)
        f = jax.nn.gelu(x1 @ W1 + b1, approximate=False) @ W2 + b2
        out = layer_norm(x1 + f, ln2_w, ln2_b)
        return out

    def _L0_mix_ref(x, Wq, bq, Wk, bk, Wv, bv, Wp, bp):
        import jax, jax.numpy as jnp
        import numpy as np
        DIM, HEADS, DIM_HEAD = (512, 8, 64)
        B, T, _ = x.shape
        H, D = (HEADS, DIM_HEAD)

        def proj(W, b):
            return (x @ W.T + b).reshape(B, T, H, D).transpose(0, 2, 1, 3)
        q = jax.nn.softmax(proj(Wq, bq), axis=-1)
        k = jax.nn.softmax(proj(Wk, bk), axis=-1)
        v = proj(Wv, bv)
        k_sum = k.sum(axis=2, keepdims=True)
        D_inv = 1.0 / (q * k_sum).sum(axis=-1, keepdims=True)
        context = jnp.einsum('bhtd,bhte->bhde', k, v)
        out = jnp.einsum('bhtd,bhde->bhte', q, context) * D_inv + q
        out = out.transpose(0, 2, 1, 3).reshape(B, T, H * D)
        return out @ Wp.T + bp

    def _L0_ffn_ref(x, w_gate, w_up, w_down):
        import jax, jax.numpy as jnp
        import numpy as np
        DIM = 512
        FFN_DIM = 1408
        GROUP = 128
        EPS = 1e-05

        def _quantize_weight(w, group_size):
            o, i = w.shape
            wg = w.reshape(o, i // group_size, group_size)
            scale = jnp.mean(jnp.abs(wg), axis=-1, keepdims=True) + EPS
            wq = jnp.clip(jnp.round(wg / scale), -1.0, 1.0) * scale
            return wq.reshape(o, i)

        def _bitlinear(x, w, group_size=GROUP):
            wq = w + jax.lax.stop_gradient(_quantize_weight(w, group_size) - w)
            return jnp.einsum('bsd,fd->bsf', x, wq)
        gate = _bitlinear(x, w_gate)
        up = _bitlinear(x, w_up)
        h = jax.nn.silu(gate) * up
        return _bitlinear(h, w_down)
    edge_index = jnp.stack([src, dst])
    xn = _layernorm(x, axis=-1)
    x = x + _L0_gnn_ref(xn, edge_index, edge_type_4, L0_gnn_self_W, L0_gnn_self_b, L0_gnn_rel_W, L0_gnn_rel_b, L0_gnn_ln1_w, L0_gnn_ln1_b, L0_gnn_W1, L0_gnn_b1, L0_gnn_W2, L0_gnn_b2, L0_gnn_ln2_w, L0_gnn_ln2_b) + _L0_mix_ref(xn[None], L0_mix_Wq, L0_mix_bq, L0_mix_Wk, L0_mix_bk, L0_mix_Wv, L0_mix_bv, L0_mix_Wp, L0_mix_bp)[0]
    x = x + _L0_ffn_ref(_layernorm(x, axis=-1)[None], L0_ffn_w_gate, L0_ffn_w_up, L0_ffn_w_down)[0]
    return x

_drawn_inputs = setup_inputs


def setup_inputs(seed=0):
    import zlib

    import numpy as np

    out = dict(_drawn_inputs(seed))
    spreads = {'L0_gnn_self_b': (0.0, 0.1),
     'L0_gnn_rel_b': (0.0, 0.323),
     'L0_gnn_ln1_w': (1.0, 0.2),
     'L0_gnn_ln1_b': (0.0, 0.1),
     'L0_gnn_b1': (0.0, 0.429),
     'L0_gnn_b2': (0.0, 0.1),
     'L0_gnn_ln2_w': (1.0, 0.2),
     'L0_gnn_ln2_b': (0.0, 0.1)}
    factors = {'L0_mix_Wq': 8.0,
     'L0_mix_bq': 8.0,
     'L0_mix_Wk': 8.0,
     'L0_mix_bk': 8.0,
     'L0_mix_Wv': 8.0,
     'L0_mix_bv': 7.574,
     'L0_mix_Wp': 4.126,
     'L0_mix_bp': 4.413}
    for name, (base, spread) in spreads.items():
        noise = np.random.default_rng([zlib.crc32(name.encode()), seed]).standard_normal(out[name].shape)
        drawn = base * np.exp(spread * noise) if base else spread * noise
        out[name] = jnp.asarray(drawn.astype(out[name].dtype))
    for name, factor in factors.items():
        out[name] = (out[name] * factor).astype(out[name].dtype)
    return out
```

```python
from contextlib import ExitStack

import numpy as np
import concourse.bass as bass
from concourse import mybir

F32, F32R, F16, I32 = mybir.dt.float32, mybir.dt.float32r, mybir.dt.float16, mybir.dt.int32
ALU, ACT, AX = mybir.AluOpType, mybir.ActivationFunctionType, mybir.AxisListType

EPS = 1e-5
N, D, E, R, HEADS = 1250, 512, 40000, 4, 8
P = 128
T, NT = 10, 125
C = D // P
DH = D // HEADS
FF1, FFN = 2 * D, 1408
K1, KF = FF1 // P, FFN // P
GROUPS_PER_TILE, GW = 4, 32
G = T * GROUPS_PER_TILE
ETILES = (E + P - 1) // P
EB = (ETILES + P - 1) // P
ROUND, HALF = 10, 5
KEY = 2048
NO_DST = 4095.0
XSCALE = 1024.0
CH = [(0, 418), (418, 834), (834, 1250)]
CHW = 418


def program(nc, a, out):
    x, src, dst, typ = a["x"], a["src"], a["dst"], a["edge_type_4"]
    xg = nc.dram_tensor("xn_parts", (N, 2 * D), F16).ap()

    top = ExitStack()
    with top:
        def sem(name):
            return top.enter_context(nc.semaphore(name))

        def tensors(stack):
            return lambda name, shape, dt=F32: stack.enter_context(nc.sbuf_tensor(name, shape, dt))

        bank = [top.enter_context(nc.psum_tensor(f"bank{i}", [P, 512], F32)) for i in range(8)]

        sb = tensors(top)
        ident = sb("ident", [P, P])
        epsc = sb("epsc", [P, 1])
        bmask = sb("bmask", [P, P])
        ctxbd = sb("ctxbd", [P, 4, P])
        ksumbd = sb("ksumbd", [P, 4, P])
        b1c = sb("b1c", [P, K1])
        lnst = sb("lnst", [NT, T, 6])
        lnmv = sb("lnmv", [NT, T, 2])
        lnsd = sb("lnsd", [NT, T])
        lnrs = sb("lnrs", [NT, T])
        st = ExitStack()
        sb = tensors(st)
        xs2 = sb("xs2", [NT, 2, D])
        wrawA = [sb(f"wrawA{s}", [P, K1 * P]) for s in range(2)]
        tmpA = [sb(f"tmpA{s}", [P, CHW]) for s in range(2)]
        st.close()
        sb = tensors(top)
        yx = sb("yx", [NT, T, D])
        qs = sb("qs", [P, 4, KF])

        low = ExitStack()
        sb = tensors(low)
        xn = sb("xn", [NT, T, D])
        qT = sb("qT", [P, C, N])

        st = ExitStack()
        sb = tensors(st)
        wstage = sb("wstage", [P, 3, C, D])
        xgst = sb("xgst", [NT, 2, 2 * D], F16)
        ei = sb("ei", [P, 3, EB, P], I32)
        ekey = sb("ekey", [P, EB, P])
        esrc = sb("esrc", [P, EB, P])
        edst = sb("edst", [P, EB, P])
        emin = sb("emin", [P, EB])
        emax = sb("emax", [P, EB])
        gbi = sb("gbi", [P, G + 1], I32)
        tni = sb("tni", [P, EB], I32)
        tn = sb("tn", [P, EB])
        tnr = sb("tnr", [P, EB])
        ga = sb("ga", [P, G + 1])
        gv = sb("gv", [P, EB, 2, G + 1])
        gm = sb("gm", [2 * (G + 1), 1])
        gr = sb("gr", [1, 2 * (G + 1)])
        ikey = sb("ikey", [P, P], I32)
        st.close()

        st = ExitStack()
        sb = tensors(st)
        ST = sb("ST", [P, C, R, P])
        S_sb = sb("S_sb", [P, 2, D])
        t1 = sb("t1", [NT, D])
        y1 = sb("y1", [NT, D])
        qf = sb("qf", [NT, D])
        kf = sb("kf", [NT, D])
        relW = sb("relW", [P, R * C, D])
        vf = sb("vf", [NT, 4, 130])
        wqkv = sb("wqkv", [P, C, 3, D])
        selfW = sb("selfW", [P, C, D])
        ring = sb("ring", [P, ROUND, 2 * D], F16)
        bcast = {n: sb("b_" + n, [NT, D]) for n in ("bq", "bk", "bv", "self_b", "ln1_w", "ln1_b")}
        relb = sb("relb", [P, D])
        xs = sb("xs", [NT, D])
        xT = sb("xT", [P, C, NT])
        oh = sb("oh", [P, 2, HALF, P], F16)
        keyT = sb("keyT", [P, EB * P])
        srcT = sb("srcT", [P, EB * P], I32)
        idx = sb("idx", [P, 2, HALF], I32)
        gb = sb("gb", [P, G + 1])
        bounds = sb("bounds", [1, 2 * (G + 1)], I32)
        iotaK = sb("iotaK", [P, P])
        iotaG = sb("iotaG", [P, P])
        gmask = sb("gmask", [P, 4, GW])
        gmi = sb("gmi", [P, 4, GW], I32)
        cntb = sb("cntb", [P, GW])
        cntT = sb("cntT", [P, GW])
        A = sb("A", [P, 4, GW])
        zero16 = sb("zero16", [P, D], F16)
        one16 = sb("one16", [P, 2], F16)
        ones = sb("ones", [P, 2])
        mxq = sb("mxq", [NT, HEADS])
        mxk = sb("mxk", [NT, HEADS])
        smq = sb("smq", [NT, HEADS])
        smk = sb("smk", [NT, HEADS])
        rdeg = sb("rdeg", [NT, 1])
        st6 = sb("st6", [NT, 6])
        mv = sb("mv", [NT, 2])
        sd = sb("sd", [NT, 1])
        rs = sb("rs", [NT, 1])
        st.close()

        st = ExitStack()
        sb = tensors(st)
        x1h = sb("x1h", [P, C, N], F32R)
        x1l = sb("x1l", [P, C, N], F32R)
        gh = sb("gh", [P, K1, N], F32R)
        gl = sb("gl", [P, K1, N], F32R)
        whA = [sb(f"whA{s}", [P, K1 * P], F32R) for s in range(2)]
        wlA = [sb(f"wlA{s}", [P, K1 * P], F32R) for s in range(2)]
        outTA = sb("outTA", [P, N])
        st.close()

        st = ExitStack()
        sb = tensors(st)
        ah = sb("ah", [P, C, N], F32R)
        al = sb("al", [P, C, N], F32R)
        rd = [sb(f"rd{s}", [P, CHW]) for s in range(2)]
        at = [sb(f"at{s}", [P, CHW]) for s in range(2)]
        wrawP = [sb(f"wrawP{s}", [P, C * P]) for s in range(2)]
        whP = [sb(f"whP{s}", [P, C * P], F32R) for s in range(2)]
        wlP = [sb(f"wlP{s}", [P, C * P], F32R) for s in range(2)]
        outTP = sb("outTP", [P, N])
        bcast2 = {n: sb("c_" + n, [NT, D]) for n in ("b2", "ln2_w", "ln2_b", "bp")}
        st.close()
        low.close()

        st = ExitStack()
        sb = tensors(st)
        hh = sb("hh", [P, KF, N], F32R)
        hl = sb("hl", [P, KF, N], F32R)
        up = ExitStack()
        sb = tensors(up)
        xs3 = sb("xs3", [NT, 2, D])
        nh = sb("nh", [P, C, N], F32R)
        nl = sb("nl", [P, C, N], F32R)
        wrawF = [sb(f"wrawF{s}", [P, C * P]) for s in range(2)]
        wqF = [sb(f"wqF{s}", [P, C * P]) for s in range(2)]
        wnF = sb("wnF", [P, C * P])
        whF = [sb(f"whF{s}", [P, C * P], F32R) for s in range(2)]
        wlF = [sb(f"wlF{s}", [P, C * P], F32R) for s in range(2)]
        sg = [sb(f"sg{s}", [P, CHW]) for s in range(3)]
        hf = [sb(f"hf{s}", [P, CHW]) for s in range(3)]
        up.close()
        sb = tensors(st)
        wrawD = [sb(f"wrawD{s}", [P, KF * P]) for s in range(2)]
        wqD = [sb(f"wqD{s}", [P, KF * P]) for s in range(2)]
        wnD = sb("wnD", [P, KF * P])
        whD = [sb(f"whD{s}", [P, KF * P], F32R) for s in range(2)]
        wlD = [sb(f"wlD{s}", [P, KF * P], F32R) for s in range(2)]
        outTD = sb("outTD", [P, N])
        st.close()

        N_CONSTS = 9
        QSTEPS = 7
        N_BOUND = 5 + 4 * EB

        s = {}

        def S(name):
            if name not in s:
                s[name] = sem(name)
            return s[name]

        xg_stored = [S("xg_stored0"), S("xg_stored1")]
        gathered = [S(f"gathered{k}") for k in range(ROUND)]

        PER_TILE = dict(
            xs_ready=1, xnT_ps=1, xT_ready=1, q_ps=1, k_ps=1, v_ps=1, self_ps=1,
            q_biased=1, k_biased=1, v_biased=1, self_added=1, q_shift=1, k_shift=1, q_exp=1, k_exp=1,
            q_soft=1, k_soft=1, qT_ps=1, qT_saved=1, ctx_done=1,
            group_done=4, S_saved=8, ST_ps=4, ST_saved=4, cnt_ready=1, A_ready=1, rel_done=1, y_ready=1,
            var_ready=1, sd_ready=1, x1_ready=1, soft_step=6, tail_step=7)

        def cur(name, i, k=1):
            return PER_TILE[name] * (i + 1) + k

        def prev(name, i):
            return PER_TILE[name] * (i + 1)

        def start_credit(eng, names):
            for n in names:
                eng.sem_inc(S(n), PER_TILE[n])

        def transposes(dst_bank, src_of, n, rows, cols, width):
            for c in range(n):
                last = nc.tensor.transpose(dst_bank[0:cols, c * width:c * width + rows], src_of(c), ident[0:rows, 0:rows])
            return last

        def bview(b, n, w):
            return b[:, 0:n * w].rearrange("p (c w) -> p c w", c=n)

        TS, QK, SPS, AGG, CTX = bank[1], (bank[2], bank[3]), bank[4], bank[5], (bank[6], bank[7])
        TP = bank[0]
        SUMT = (TS, bank[3], TS, TS)
        CNT = bank[0][:, 504:505]
        DEG = bank[0][0:NT, 506:508]
        MARK = bank[0][:, 508:509]

        CREDIT = 4
        PASS_COUNTS = dict(loaded=0) | {k: CREDIT for k in ("whi", "wlo", "mm", "wT", "quant", "outT", "backT", "backed", "used")}

        class Pass:
            def __init__(self, name, U, K, src, raw, h, l, act, mode, q=None, wn=None, outT=None):
                self.name, self.U, self.K, self.src, self.raw, self.h, self.l = name, U, K, src, raw, h, l
                self.act, self.mode, self.q, self.wn, self.outT = act, mode, q, wn, outT
                self.transposed = mode in ("gateup", "down", "mix")
                self.chunks = [(k, min(k + 4, K)) for k in range(0, K, 4)] if self.transposed else [(0, K)]
                self.back = mode in ("down", "mix", "w2")
                self.raw_free = "quant" if q else "wT" if self.transposed else "wlo"
                n = len(self.chunks)
                self.per = dict(loaded=16, whi=n, wlo=n, mm=3)
                self.per |= dict(wT=n) if self.transposed else {}
                self.per |= dict(quant=1) if q else {}
                self.per |= dict(outT=3, backT=3, backed=3) if self.back else dict(used=3)
                self.base = dict(PASS_COUNTS)
                for k, m in self.per.items():
                    PASS_COUNTS[k] += m * U

            def s(self, what, slot):
                return S(f"pass_{what}{slot}")

            def cur(self, what, u, k=None):
                m = self.per[what]
                return u * m + (self.base[what] + (m if k is None else k))

            def prev(self, what, u):
                return u * self.per[what] + self.base[what]

        w1_src = lambda u, sl: a["L0_gnn_W1"].rearrange("(c p) f -> p c f", p=P)[:, :, bass.ds((2 * u + sl) * P, P)]
        w2_src = lambda u, sl: a["L0_gnn_W2"].rearrange("(c p) f -> p c f", p=P)[:, :, bass.ds((2 * u + sl) * P, P)]
        wp_src = lambda u, sl: a["L0_mix_Wp"][bass.ds((2 * u + sl) * P, P), :]
        gu_src = lambda u, sl: a[("L0_ffn_w_gate", "L0_ffn_w_up")[sl]][bass.ds(u * P, P), :]
        wd_src = lambda u, sl: a["L0_ffn_w_down"][bass.ds((2 * u + sl) * P, P), :]
        W1 = Pass("w1", 4, C, w1_src, wrawA, whA, wlA, (x1h, x1l), "gelu")
        W2 = Pass("w2", 2, K1, w2_src, wrawA, whA, wlA, (gh, gl), "w2", outT=outTA)
        WP = Pass("wp", 2, C, wp_src, wrawP, whP, wlP, (ah, al), "mix", outT=outTP)
        GU = Pass("gu", KF, C, gu_src, wrawF, whF, wlF, (nh, nl), "gateup", q=wqF, wn=wnF)
        WD = Pass("wd", 2, KF, wd_src, wrawD, whD, wlD, (hh, hl), "down", q=wqD, wn=wnD, outT=outTD)
        TB = (bank[6], bank[7])
        MB = ((bank[0], bank[1], bank[2]), (bank[3], bank[4], bank[5]))

        def pass_credit(eng, whats):
            for w in whats:
                for sl in range(2):
                    eng.sem_inc(S(f"pass_{w}{sl}"), CREDIT)

        BACK = [(0, 4), (4, 8), (8, 10)]

        def tb_of(p, sl, ci):
            return (sl * len(p.chunks) + ci) % 2

        block = top.enter_context(nc.Block())

        @block.sync
        def _(sp):
            xv = x.rearrange("(t p) f -> p t f", p=NT)
            sp.dma_start(xn[0:112, :, :], xv[0:112, :, :]).then_inc(S("x_loaded"), 16)
            sp.dma_start(xn[112:NT, :, :], xv[112:NT, :, :]).then_inc(S("x_loaded"), 16)
            sp.wait_ge(S("epad"), 1)
            full = (EB - 1) * P
            rest = E // P - full
            for n, v in enumerate((src, dst, typ)):
                sp.dma_start(ei[:, n, 0:EB - 1, :], v[0:full * P].rearrange("(b t e) -> t b e", t=P, e=P)).then_inc(S("edges_loaded"), 16)
                sp.dma_start(ei[0:rest, n, EB - 1, :], v[full * P:(full + rest) * P].rearrange("(t e) -> t e", e=P)).then_inc(S("edges_loaded"), 16)
                sp.dma_start(ei[rest:rest + 1, n, EB - 1, 0:E % P], v[(full + rest) * P:E].rearrange("(t e) -> t e", t=1)).then_inc(S("edges_loaded"), 16)
            for n, m in enumerate(("q", "k", "v")):
                sp.dma_start(wstage[:, n, :, :], a["L0_mix_W" + m].rearrange("(b p) f -> p b f", p=P)).then_inc(S(f"w{m}_loaded"), 16)
            for t in range(T):
                sp.wait_ge(S("xlo_ready"), t + 1)
                sp.wait_ge(S("xhi_ready"), t + 1)
                sp.dma_start(xg[t * NT:(t + 1) * NT, :], xgst[:, t % 2, :]).then_inc(xg_stored[t % 2], 16)
            for n, v in (("bq", "L0_mix_bq"), ("bk", "L0_mix_bk"), ("bv", "L0_mix_bv"),
                         ("self_b", "L0_gnn_self_b"), ("ln1_w", "L0_gnn_ln1_w"), ("ln1_b", "L0_gnn_ln1_b")):
                sp.dma_start(bcast[n][:, :], a[v].rearrange("(o f) -> o f", o=1).broadcast_to([NT, D])).then_inc(S("biases_loaded"), 16)
            for r in range(R):
                sp.dma_start(relb[r * GW:(r + 1) * GW, :], a["L0_gnn_rel_b"][r:r + 1, :].broadcast_to([GW, D])).then_inc(S("biases_loaded"), 16)
            sp.dma_start(selfW[:, :, :], a["L0_gnn_self_W"].rearrange("(c p) f -> p c f", p=P)).then_inc(S("selfW_loaded"), 16)
            sp.dma_start(b1c[:, :], a["L0_gnn_b1"].rearrange("(c p) -> p c", p=P), allow_slow_non_contiguous=True).then_inc(S("biases_loaded"), 16)
            sp.wait_ge(S("wT_ps"), 3 * C)
            sp.wait_ge(S("bound_int"), 1)
            sp.wait_ge(S("edge_out"), 2)
            sp.wait_ge(S("consts_vec"), N_CONSTS)
            for k in range(2):
                sp.wait_ge(xg_stored[k], 16 * T // 2)
            sp.dma_start(relW[:, :, :], a["L0_gnn_rel_W"].rearrange("r (c p) f -> p (r c) f", p=P)).then_inc(S("relW_loaded"), 16)

            def load_pass(p):
                with sp.Fori(0, p.U) as u:
                    for sl in range(2):
                        sp.wait_ge(p.s(p.raw_free, sl), p.prev(p.raw_free, u))
                        dst_ap = p.raw[sl][:, 0:p.K * P]
                        if not p.transposed:
                            dst_ap = dst_ap.rearrange("p (k f) -> p k f", k=p.K)
                        sp.dma_start(dst_ap, p.src(u, sl)).then_inc(p.s("loaded", sl), 16)

            sp.wait_ge(S("rel_done"), cur("rel_done", T - 1))
            sp.wait_ge(S("x1_ready"), cur("x1_ready", T - 1))
            sp.wait_ge(S("sd_ready"), cur("sd_ready", T - 1))
            sp.wait_ge(S("ctx_bd_ready"), 1)
            load_pass(W1)
            load_pass(W2)
            for sl in range(2):
                sp.wait_ge(W2.s("backed", sl), W2.cur("backed", W2.U - 1))
            sp.dma_start(yx[0:112, :, :], xv[0:112, :, :]).then_inc(S("x_again"), 16)
            sp.dma_start(yx[112:NT, :, :], xv[112:NT, :, :]).then_inc(S("x_again"), 16)
            for n in bcast2:
                v = {"b2": "L0_gnn_b2", "ln2_w": "L0_gnn_ln2_w", "ln2_b": "L0_gnn_ln2_b", "bp": "L0_mix_bp"}[n]
                sp.dma_start(bcast2[n][:, :], a[v].rearrange("(o f) -> o f", o=1).broadcast_to([NT, D])).then_inc(S("bias2_loaded"), 16)
            load_pass(WP)
            for sl in range(2):
                sp.wait_ge(WP.s("backed", sl), WP.cur("backed", WP.U - 1))
            sp.wait_ge(S("ln2_done"), T)
            load_pass(GU)
            for sl in range(2):
                sp.wait_ge(GU.s("mm", sl), GU.cur("mm", GU.U - 1))
            sp.wait_ge(S("plo"), 3 * W1.U * 2 + 2 + 3 * GU.U)
            load_pass(WD)
            ov = out.rearrange("(t p) f -> p t f", p=NT)
            for o in range(2 * WD.U):
                sp.wait_ge(WD.s("backed", o % 2), WD.cur("backed", o // 2))
                sp.dma_start(ov[0:112, :, o * P:(o + 1) * P], yx[0:112, :, o * P:(o + 1) * P]).then_inc(S("out_stored"), 16)
                sp.dma_start(ov[112:NT, :, o * P:(o + 1) * P], yx[112:NT, :, o * P:(o + 1) * P]).then_inc(S("out_stored"), 16)
            sp.wait_ge(S("out_stored"), 16 * 4 * WD.U)


        @block.gpsimd
        def _(pool):
            nc.gpsimd.memset(ident[:, :], 0.0).then_inc(S("consts_mem"), 1)
            nc.gpsimd.memset(bmask[:, :], 0.0).then_inc(S("consts_mem"), 1)
            pool.wait_ge(S("consts_mem"), 2)
            nc.gpsimd.affine_select(out=ident[:, :], in_=ident[:, :], compare_op=ALU.not_equal, fill=1.0, base=0,
                                    pattern=[[-1, P]], channel_multiplier=1).then_inc(S("consts_iota"), 1)
            nc.gpsimd.iota(gbi[:, 0:G], pattern=[[NT, T], [GW, 4]], base=0, channel_multiplier=0).then_inc(S("consts_iota"), 1)
            nc.gpsimd.memset(gbi[:, G:G + 1], N).then_inc(S("consts_iota"), 1)
            nc.gpsimd.iota(tni[:, :], pattern=[[P, EB]], base=0, channel_multiplier=1).then_inc(S("consts_iota"), 1)
            nc.gpsimd.iota(ikey[:, :], pattern=[[KEY, R], [1, GW]], base=0, channel_multiplier=0).then_inc(S("consts_iota"), 1)
            nc.gpsimd.iota(gmi[:, :, :], pattern=[[-1, 4], [0, GW]], base=0, channel_multiplier=1).then_inc(S("consts_iota"), 1)

            pool.wait_ge(S("bound_int"), 1)
            pool.wait_ge(S("edge_out"), 2)
            for k in range(2):
                pool.wait_ge(xg_stored[k], 16 * T // 2)
            n = pool.alloc_register("gather_round")
            pool.reg_mov(n, 0)
            with pool.Fori(0, G) as g:
                lo = pool.value_load(bounds[0:1, bass.ds(g, 1)], min_val=0, max_val=ETILES)
                hi = pool.value_load(bounds[0:1, bass.ds(g + (G + 1), 1)], min_val=0, max_val=ETILES)
                with pool.Fori(lo, hi, ROUND) as tb:
                    m = pool.snap(n, min_val=0, max_val=G * 33)
                    for h in range(2):
                        pool.wait_ge(S("slots_used"), m * ROUND + HALF * (h + 1))
                        nc.gpsimd.tensor_copy(idx[:, h, :], srcT[:, bass.ds(tb + HALF * h, HALF)]).then_inc(S("idx_ready"), 1)
                        pool.wait_ge(S("idx_ready"), m * 2 + (h + 1))
                        pool.sem_inc(S("pool_passed"), 1)
                        for k in range(HALF):
                            slot = HALF * h + k
                            nc.gpsimd.indirect_dma_start(
                                out=ring[:, slot, :], out_offset=None, in_=xg[:, :],
                                in_offset=bass.IndirectOffsetOnAxis(ap=idx[:, h, k:k + 1], axis=0)).then_inc(gathered[slot], 16)
                    pool.reg_add(n, n, 1)

        @block.scalar
        def _(act):
            start_credit(act, ["xs_ready", "xT_ready", "q_exp", "k_exp", "qT_saved", "S_saved", "ST_saved", "sd_ready"])
            pass_credit(act, ["whi", "outT", "used"])
            act.wait_ge(S("ln0_stats"), T + 1)
            nc.scalar.activation(lnsd[:, :], lnmv[:, :, 1], ACT.Sqrt, bias=epsc[0:NT, 0:1]).then_inc(S("ln0_sd"), 1)

            def save_w(n, c):
                act.wait_ge(S("wT_ps"), n * C + c + 1)
                nc.scalar.copy(wqkv[:, c, n, :], bank[(n * C + c) % 4][:, :]).then_inc(S("wT_saved"), 1)

            for n in range(2):
                for c in range(C):
                    save_w(n, c)
            for t in range(T):
                act.wait_ge(S("xn_rows"), t + 1)
                if t >= 2:
                    act.wait_ge(xg_stored[t % 2], 16 * (t // 2))
                nc.scalar.activation(xgst[:, t % 2, 0:D], xn[:, t, :], ACT.Identity, scale=XSCALE).then_inc(S("xhi_ready"), 1)
            for c in range(C):
                save_w(2, c)

            def copy_rows(t):
                nc.scalar.copy(xs[:, :], xn[:, bass.ds(t, 1), :].rearrange("p o f -> p (o f)")).then_inc(S("xs_ready"), 1)

            def tail_sd(i):
                act.wait_ge(S("var_ready"), cur("var_ready", i))
                nc.scalar.activation(sd[:, :], mv[:, 1:2], ACT.Sqrt, bias=epsc[0:NT, 0:1]).then_inc(S("sd_ready"), 1)

            def tile(i, first):
                def save_S(j):
                    act.wait_ge(S("group_done"), cur("group_done", i, j + 1))
                    if j == 0:
                        act.wait_ge(S("cnt_ready"), prev("cnt_ready", i))
                    nc.scalar.copy(cntb[:, j:j + 1], CNT).then_inc(S("S_saved"), 1)
                    nc.scalar.activation(S_sb[:, j % 2, :], SPS[:, :], ACT.Copy, scale=1.0 / XSCALE).then_inc(S("S_saved"), 1)

                def save_ST(j):
                    act.wait_ge(S("ST_ps"), cur("ST_ps", i, j + 1))
                    nc.scalar.copy(ST[:, :, :, GW * j:GW * (j + 1)],
                                   SUMT[j][:, :].rearrange("p (c t d) -> p c t d", c=C, t=R)).then_inc(S("ST_saved"), 1)

                save_S(0)
                save_S(1)
                act.wait_ge(S("xnT_ps"), cur("xnT_ps", i))
                act.wait_ge(S("self_ps"), prev("self_ps", i))
                nc.scalar.copy(xT[:, :, :], bview(TP, C, NT)).then_inc(S("xT_ready"), 1)
                if not first:
                    act.wait_ge(S("rel_done"), cur("rel_done", i - 1))
                save_ST(0)
                save_ST(1)
                if not first:
                    tail_sd(i - 1)
                save_S(2)
                act.wait_ge(S("q_shift"), cur("q_shift", i))
                nc.scalar.activation(qf[:, :], qf[:, :], ACT.Exp).then_inc(S("q_exp"), 1)
                act.wait_ge(S("k_shift"), cur("k_shift", i))
                nc.scalar.activation(kf[:, :], kf[:, :], ACT.Exp).then_inc(S("k_exp"), 1)
                save_ST(2)
                save_S(3)
                act.wait_ge(S("qT_ps"), cur("qT_ps", i))
                nc.scalar.copy(qT[:, :, bass.ds(i * NT, NT)], bview(TP, C, NT)).then_inc(S("qT_saved"), 1)
                save_ST(3)

            copy_rows(0)
            tile(0, True)
            with act.Fori(1, T) as i:
                copy_rows(i)
                tile(i, False)
            tail_sd(T - 1)

            act.wait_ge(S("x1_ready"), cur("x1_ready", T - 1))
            act.wait_ge(S("ctx_bd_ready"), 1)
            act.wait_ge(S("rel_done"), cur("rel_done", T - 1))
            for sl in range(2):
                act.sem_inc(S(f"x1c_rows{sl}"), 1)
                act.sem_inc(S(f"x1c_hi{sl}"), 1)
            with act.Fori(0, T // 2) as u:
                for sl in range(2):
                    act.wait_ge(S(f"x1c_ps{sl}"), u + 1)
                    nc.scalar.copy(xs2[:, sl, :], xn[:, bass.ds(2 * u + sl, 1), :].rearrange("p o f -> p (o f)")).then_inc(S(f"x1c_rows{sl}"), 1)
                for sl in range(2):
                    act.wait_ge(S(f"x1c_ps{sl}"), u + 2)
                    nc.scalar.copy(x1h[:, :, bass.ds((2 * u + sl) * NT, NT)], bview(TB[sl], C, NT)).then_inc(S(f"x1c_hi{sl}"), 1)

            count = {"tmp": 0, "sil": 0}

            def weights_hi(p, u, sl):
                for ci, (k0, k1) in enumerate(p.chunks):
                    if p.transposed:
                        act.wait_ge(p.s("wT", sl), p.cur("wT", u, ci + 1))
                        source = TB[tb_of(p, sl, ci)][:, 0:(k1 - k0) * P]
                    else:
                        act.wait_ge(p.s("loaded", sl), p.cur("loaded", u))
                        source = p.raw[sl][:, 0:p.K * P]
                    if ci == 0:
                        act.wait_ge(p.s("mm", sl), p.prev("mm", u))
                    nc.scalar.copy(p.h[sl][:, k0 * P:k1 * P], source).then_inc(p.s("whi", sl), 1)

            def results(p, u, sl):
                for ch, (n0, n1) in enumerate(CH):
                    w = n1 - n0
                    if p.mode == "gelu":
                        act.wait_ge(p.s("mm", sl), p.cur("mm", u, ch + 1))
                        b = (3 * sl + ch) % 2
                        act.wait_ge(S("plo"), 6 * u + 3 * sl + ch + 1 )
                        act.sem_inc(S("act_passed"), 1)
                        nc.scalar.activation(tmpA[b][:, 0:w], MB[sl][ch][:, 0:w], ACT.Gelu,
                                             bias=b1c[:, bass.ds(2 * u + sl, 1)]).then_inc(p.s("used", sl), 1)
                        act.wait_ge(p.s("used", sl), p.cur("used", u, ch + 1))
                        nc.scalar.copy(gh[:, bass.ds(2 * u + sl, 1), n0:n1].rearrange("p o n -> p (o n)"), tmpA[b][:, 0:w]).then_inc(S("phi"), 1)
                    elif p.mode == "gateup":
                        if sl == 0:
                            act.wait_ge(p.s("mm", 0), p.cur("mm", u, ch + 1))
                            act.wait_ge(p.s("used", 1), p.cur("used", u, ch - 2))
                            nc.scalar.activation(sg[ch][:, 0:w], MB[0][ch][:, 0:w], ACT.Silu).then_inc(p.s("used", 0), 1)
                        else:
                            act.wait_ge(p.s("used", 1), p.cur("used", u, ch + 1))
                            nc.scalar.copy(hh[:, bass.ds(u, 1), n0:n1].rearrange("p o n -> p (o n)"), hf[ch][:, 0:w]).then_inc(S("sil"), 1)
                    else:
                        act.wait_ge(p.s("mm", sl), p.cur("mm", u, ch + 1))
                        if ch == 0:
                            if sl == 0:
                                act.wait_ge(p.s("backT", 1), p.prev("backT", u))
                            else:
                                act.wait_ge(p.s("backT", 0), p.cur("backT", u))
                        nc.scalar.copy(p.outT[:, n0:n1], MB[sl][ch][:, 0:w]).then_inc(p.s("outT", sl), 1)

            def run(p):
                weights_hi(p, 0, 0)

                def body(u, last):
                    weights_hi(p, u, 1)
                    results(p, u, 0)
                    if not last:
                        weights_hi(p, u + 1, 0)
                    results(p, u, 1)
                with act.Fori(0, p.U - 1) as u:
                    body(u, False)
                body(p.U - 1, True)

            act.wait_ge(S("biases_loaded"), 16 * 11)
            run(W1)
            run(W2)
            for k in range(3 * C):
                n0, n1 = CH[k % 3]
                act.wait_ge(S("attn_full"), k + 1)
                nc.scalar.copy(ah[:, k // 3, n0:n1], at[k % 2][:, 0:n1 - n0]).then_inc(S("attn_hi"), 1)
            run(WP)
            act.wait_ge(S("ln2_stats"), T)
            nc.scalar.activation(lnsd[:, :], lnmv[:, :, 1], ACT.Sqrt, bias=epsc[0:NT, 0:1]).then_inc(S("ln2_sd"), 1)
            act.wait_ge(S("ln3_stats"), T)
            nc.scalar.activation(lnsd[:, :], lnmv[:, :, 1], ACT.Sqrt, bias=epsc[0:NT, 0:1]).then_inc(S("ln3_sd"), 1)
            for sl in range(2):
                act.sem_inc(S(f"n3c_hi{sl}"), 1)
            with act.Fori(0, T // 2) as u:
                for sl in range(2):
                    act.wait_ge(S(f"n3c_ps{sl}"), u + 2)
                    nc.scalar.copy(nh[:, :, bass.ds((2 * u + sl) * NT, NT)], bview(TB[sl], C, NT)).then_inc(S(f"n3c_hi{sl}"), 1)
            run(GU)
            run(WD)

        @block.tensor
        def _(pe):
            start_credit(pe, ["xnT_ps", "q_ps", "k_ps", "v_ps", "self_ps", "qT_ps", "ctx_done", "group_done", "ST_ps", "rel_done"])
            pe.sem_inc(S("slots_used"), ROUND)
            pass_credit(pe, ["mm", "wT", "backT"])
            pe.wait_ge(S("consts_iota"), 1)

            def weights_T(n):
                pe.wait_ge(S(f"w{'qkv'[n]}_loaded"), 16)
                for c in range(C):
                    k = n * C + c
                    if k >= 4:
                        pe.wait_ge(S("wT_saved"), k - 3)
                    transposes(bank[k % 4], lambda b: wstage[:, n, b, c * P:(c + 1) * P], C, P, P, P).then_inc(S("wT_ps"), 1)

            weights_T(0)
            weights_T(1)
            pe.wait_ge(S("edge_prep"), 2)
            transposes(bank[4], lambda b: ekey[:, b, :], EB, P, P, P)
            transposes(bank[5], lambda b: esrc[:, b, :], EB, P, P, P).then_inc(S("edge_T"), 1)
            pe.wait_ge(S("bound_val"), N_BOUND)
            W2G = 2 * (G + 1)
            transposes(bank[6], lambda b: gv[:, b, :, :].rearrange("p a g -> p (a g)"), EB, P, W2G, P).then_inc(S("bound_T"), 1)
            pe.wait_ge(S("bound_max"), 1)
            nc.tensor.transpose(bank[7][0:1, 0:W2G], gm[:, 0:1], ident[0:W2G, 0:W2G]).then_inc(S("bound_T"), 1)
            weights_T(2)
            pe.wait_ge(S("consts_vec"), N_CONSTS)
            pe.wait_ge(S("bound_int"), 1)
            for b in CTX:
                nc.tensor.matmul(b[:, :], zero16[:, 0:P], zero16[:, :], start=True, stop=True, skip_group_check=True)
            pe.wait_ge(S("edge_out"), 2)
            pe.wait_ge(S("wT_saved"), 3 * C)

            n = pe.alloc_register("agg_round")
            pe.reg_mov(n, 0)
            def relations(i, r0, r1):
                for r in range(r0, r1):
                    for c in range(C):
                        nc.tensor.matmul(AGG[0:NT, :], ST[:, c, r, 0:NT], relW[:, r * C + c, :], start=r + c == 0, stop=False)

            def relation_biases(i):
                pe.wait_ge(S("A_ready"), cur("A_ready", i))
                av = A[:, :, :].rearrange("p g d -> p (g d)")[:, 0:NT]
                nc.tensor.matmul(AGG[0:NT, :], av, relb[:, :], start=False, stop=True)
                nc.tensor.matmul(DEG, av, ones[:, :], start=True, stop=True, skip_group_check=True).then_inc(S("rel_done"), 1)

            def tile(i, first):
                def neighbours(j):
                    lo = pe.value_load(bounds[0:1, bass.ds(i * 4 + j, 1)], min_val=0, max_val=ETILES)
                    hi = pe.value_load(bounds[0:1, bass.ds(i * 4 + (j + G + 1), 1)], min_val=0, max_val=ETILES)
                    pe.wait_ge(S("S_saved"), 2 * (i * 4 + j) + 8)
                    nc.tensor.matmul(SPS[:, :], zero16[:, 0:P], zero16[:, :], start=True, stop=False, skip_group_check=True)
                    if j == 0:
                        pe.wait_ge(S("qT_saved"), prev("qT_saved", i))
                    if j == 2:
                        pe.wait_ge(S("xT_ready"), cur("xT_ready", i))
                        if not first:
                            pe.wait_ge(S("y_ready"), cur("y_ready", i - 1))
                    nc.tensor.matmul(CNT, zero16[:, 0:P], zero16[:, 0:1], start=True, stop=False, skip_group_check=True)
                    with pe.Fori(lo, hi, ROUND) as tb:
                        m = pe.snap(n, min_val=0, max_val=G * 33)
                        for h in range(2):
                            pe.wait_ge(S("oh_ready"), m * 2 + (h + 3))
                            for k in range(HALF):
                                slot = HALF * h + k
                                pe.wait_ge(gathered[slot], m * 16 + 16)
                                nc.tensor.matmul(SPS[:, :], oh[:, h, k, :], ring[:, slot, 0:D], start=False, stop=False, skip_group_check=True)
                                nc.tensor.matmul(SPS[:, :], oh[:, h, k, :], ring[:, slot, D:2 * D], start=False, stop=False, skip_group_check=True)
                                nc.tensor.matmul(CNT, oh[:, h, k, :], one16[:, 0:1], start=False, stop=False,
                                                 skip_group_check=True).then_inc(S("slots_used"), 1)
                        pe.reg_add(n, n, 1)
                    nc.tensor.matmul(MARK, zero16[:, 0:P], zero16[:, 0:1], start=False, stop=True,
                                     skip_group_check=True).then_inc(S("group_done"), 1)

                def sums_T(j):
                    pe.wait_ge(S("S_saved"), 2 * (i * 4 + j) + 10)
                    transposes(SUMT[j], lambda c: S_sb[:, j % 2, c * P:(c + 1) * P], C, P, P, P).then_inc(S("ST_ps"), 1)

                def project(b, w, name):
                    for c in range(C):
                        last = nc.tensor.matmul(b[0:NT, :], xT[:, c, :], w(c), start=c == 0, stop=c == C - 1)
                    last.then_inc(S(name), 1)

                neighbours(0)
                if not first:
                    relations(i - 1, 0, R // 2)
                neighbours(1)
                pe.wait_ge(S("S_saved"), 2 * (i * 4 + 1) + 10)
                pe.wait_ge(S("xs_ready"), cur("xs_ready", i))
                transposes(TP, lambda c: xs[:, c * P:(c + 1) * P], C, NT, P, NT).then_inc(S("xnT_ps"), 1)
                if not first:
                    relations(i - 1, R // 2, R)
                    pe.wait_ge(S("xT_ready"), cur("xT_ready", i))
                    relation_biases(i - 1)
                pe.wait_ge(S("ST_saved"), prev("ST_saved", i))
                sums_T(0)
                pe.wait_ge(S("self_added"), prev("self_added", i))
                sums_T(1)
                neighbours(2)
                pe.wait_ge(S("xT_ready"), cur("xT_ready", i))
                pe.wait_ge(S("v_biased"), prev("v_biased", i))
                project(QK[0], lambda c: wqkv[:, c, 0, :], "q_ps")
                pe.wait_ge(S("ST_saved"), cur("ST_saved", i, 2))
                project(QK[1], lambda c: wqkv[:, c, 1, :], "k_ps")
                sums_T(2)
                neighbours(3)
                pe.wait_ge(S("q_biased"), cur("q_biased", i))
                project(QK[0], lambda c: wqkv[:, c, 2, :], "v_ps")
                pe.wait_ge(S("q_soft"), cur("q_soft", i))
                pe.wait_ge(S("S_saved"), 2 * (i * 4 + 3) + 10)
                transposes(TP, lambda c: qf[:, c * P:(c + 1) * P], C, NT, P, NT).then_inc(S("qT_ps"), 1)
                pe.wait_ge(S("k_biased"), cur("k_biased", i))
                project(QK[1], lambda c: selfW[:, c, :], "self_ps")
                pe.wait_ge(S("k_soft"), cur("k_soft", i))
                pe.wait_ge(S("v_biased"), cur("v_biased", i))
                for pr in range(4):
                    last = nc.tensor.matmul(CTX[pr // 2][:, 130 * (pr % 2):130 * (pr % 2) + 130], kf[:, pr * P:(pr + 1) * P], vf[:, pr, :],
                                            start=False, stop=True, skip_group_check=True)
                last.then_inc(S("ctx_done"), 1)
                pe.wait_ge(S("ST_saved"), cur("ST_saved", i, 3))
                sums_T(3)

            pe.wait_ge(S("selfW_loaded"), 16)
            tile(0, True)
            pe.wait_ge(S("relW_loaded"), 16)
            pe.wait_ge(S("biases_loaded"), 16 * 11)
            with pe.Fori(1, T) as i:
                pe.wait_ge(S("ST_saved"), prev("ST_saved", i))
                tile(i, False)
            pe.wait_ge(S("ST_saved"), cur("ST_saved", T - 1, 4))
            relations(T - 1, 0, R)
            relation_biases(T - 1)

            pe.sem_inc(S("x1c_ps0"), 1)
            pe.sem_inc(S("x1c_ps1"), 1)
            pe.wait_ge(S("ctx_bd_ready"), 1)

            def to_columns(name, rows):
                with pe.Fori(0, T // 2) as u:
                    for sl in range(2):
                        pe.wait_ge(S(f"{name}_rows{sl}"), u + 2)
                        pe.wait_ge(S(f"{name}_hi{sl}"), u + 1)
                        pe.wait_ge(S(f"{name}_lo{sl}"), u + 1)
                        transposes(TB[sl], lambda c: rows[:, sl, c * P:(c + 1) * P], C, NT, P, NT).then_inc(S(f"{name}_ps{sl}"), 1)

            to_columns("x1c", xs2)

            def weights_T2(p, u, sl):
                if not p.transposed:
                    return
                w = p.q if p.q else p.raw
                pe.wait_ge(p.s("quant", sl), p.cur("quant", u)) if p.q else pe.wait_ge(p.s("loaded", sl), p.cur("loaded", u))
                total = len(p.chunks)
                for ci, (k0, k1) in enumerate(p.chunks):
                    b = sl * total + ci
                    back = b - 2
                    if back >= 0:
                        osl, oci, ou = back // total, back % total, u
                        pe.wait_ge(p.s("whi", osl), p.cur("whi", ou, oci + 1))
                        pe.wait_ge(p.s("wlo", osl), p.cur("wlo", ou, oci + 1))
                    else:
                        osl, oci = (back + 2 * total) // total, (back + 2 * total) % total
                        pe.wait_ge(p.s("whi", osl), p.cur("whi", u, oci + 1 - total))
                        pe.wait_ge(p.s("wlo", osl), p.cur("wlo", u, oci + 1 - total))
                    if p.back:
                        pe.wait_ge(p.s("backed", sl), p.prev("backed", u))
                    last = transposes(TB[b % 2], lambda c: w[sl][:, (k0 + c) * P:(k0 + c + 1) * P], k1 - k0, P, P, P)
                    last.then_inc(p.s("wT", sl), 1)

            def products(p, u, sl):
                for ch, (n0, n1) in enumerate(CH):
                    w = n1 - n0
                    if ch == 0:
                        pe.wait_ge(p.s("whi", sl), p.cur("whi", u))
                        pe.wait_ge(p.s("wlo", sl), p.cur("wlo", u))
                    done = "outT" if p.back else "used"
                    pe.wait_ge(p.s(done, sl), p.cur(done, u, ch - 2))
                    k = 0
                    for kc in range(p.K):
                        ws = slice(kc * P, (kc + 1) * P)
                        for wgt, mov in ((p.h, p.act[0]), (p.h, p.act[1]), (p.l, p.act[0])):
                            last = nc.tensor.matmul(MB[sl][ch][:, 0:w], wgt[sl][:, ws], mov[:, kc, n0:n1],
                                                    start=k == 0, stop=k == 3 * p.K - 1)
                            k += 1
                    last.then_inc(p.s("mm", sl), 1)

            def back(p, u, sl, ahead):
                if not p.back:
                    return
                pe.wait_ge(p.s("outT", sl), p.cur("outT", u))
                for q, (t0, t1_) in enumerate(BACK):
                    total = len(p.chunks)
                    if q < 2 and p.transposed:
                        for osl in range(2):
                            at_u = u + 1 if ahead and osl == 0 else u
                            pe.wait_ge(p.s("whi", osl), p.cur("whi", at_u))
                            pe.wait_ge(p.s("wlo", osl), p.cur("wlo", at_u))
                    if sl == 0:
                        pe.wait_ge(p.s("backed", 1), p.prev("backed", u))
                    else:
                        pe.wait_ge(p.s("backed", 0), p.cur("backed", u))
                    if q == 2:
                        pe.wait_ge(p.s("backed", sl), p.cur("backed", u, 1))
                    for t in range(t0, t1_):
                        last = nc.tensor.transpose(TB[q % 2][0:NT, (t - t0) * P:(t - t0 + 1) * P],
                                                   p.outT[:, t * NT:(t + 1) * NT], ident[:, :])
                    last.then_inc(p.s("backT", sl), 1)

            def run(p):
                weights_T2(p, 0, 0)

                def body(u, last):
                    weights_T2(p, u, 1)
                    products(p, u, 0)
                    back(p, u, 0, False)
                    if not last:
                        weights_T2(p, u + 1, 0)
                    products(p, u, 1)
                    back(p, u, 1, not last)
                with pe.Fori(0, p.U - 1) as u:
                    body(u, False)
                body(p.U - 1, True)

            for sl in range(2):
                pe.wait_ge(S(f"x1c_hi{sl}"), T // 2 + 1)
                pe.wait_ge(S(f"x1c_lo{sl}"), T // 2 + 1)
            run(W1)
            pe.wait_ge(S("phi"), 3 * 2 * W1.U)
            pe.wait_ge(S("plo"), 3 * 2 * W1.U + 2)
            run(W2)
            for sl in range(2):
                pe.wait_ge(W2.s("backed", sl), W2.cur("backed", W2.U - 1))
            for k in range(3 * C):
                n0, n1 = CH[k % 3]
                if k >= 2:
                    pe.wait_ge(S("attn_nd"), 2 * (k - 1))
                nc.tensor.matmul(MB[0][k % 2][:, 0:n1 - n0], ksumbd[:, k // 3, :], qT[:, k // 3, n0:n1], start=True, stop=True)
                nc.tensor.matmul(MB[1][k % 2][:, 0:n1 - n0], ctxbd[:, k // 3, :], qT[:, k // 3, n0:n1], start=True, stop=True).then_inc(S("attn_rd"), 1)
            pe.wait_ge(S("attn_nd"), 2 * 3 * C)
            pe.wait_ge(S("attn_hi"), 3 * C)
            pe.wait_ge(S("attn_lo"), 3 * C)
            run(WP)
            for sl in range(2):
                pe.wait_ge(WP.s("backed", sl), WP.cur("backed", WP.U - 1))
                pe.sem_inc(S(f"n3c_ps{sl}"), 1)
            to_columns("n3c", xs3)
            for sl in range(2):
                pe.wait_ge(S(f"n3c_hi{sl}"), T // 2 + 1)
                pe.wait_ge(S(f"n3c_lo{sl}"), T // 2 + 1)
            run(GU)
            pe.wait_ge(S("sil"), 3 * GU.U)
            pe.wait_ge(S("plo"), 3 * 2 * W1.U + 2 + 3 * GU.U)
            run(WD)

        @block.vector
        def _(dve):
            V = nc.vector
            start_credit(dve, ["q_biased", "k_biased", "v_biased", "self_added", "q_shift", "k_shift", "q_soft", "k_soft",
                               "cnt_ready", "A_ready", "y_ready", "var_ready", "x1_ready", "soft_step", "tail_step"])
            dve.sem_inc(S("oh_ready"), 2)
            dve.sem_inc(S("plo"), 2)
            dve.sem_inc(S("quant_step"), QSTEPS)
            pass_credit(dve, ["wlo", "backed", "quant"])

            V.memset(epsc[:, :], EPS)
            V.memset(ei[:, 0, EB - 1, :], 0)
            V.memset(ei[:, 2, EB - 1, :], 0)
            V.memset(ei[:, 1, EB - 1, :], int(NO_DST)).then_inc(S("epad"), 1)

            def const(ins):
                ins.then_inc(S("consts_vec"), 1)

            const(V.memset(zero16[:, :], 0.0))
            const(V.memset(one16[:, :], 1.0))
            const(V.memset(ones[:, :], 1.0))
            const(V.memset(cntb[:, :], 0.0))
            dve.wait_ge(S("consts_iota"), 6)
            const(V.tensor_copy(gb[:, :], gbi[:, :]))
            const(V.tensor_copy(iotaK[:, :], ikey[:, :]))
            const(V.tensor_copy(gmask[:, :, :], gmi[:, :, :]))
            dve.wait_ge(S("consts_vec"), 7)
            for q in range(4):
                quad = gmask[GW * q:GW * (q + 1), :, :]
                last = V.tensor_scalar(quad, quad, float(GW * q), None, ALU.is_equal)
            const(last)
            dve.wait_ge(S("consts_mem"), 2)
            V.memset(bmask[0:DH, 0:DH], 1.0)
            const(V.memset(bmask[DH:P, DH:P], 1.0))
            V.memset(vf[:, :, P:130], 1.0)

            dve.wait_ge(S("x_loaded"), 32)
            for t in range(T):
                V.bn_stats(lnst[:, t, :], xn[:, t, :]).then_inc(S("ln0_stats"), 1)
            dve.wait_ge(S("ln0_stats"), T)
            for t in range(T):
                last = V.bn_aggr(lnmv[:, t, :], lnst[:, t, :])
            last.then_inc(S("ln0_stats"), 1)

            dve.wait_ge(S("edges_loaded"), 16 * 9)
            V.scalar_tensor_tensor(ekey[:, :, :], ei[:, 2, :, :], float(KEY), ei[:, 1, :, :], ALU.mult, ALU.add).then_inc(S("edge_prep"), 1)
            V.tensor_copy(esrc[:, :, :], ei[:, 0, :, :]).then_inc(S("edge_prep"), 1)
            bv = [0]

            def bound(ins, wait=True):
                bv[0] += 1
                ins.then_inc(S("bound_val"), 1)
                if wait:
                    dve.wait_ge(S("bound_val"), bv[0])

            bound(V.tensor_reduce(emin[:, :], ei[:, 1, :, :], AX.X, ALU.min), False)
            bound(V.tensor_reduce(emax[:, :], ei[:, 1, :, :], AX.X, ALU.max), False)
            bound(V.tensor_copy(tn[:, :], tni[:, :]))
            bound(V.tensor_scalar(emin[:, :], emin[:, :], 1.0 - GW, None, ALU.add), False)
            bound(V.tensor_scalar(tnr[:, :], tn[:, :], -1.0, 400.0, ALU.mult, ALU.add))
            for b in range(EB):
                bound(V.tensor_scalar(ga[:, :], gb[:, :], emin[:, b:b + 1], None, ALU.is_ge))
                bound(V.scalar_tensor_tensor(ga[:, :], gb[:, :], emax[:, b:b + 1], ga[:, :], ALU.is_le, ALU.mult))
                bound(V.tensor_scalar(gv[:, b, 0, :], ga[:, :], tnr[:, b:b + 1], None, ALU.mult), False)
                bound(V.scalar_tensor_tensor(gv[:, b, 1, :], ga[:, :], tn[:, b:b + 1], ga[:, :], ALU.mult, ALU.add))
            assert bv[0] == N_BOUND
            dve.wait_ge(S("ln0_sd"), 1)
            V.reciprocal(lnrs[:, :], lnsd[:, :]).then_inc(S("ln0_rs"), 1)
            dve.wait_ge(S("ln0_rs"), 1)
            for t in range(T):
                V.tensor_scalar(xn[:, t, :], xn[:, t, :], lnmv[:, t, 0:1], lnrs[:, t:t + 1], ALU.subtract, ALU.mult).then_inc(S("xn_rows"), 1)
            dve.wait_ge(S("edge_T"), 1)
            V.tensor_copy(keyT[:, :], bank[4][:, 0:EB * P]).then_inc(S("edge_out"), 1)
            V.tensor_copy(srcT[:, :], bank[5][:, 0:EB * P]).then_inc(S("edge_out"), 1)
            dve.wait_ge(S("bound_T"), 1)
            V.reduce_max(gm[:, :], bank[6][0:2 * (G + 1), 0:EB * P], AX.X).then_inc(S("bound_max"), 1)
            dve.wait_ge(S("bound_T"), 2)
            V.tensor_scalar(gr[:, :], bank[7][0:1, 0:2 * (G + 1)], -1.0, 400.0, ALU.mult, ALU.add).then_inc(S("bound_row"), 1)
            dve.wait_ge(S("bound_row"), 1)
            V.tensor_scalar(bounds[:, 0:G + 1], gr[:, 0:G + 1], float(ETILES - 1), None, ALU.min)
            V.tensor_copy(bounds[:, G + 1:], bank[7][0:1, G + 1:2 * (G + 1)]).then_inc(S("bound_int"), 1)
            for t in range(T):
                dve.wait_ge(S("xhi_ready"), t + 1)
                V.scalar_tensor_tensor(xgst[:, t % 2, D:2 * D], xn[:, t, :], XSCALE, xgst[:, t % 2, 0:D],
                                       ALU.mult, ALU.subtract).then_inc(S("xlo_ready"), 1)

            n = dve.alloc_register("onehot_round")
            dve.reg_mov(n, 0)

            def onehots(g):
                lo = dve.value_load(bounds[0:1, bass.ds(g, 1)], min_val=0, max_val=ETILES)
                hi = dve.value_load(bounds[0:1, bass.ds(g + (G + 1), 1)], min_val=0, max_val=ETILES)
                m = dve.snap(n, min_val=0, max_val=G * 33)
                dve.wait_ge(S("oh_ready"), m * 2 + 2)
                V.tensor_scalar(iotaG[:, :], iotaK[:, :], gb[:, bass.ds(g, 1)], None, ALU.add).then_inc(S("iotaG_ready"), 1)
                with dve.Fori(lo, hi, ROUND) as tb:
                    m = dve.snap(n, min_val=0, max_val=G * 33)
                    for h in range(2):
                        dve.wait_ge(S("slots_used"), m * ROUND + HALF * (h + 1))
                        dve.wait_ge(S("iotaG_ready"), g + 1)
                        V.tensor_tensor(oh[:, h, :, :], iotaG[:, :].rearrange("p (o c) -> p o c", o=1).broadcast_to([P, HALF, P]),
                                        keyT[:, bass.ds(tb + HALF * h, HALF)].rearrange("p (k o) -> p k o", o=1).broadcast_to([P, HALF, P]),
                                        ALU.is_equal).then_inc(S("oh_ready"), 1)
                    dve.reg_add(n, n, 1)

            dve.wait_ge(S("edge_out"), 2)
            dve.wait_ge(S("bound_int"), 1)
            for k in range(2):
                dve.wait_ge(xg_stored[k], 16 * T // 2)
            dve.wait_ge(S("wT_ps"), 3 * C)
            dve.wait_ge(S("biases_loaded"), 16 * 11)
            onehots(0)

            def heads(v):
                return v[:, :].rearrange("p (h e) -> p h e", h=HEADS)

            def over(v):
                return v[:, :].rearrange("p (h o) -> p h o", o=1).broadcast_to([NT, HEADS, DH])

            def tail(i):
                dve.wait_ge(S("rel_done"), cur("rel_done", i))
                V.tensor_scalar(rdeg[:, :], DEG[:, 0:1], 1.0, None, ALU.max).then_inc(S("tail_step"), 1)
                dve.wait_ge(S("tail_step"), cur("tail_step", i, 2))
                V.reciprocal(rdeg[:, :], rdeg[:, :]).then_inc(S("tail_step"), 1)
                dve.wait_ge(S("tail_step"), cur("tail_step", i, 3))
                V.scalar_tensor_tensor(y1[:, :], AGG[0:NT, :], rdeg[:, 0:1], t1[:, :], ALU.mult, ALU.add).then_inc(S("y_ready"), 1)
                dve.wait_ge(S("y_ready"), cur("y_ready", i))
                V.bn_stats(st6[:, :], y1[:, :]).then_inc(S("tail_step"), 1)
                dve.wait_ge(S("tail_step"), cur("tail_step", i, 4))
                dve.sem_inc(S("dve_passed"), 1)
                V.bn_aggr(mv[:, :], st6[:, :]).then_inc(S("var_ready"), 1)
                dve.wait_ge(S("sd_ready"), cur("sd_ready", i))
                V.reciprocal(rs[:, :], sd[:, :]).then_inc(S("tail_step"), 1)
                dve.wait_ge(S("tail_step"), cur("tail_step", i, 5))
                V.tensor_scalar(y1[:, :], y1[:, :], mv[:, 0:1], rs[:, 0:1], ALU.subtract, ALU.mult).then_inc(S("tail_step"), 1)
                dve.wait_ge(S("tail_step"), cur("tail_step", i, 6))
                V.tensor_tensor(y1[:, :], y1[:, :], bcast["ln1_w"][:, :], ALU.mult).then_inc(S("tail_step"), 1)
                dve.wait_ge(S("tail_step"), cur("tail_step", i, 7))
                V.tensor_tensor(xn[:, bass.ds(i, 1), :].rearrange("p o f -> p (o f)"), y1[:, :], bcast["ln1_b"][:, :],
                                ALU.add).then_inc(S("x1_ready"), 1)

            def tile(i, first):
                def shifted(b, name, z, mx, k):
                    dve.wait_ge(S(name + "_ps"), cur(name + "_ps", i))
                    V.tensor_tensor(z[:, :], b[0:NT, :], bcast["b" + name][:, :], ALU.add).then_inc(S(name + "_biased"), 1)
                    dve.wait_ge(S(name + "_biased"), cur(name + "_biased", i))
                    V.reduce_max(mx[:, :], heads(z), AX.X).then_inc(S("soft_step"), 1)
                    dve.wait_ge(S("soft_step"), cur("soft_step", i, k))
                    V.tensor_tensor(heads(z), heads(z), over(mx), ALU.subtract).then_inc(S(name + "_shift"), 1)

                def normed(name, z, sm, k):
                    dve.wait_ge(S(name + "_exp"), cur(name + "_exp", i))
                    V.reduce_sum(sm[:, :], heads(z), AX.X).then_inc(S("soft_step"), 1)
                    dve.wait_ge(S("soft_step"), cur("soft_step", i, k))
                    V.reciprocal(sm[:, :], sm[:, :]).then_inc(S("soft_step"), 1)
                    dve.wait_ge(S("soft_step"), cur("soft_step", i, k + 1))
                    V.tensor_tensor(heads(z), heads(z), over(sm), ALU.mult).then_inc(S(name + "_soft"), 1)

                onehots(i * 4 + 1)
                onehots(i * 4 + 2)
                if not first:
                    tail(i - 1)
                onehots(i * 4 + 3)
                dve.wait_ge(S("qT_ps"), prev("qT_ps", i))
                shifted(QK[0], "q", qf, mxq, 1)
                dve.wait_ge(S("ctx_done"), prev("ctx_done", i))
                shifted(QK[1], "k", kf, mxk, 2)
                normed("q", qf, smq, 3)
                normed("k", kf, smk, 5)
                onehots(i * 4 + 4)
                dve.wait_ge(S("v_ps"), cur("v_ps", i))
                V.tensor_tensor(vf[:, :, 0:P], QK[0][0:NT, :].rearrange("p (a b) -> p a b", a=4),
                                bcast["bv"][:, :].rearrange("p (a b) -> p a b", a=4), ALU.add).then_inc(S("v_biased"), 1)
                dve.wait_ge(S("self_ps"), cur("self_ps", i))
                V.tensor_tensor(t1[:, :], QK[1][0:NT, :], bcast["self_b"][:, :], ALU.add).then_inc(S("self_added"), 1)
                dve.wait_ge(S("self_added"), cur("self_added", i))
                V.tensor_tensor(t1[:, :], t1[:, :], xn[:, bass.ds(i, 1), :].rearrange("p o f -> p (o f)"), ALU.add).then_inc(S("tail_step"), 1)
                dve.wait_ge(S("S_saved"), cur("S_saved", i, 8))
                V.transpose(cntT[:, :], cntb[:, :]).then_inc(S("cnt_ready"), 1)
                dve.wait_ge(S("cnt_ready"), cur("cnt_ready", i))
                V.tensor_tensor(A[:, :, :], gmask[:, :, :], cntT[:, :].rearrange("p (o d) -> p o d", o=1).broadcast_to([P, 4, GW]),
                                ALU.mult).then_inc(S("A_ready"), 1)

            tile(0, True)
            with dve.Fori(1, T) as i:
                tile(i, False)
            tail(T - 1)

            dve.wait_ge(S("ctx_done"), cur("ctx_done", T - 1))
            for pr in range(4):
                o = 130 * (pr % 2)
                V.tensor_tensor(ctxbd[:, pr, :], CTX[pr // 2][:, o:o + P], bmask[:, :], ALU.mult)
                last = V.tensor_scalar(ksumbd[:, pr, :], bmask[:, :], CTX[pr // 2][:, o + P:o + P + 1], None, ALU.mult)
            last.then_inc(S("ctx_bd_ready"), 1)

            def f32(v):
                return v.bitcast(F32)

            dve.wait_ge(S("rel_done"), cur("rel_done", T - 1))
            for sl in range(2):
                dve.sem_inc(S(f"x1c_lo{sl}"), 1)
            with dve.Fori(0, T // 2) as u:
                for sl in range(2):
                    nodes = bass.ds((2 * u + sl) * NT, NT)
                    dve.wait_ge(S(f"x1c_hi{sl}"), u + 2)
                    V.tensor_tensor(x1l[:, :, nodes], bview(TB[sl], C, NT), f32(x1h[:, :, nodes]), ALU.subtract).then_inc(S(f"x1c_lo{sl}"), 1)

            def weights_lo(p, u, sl):
                for ci, (k0, k1) in enumerate(p.chunks):
                    dve.wait_ge(p.s("whi", sl), p.cur("whi", u, ci + 1))
                    source = TB[tb_of(p, sl, ci)][:, 0:(k1 - k0) * P] if p.transposed else p.raw[sl][:, 0:p.K * P]
                    V.tensor_tensor(p.l[sl][:, k0 * P:k1 * P], source, f32(p.h[sl][:, k0 * P:k1 * P]), ALU.subtract).then_inc(p.s("wlo", sl), 1)

            def quantise(p, u, sl):
                if not p.q:
                    return
                step = S("quant_step")
                tiles_before = 2 * (p.base["quant"] - CREDIT)
                at_step = lambda k: u * (2 * QSTEPS) + ((tiles_before + sl + 1) * QSTEPS + k)
                w, wq, wn, K = p.raw[sl], p.q[sl], p.wn, p.K
                kv = lambda v: v[:, 0:K * P].rearrange("p (k f) -> p k f", k=K)
                dve.wait_ge(p.s("loaded", sl), p.cur("loaded", u))
                dve.wait_ge(p.s("wT", sl), p.prev("wT", u))
                dve.wait_ge(step, at_step(0))
                V.tensor_reduce(qs[:, 0, 0:K], kv(w), AX.X, ALU.add, apply_absolute_value=True).then_inc(step, 1)
                dve.wait_ge(step, at_step(1))
                V.tensor_scalar(qs[:, 1, 0:K], qs[:, 0, 0:K], 1.0 / P, EPS, ALU.mult, ALU.add).then_inc(step, 1)
                dve.wait_ge(step, at_step(2))
                V.tensor_scalar(qs[:, 2, 0:K], qs[:, 1, 0:K], 0.5, None, ALU.mult).then_inc(step, 1)
                V.tensor_scalar(qs[:, 3, 0:K], qs[:, 1, 0:K], -0.5, None, ALU.mult).then_inc(step, 1)
                dve.wait_ge(step, at_step(4))
                for k in range(K):
                    ws = slice(k * P, (k + 1) * P)
                    V.tensor_scalar(wq[:, ws], w[:, ws], qs[:, 2, k:k + 1], qs[:, 1, k:k + 1], ALU.is_gt, ALU.mult)
                    last = V.tensor_scalar(wn[:, ws], w[:, ws], qs[:, 3, k:k + 1], qs[:, 1, k:k + 1], ALU.is_lt, ALU.mult)
                last.then_inc(step, 1)
                dve.wait_ge(step, at_step(5))
                V.tensor_tensor(wq[:, 0:K * P], wq[:, 0:K * P], w[:, 0:K * P], ALU.subtract).then_inc(step, 1)
                dve.wait_ge(step, at_step(6))
                V.tensor_tensor(wq[:, 0:K * P], wq[:, 0:K * P], wn[:, 0:K * P], ALU.subtract).then_inc(step, 1)
                dve.wait_ge(step, at_step(7))
                V.tensor_tensor(wq[:, 0:K * P], wq[:, 0:K * P], w[:, 0:K * P], ALU.add).then_inc(p.s("quant", sl), 1)

            def results(p, u, sl):
                if p.mode == "gelu":
                    for ch, (n0, n1) in enumerate(CH):
                        g = (bass.ds(2 * u + sl, 1), slice(n0, n1))
                        dve.wait_ge(S("phi"), 6 * u + (3 * sl + ch + 1))
                        V.tensor_tensor(gl[:, g[0], g[1]].rearrange("p o n -> p (o n)"), tmpA[(3 * sl + ch) % 2][:, 0:n1 - n0],
                                        f32(gh[:, g[0], g[1]]).rearrange("p o n -> p (o n)"), ALU.subtract).then_inc(S("plo"), 1)
                elif p.mode == "gateup":
                    if sl == 0:
                        return
                    done = 3 * 2 * W1.U + 2
                    dve.wait_ge(S("plo"), 3 * u + done)
                    for ch, (n0, n1) in enumerate(CH):
                        w = n1 - n0
                        dve.wait_ge(p.s("used", 0), p.cur("used", u, ch + 1))
                        dve.wait_ge(p.s("mm", 1), p.cur("mm", u, ch + 1))
                        V.tensor_tensor(hf[ch][:, 0:w], MB[1][ch][:, 0:w], sg[ch][:, 0:w], ALU.mult).then_inc(p.s("used", 1), 1)
                    for ch, (n0, n1) in enumerate(CH):
                        dve.wait_ge(S("sil"), 3 * u + (ch + 1))
                        V.tensor_tensor(hl[:, bass.ds(u, 1), n0:n1].rearrange("p o n -> p (o n)"), hf[ch][:, 0:n1 - n0],
                                        f32(hh[:, bass.ds(u, 1), n0:n1]).rearrange("p o n -> p (o n)"), ALU.subtract).then_inc(S("plo"), 1)
                else:
                    rows = xn if p.mode == "w2" else yx
                    for q, (t0, t1_) in enumerate(BACK):
                        dve.wait_ge(p.s("backT", sl), p.cur("backT", u, q + 1))
                        r = rows[:, t0:t1_, bass.ds((2 * u + sl) * P, P)]
                        V.tensor_tensor(r, r, TB[q % 2][0:NT, 0:(t1_ - t0) * P].rearrange("p (t f) -> p t f", f=P),
                                        ALU.add).then_inc(p.s("backed", sl), 1)

            def run(p):
                quantise(p, 0, 0)
                quantise(p, 0, 1)
                weights_lo(p, 0, 0)

                def body(u, last):
                    weights_lo(p, u, 1)
                    if not last:
                        quantise(p, u + 1, 0)
                    results(p, u, 0)
                    if not last:
                        weights_lo(p, u + 1, 0)
                        quantise(p, u + 1, 1)
                    results(p, u, 1)
                with dve.Fori(0, p.U - 1) as u:
                    body(u, False)
                body(p.U - 1, True)

            run(W1)
            run(W2)
            steps = 3 * C

            def attention_lo(k):
                n0, n1 = CH[k % 3]
                dve.wait_ge(S("attn_hi"), k + 1)
                V.tensor_tensor(al[:, k // 3, n0:n1], at[k % 2][:, 0:n1 - n0], f32(ah[:, k // 3, n0:n1]), ALU.subtract).then_inc(S("attn_lo"), 1)

            for k in range(steps):
                n0, n1 = CH[k % 3]
                w = n1 - n0
                if k >= 2:
                    dve.wait_ge(S("attn_lo"), k - 1)
                dve.wait_ge(S("attn_rd"), k + 1)
                V.reciprocal(rd[k % 2][:, 0:w], MB[0][k % 2][:, 0:w]).then_inc(S("attn_nd"), 1)
                dve.wait_ge(S("attn_nd"), 2 * k + 1)
                V.tensor_tensor(at[k % 2][:, 0:w], MB[1][k % 2][:, 0:w], rd[k % 2][:, 0:w], ALU.mult).then_inc(S("attn_nd"), 1)
                dve.wait_ge(S("attn_nd"), 2 * k + 2)
                V.tensor_tensor(at[k % 2][:, 0:w], at[k % 2][:, 0:w], qT[:, k // 3, n0:n1], ALU.add).then_inc(S("attn_full"), 1)
                if k >= 1:
                    attention_lo(k - 1)
            attention_lo(steps - 1)
            dve.wait_ge(S("x_again"), 32)
            run(WP)

            lc = [0]

            def step(ins, wait=False):
                lc[0] += 1
                ins.then_inc(S("ln2_step"), 1)
                if wait:
                    dve.wait_ge(S("ln2_step"), lc[0])

            dve.wait_ge(S("bias2_loaded"), 64)
            for sl in range(2):
                dve.wait_ge(W2.s("backed", sl), W2.cur("backed", W2.U - 1))
                dve.wait_ge(WP.s("backed", sl), WP.cur("backed", WP.U - 1))
            step(V.tensor_tensor(bcast2["bp"][:, :], bcast2["bp"][:, :], bcast2["ln2_b"][:, :], ALU.add))
            for t in range(T):
                step(V.tensor_tensor(xn[:, t, :], xn[:, t, :], bcast2["b2"][:, :], ALU.add), t == T - 1)
            for t in range(T):
                step(V.bn_stats(lnst[:, t, :], xn[:, t, :]), t == T - 1)
            for t in range(T):
                V.bn_aggr(lnmv[:, t, :], lnst[:, t, :]).then_inc(S("ln2_stats"), 1)
            dve.wait_ge(S("ln2_sd"), 1)
            step(V.reciprocal(lnrs[:, :], lnsd[:, :]), True)
            for t in range(T):
                step(V.tensor_scalar(xn[:, t, :], xn[:, t, :], lnmv[:, t, 0:1], lnrs[:, t:t + 1], ALU.subtract, ALU.mult), t == T - 1)
            for t in range(T):
                step(V.tensor_tensor(xn[:, t, :], xn[:, t, :], bcast2["ln2_w"][:, :], ALU.mult))
                step(V.tensor_tensor(yx[:, t, :], yx[:, t, :], bcast2["bp"][:, :], ALU.add), t == T - 1)
            for t in range(T):
                V.tensor_tensor(yx[:, t, :], yx[:, t, :], xn[:, t, :], ALU.add).then_inc(S("ln2_done"), 1)
            dve.wait_ge(S("ln2_done"), T)
            for t in range(T):
                step(V.bn_stats(lnst[:, t, :], yx[:, t, :]), t == T - 1)
            for t in range(T):
                V.bn_aggr(lnmv[:, t, :], lnst[:, t, :]).then_inc(S("ln3_stats"), 1)
            dve.wait_ge(S("ln3_sd"), 1)
            step(V.reciprocal(lnrs[:, :], lnsd[:, :]), True)
            for sl in range(2):
                dve.sem_inc(S(f"n3c_rows{sl}"), 1)
                dve.sem_inc(S(f"n3c_lo{sl}"), 1)
            with dve.Fori(0, T // 2) as u:
                for sl in range(2):
                    t = 2 * u + sl
                    dve.wait_ge(S(f"n3c_ps{sl}"), u + 1)
                    V.tensor_scalar(xs3[:, sl, :], yx[:, bass.ds(t, 1), :].rearrange("p o f -> p (o f)"),
                                    lnmv[:, bass.ds(t, 1), 0:1].rearrange("p o f -> p (o f)"), lnrs[:, bass.ds(t, 1)],
                                    ALU.subtract, ALU.mult).then_inc(S(f"n3c_rows{sl}"), 1)
                for sl in range(2):
                    nodes = bass.ds((2 * u + sl) * NT, NT)
                    dve.wait_ge(S(f"n3c_hi{sl}"), u + 2)
                    V.tensor_tensor(nl[:, :, nodes], bview(TB[sl], C, NT), f32(nh[:, :, nodes]), ALU.subtract).then_inc(S(f"n3c_lo{sl}"), 1)
            run(GU)
            for sl in range(2):
                dve.wait_ge(GU.s("mm", sl), GU.cur("mm", GU.U - 1))
            run(WD)


INPUTS = ("x", "src", "dst", "edge_type_4", "L0_gnn_self_W", "L0_gnn_self_b", "L0_gnn_rel_W", "L0_gnn_rel_b", "L0_gnn_ln1_w",
          "L0_gnn_ln1_b", "L0_gnn_W1", "L0_gnn_b1", "L0_gnn_W2", "L0_gnn_b2", "L0_gnn_ln2_w", "L0_gnn_ln2_b", "L0_mix_Wq",
          "L0_mix_bq", "L0_mix_Wk", "L0_mix_bk", "L0_mix_Wv", "L0_mix_bv", "L0_mix_Wp", "L0_mix_bp", "L0_ffn_w_gate",
          "L0_ffn_w_up", "L0_ffn_w_down")


def kernel(**inputs):
    import concourse.bacc as bacc
    from concourse.bass_utils import run_bass_kernel_spmd

    nc = bacc.Bacc("TRN2", target_bir_lowering=False, num_devices=1)
    arrays, aps = {}, {}
    for name in INPUTS:
        v = np.ascontiguousarray(inputs[name])
        arrays[name] = v
        aps[name] = nc.dram_tensor(name, v.shape, mybir.dt.from_np(v.dtype), kind="ExternalInput").ap()
    out = nc.dram_tensor("out", (N, D), F32, kind="ExternalOutput").ap()
    program(nc, aps, out)
    r = run_bass_kernel_spmd(nc, [arrays], core_ids=[0])
    return r.results[0]["out"]
```

```python
from contextlib import ExitStack

import numpy as np
import concourse.bass as bass
from concourse import mybir

F32, F32R, F16, I32 = mybir.dt.float32, mybir.dt.float32r, mybir.dt.float16, mybir.dt.int32
ALU, ACT, AX = mybir.AluOpType, mybir.ActivationFunctionType, mybir.AxisListType

EPS = 1e-5
N, D, E, R, HEADS = 1250, 512, 40000, 4, 8
P = 128
T, NT = 10, 125
C = D // P
DH = D // HEADS
FF1, FFN = 2 * D, 1408
K1, KF = FF1 // P, FFN // P
GROUPS_PER_TILE, GW = 4, 32
G = T * GROUPS_PER_TILE
ETILES = (E + P - 1) // P
EB = (ETILES + P - 1) // P
ROUND, HALF = 10, 5
KEY = 2048
NO_DST = 4095.0
XSCALE = 1024.0
CH = [(0, 418), (418, 834), (834, 1250)]
CHW = 418


def program(nc, a, out):
    x, src, dst, typ = a["x"], a["src"], a["dst"], a["edge_type_4"]
    xg = nc.dram_tensor("xn_parts", (N, 2 * D), F16).ap()

    top = ExitStack()
    with top:
        def sem(name):
            return top.enter_context(nc.semaphore(name))

        def tensors(stack):
            return lambda name, shape, dt=F32: stack.enter_context(nc.sbuf_tensor(name, shape, dt))

        bank = [top.enter_context(nc.psum_tensor(f"bank{i}", [P, 512], F32)) for i in range(8)]

        sb = tensors(top)
        ident = sb("ident", [P, P])
        epsc = sb("epsc", [P, 1])
        bmask = sb("bmask", [P, P])
        st = ExitStack()
        sb = tensors(st)
        ctxbd = sb("ctxbd", [P, 4, P])
        ksumbd = sb("ksumbd", [P, 4, P])
        st.close()
        sb = tensors(top)
        wrawP = [sb(f"wrawP{s}", [P, C * P]) for s in range(2)]
        pair = sb("pair", [P, 2, P])
        b1c = sb("b1c", [P, K1])
        lnst = sb("lnst", [NT, T, 6])
        lnmv = sb("lnmv", [NT, T, 2])
        lnsd = sb("lnsd", [NT, T])
        lnrs = sb("lnrs", [NT, T])
        lnsh = sb("lnsh", [NT, T])
        st = ExitStack()
        sb = tensors(st)
        wrawA = [sb(f"wrawA{s}", [P, K1 * P]) for s in range(2)]
        tmpA = [sb(f"tmpA{s}", [P, CHW]) for s in range(2)]
        at = sb("at", [P, CHW])
        b2 = sb("b2", [NT, D])
        st.close()
        sb = tensors(top)
        yx = sb("yx", [NT, T, D])
        qs = sb("qs", [P, 5, KF])

        low = ExitStack()
        sb = tensors(low)
        xn = sb("xn", [NT, T, D])
        qT = sb("qT", [P, C, N])

        st = ExitStack()
        sb = tensors(st)
        wstage = sb("wstage", [P, 3, C, D])
        xgst = sb("xgst", [NT, 2, 2 * D], F16)
        ei = sb("ei", [P, 3, EB, P], I32)
        ekey = sb("ekey", [P, EB, P])
        esrc = sb("esrc", [P, EB, P])
        edst = sb("edst", [P, EB, P])
        emin = sb("emin", [P, EB])
        emax = sb("emax", [P, EB])
        gbi = sb("gbi", [P, G + 1], I32)
        tni = sb("tni", [P, EB], I32)
        tn = sb("tn", [P, EB])
        tnr = sb("tnr", [P, EB])
        ga = sb("ga", [P, G + 1])
        gv = sb("gv", [P, EB, 2, G + 1])
        gm = sb("gm", [2 * (G + 1), 1])
        gr = sb("gr", [1, 2 * (G + 1)])
        ikey = sb("ikey", [P, P], I32)
        st.close()

        st = ExitStack()
        sb = tensors(st)
        ST = sb("ST", [P, C, R, P])
        S_sb = sb("S_sb", [P, 2, D])
        t1 = sb("t1", [NT, D])
        y1 = sb("y1", [NT, D])
        qf = sb("qf", [NT, D])
        kf = sb("kf", [NT, D])
        relW = sb("relW", [P, R * C, D])
        vf = sb("vf", [NT, 4, 130])
        wqkv = sb("wqkv", [P, C, 3, D])
        selfW = sb("selfW", [P, C, D])
        ring = sb("ring", [P, ROUND, 2 * D], F16)
        bcast = {n: sb("b_" + n, [NT, D]) for n in ("bq", "bk", "bv", "self_b", "ln1_w", "ln1_b")}
        relb = sb("relb", [P, D])
        xs = sb("xs", [NT, D])
        xT = sb("xT", [P, C, NT])
        oh = sb("oh", [P, 2, HALF, P], F16)
        keyT = sb("keyT", [P, EB * P])
        srcT = sb("srcT", [P, EB * P], I32)
        idx = sb("idx", [P, 2, HALF], I32)
        gb = sb("gb", [P, G + 1])
        bounds = sb("bounds", [1, 2 * (G + 1)], I32)
        iotaK = sb("iotaK", [P, P])
        iotaG = sb("iotaG", [P, P])
        gmask = sb("gmask", [P, 4, GW])
        gmi = sb("gmi", [P, 4, GW], I32)
        cntb = sb("cntb", [P, GW])
        cntT = sb("cntT", [P, GW])
        A = sb("A", [P, 4, GW])
        zero16 = sb("zero16", [P, D], F16)
        one16 = sb("one16", [P, 2], F16)
        ones = sb("ones", [P, 2])
        mxq = sb("mxq", [NT, HEADS])
        mxk = sb("mxk", [NT, HEADS])
        smq = sb("smq", [NT, HEADS])
        smk = sb("smk", [NT, HEADS])
        rdeg = sb("rdeg", [NT, 1])
        st6 = sb("st6", [NT, 6])
        mv = sb("mv", [NT, 2])
        sd = sb("sd", [NT, 1])
        rs = sb("rs", [NT, 1])
        st.close()

        st = ExitStack()
        sb = tensors(st)
        x1h = sb("x1h", [P, C, N], F32R)
        x1l = sb("x1l", [P, C, N], F32R)
        up = ExitStack()
        sb = tensors(up)
        gh = sb("gh", [P, K1, N], F32R)
        gl = sb("gl", [P, K1, N], F32R)
        whA = [sb(f"whA{s}", [P, K1 * P], F32R) for s in range(2)]
        wlA = [sb(f"wlA{s}", [P, K1 * P], F32R) for s in range(2)]
        outTA = sb("outTA", [P, N])
        up.close()
        sb = tensors(st)
        bcast2 = {n: sb("c_" + n, [NT, D]) for n in ("ln2_w", "ln2_b", "bp")}
        st.close()
        low.close()

        st = ExitStack()
        sb = tensors(st)
        hh = sb("hh", [P, KF, N], F32R)
        hl = sb("hl", [P, KF, N], F32R)
        up = ExitStack()
        sb = tensors(up)
        wrawF = [sb(f"wrawF{s}", [P, C * P]) for s in range(2)]
        wqF = [sb(f"wqF{s}", [P, C * P]) for s in range(2)]
        whF = [sb(f"whF{s}", [P, C * P], F32R) for s in range(2)]
        wlF = [sb(f"wlF{s}", [P, C * P], F32R) for s in range(2)]
        sg = [sb(f"sg{s}", [P, CHW]) for s in range(3)]
        nh = sb("nh", [P, C, N], F32R)
        nl = sb("nl", [P, C, N], F32R)
        wrawD0 = sb("wrawD0", [P, KF * P])
        wqD0 = sb("wqD0", [P, KF * P])
        up.close()
        sb = tensors(st)
        wrawD = [wrawD0, sb("wrawD1", [P, KF * P])]
        wqD = [wqD0, sb("wqD1", [P, KF * P])]
        whD = [sb(f"whD{s}", [P, KF * P], F32R) for s in range(2)]
        wlD = [sb(f"wlD{s}", [P, KF * P], F32R) for s in range(2)]
        outTD = sb("outTD", [P, N])
        st.close()

        N_CONSTS = 9
        QSTEPS = 8
        N_BOUND = 5 + 4 * EB

        s = {}

        def S(name):
            if name not in s:
                s[name] = sem(name)
            return s[name]

        xg_stored = [S("xg_stored0"), S("xg_stored1")]
        gathered = [S(f"gathered{k}") for k in range(ROUND)]

        PER_TILE = dict(
            xs_ready=1, xnT_ps=1, xT_ready=1, q_ps=1, k_ps=1, v_ps=1, self_ps=1,
            q_biased=1, k_biased=1, v_biased=1, self_added=1, q_shift=1, k_shift=1, q_exp=1, k_exp=1,
            q_soft=1, k_soft=1, qT_ps=1, qT_saved=1, ctx_done=1,
            group_done=4, S_saved=8, ST_ps=4, ST_saved=4, cnt_ready=1, A_ready=1, rel_done=1, y_ready=1,
            var_ready=1, sd_ready=1, x1_ready=1, soft_step=6, tail_step=7)

        def cur(name, i, k=1):
            return PER_TILE[name] * (i + 1) + k

        def prev(name, i):
            return PER_TILE[name] * (i + 1)

        def start_credit(eng, names):
            for n in names:
                eng.sem_inc(S(n), PER_TILE[n])

        def transposes(dst_bank, src_of, n, rows, cols, width):
            for c in range(n):
                last = nc.tensor.transpose(dst_bank[0:cols, c * width:c * width + rows], src_of(c), ident[0:rows, 0:rows])
            return last

        def bview(b, n, w):
            return b[:, 0:n * w].rearrange("p (c w) -> p c w", c=n)

        TS, QK, SPS, AGG, CTX = bank[1], (bank[2], bank[3]), bank[4], bank[5], (bank[6], bank[7])
        TP = bank[0]
        SUMT = (TS, bank[3], TS, TS)
        CNT = bank[0][:, 504:505]
        DEG = bank[0][0:NT, 506:508]
        MARK = bank[0][:, 508:509]

        CREDIT = 4
        PASS_COUNTS = dict(loaded=0) | {k: CREDIT for k in ("whi", "wlo", "mm", "wT", "quant", "outT", "backT", "backed", "used")}

        class Pass:
            def __init__(self, name, U, K, src, raw, h, l, act, mode, q=None, outT=None):
                self.name, self.U, self.K, self.src, self.raw, self.h, self.l = name, U, K, src, raw, h, l
                self.act, self.mode, self.q, self.outT = act, mode, q, outT
                self.transposed = mode in ("gateup", "down", "mix")
                self.chunks = [(k, min(k + 4, K)) for k in range(0, K, 4)] if self.transposed else [(0, K)]
                self.back = mode in ("down", "mix", "w2")
                self.raw_free = "quant" if q else "wT" if self.transposed else "wlo"
                n = len(self.chunks)
                self.per = dict(loaded=16, whi=n, wlo=n, mm=3)
                self.per |= dict(wT=n) if self.transposed else {}
                self.per |= dict(quant=1) if q else {}
                self.per |= dict(outT=3, backT=3, backed=3) if self.back else dict(used=3)
                self.base = dict(PASS_COUNTS) | dict(loaded=0)
                for k, m in self.per.items():
                    PASS_COUNTS[k] += m * U

            def s(self, what, slot):
                return S(f"{self.name}_loaded{slot}" if what == "loaded" else f"pass_{what}{slot}")

            def cur(self, what, u, k=None):
                m = self.per[what]
                return u * m + (self.base[what] + (m if k is None else k))

            def prev(self, what, u):
                return u * self.per[what] + self.base[what]

        w1_src = lambda u, sl: a["L0_gnn_W1"].rearrange("(c p) f -> p c f", p=P)[:, :, bass.ds((2 * u + sl) * P, P)]
        w2_src = lambda u, sl: a["L0_gnn_W2"].rearrange("(c p) f -> p c f", p=P)[:, :, bass.ds((2 * u + sl) * P, P)]
        wp_src = lambda u, sl: a["L0_mix_Wp"][bass.ds((2 * u + sl) * P, P), :]
        gu_src = lambda u, sl: a[("L0_ffn_w_gate", "L0_ffn_w_up")[sl]][bass.ds(u * P, P), :]
        wd_src = lambda u, sl: a["L0_ffn_w_down"][bass.ds((2 * u + sl) * P, P), :]
        W1 = Pass("w1", 4, C, w1_src, wrawA, whA, wlA, (x1h, x1l), "gelu")
        W2 = Pass("w2", 2, K1, w2_src, wrawA, whA, wlA, (gh, gl), "w2", outT=outTA)
        WP = Pass("wp", 2, C, wp_src, wrawP, whA, wlA, (x1h, x1l), "mix", outT=outTA)
        GU = Pass("gu", KF, C, gu_src, wrawF, whF, wlF, (nh, nl), "gateup", q=wqF)
        WD = Pass("wd", 2, KF, wd_src, wrawD, whD, wlD, (hh, hl), "down", q=wqD, outT=outTD)
        TB = (bank[6], bank[7])
        XB = bank[1:5]
        MB = ((bank[0], bank[1], bank[2]), (bank[3], bank[4], bank[5]))

        PLO_W1 = 2 + 3 * 2 * W1.U
        LN2_HALF = T // 2
        ATTN_AT = [(0, 1), (1, 0), (1, 2)]

        def quant_at(p, u, sl, k):
            tiles_before = 2 * (p.base["quant"] - CREDIT)
            return u * (2 * QSTEPS) + ((tiles_before + sl + 1) * QSTEPS + k)

        def f32(v):
            return v.bitcast(F32)

        def pass_credit(eng, whats):
            for w in whats:
                for sl in range(2):
                    eng.sem_inc(S(f"pass_{w}{sl}"), CREDIT)

        BACK = [(0, 4), (4, 8), (8, 10)]

        def tb_of(p, sl, ci):
            return (sl * len(p.chunks) + ci) % 2

        block = top.enter_context(nc.Block())

        @block.sync
        def _(sp):
            xv = x.rearrange("(t p) f -> p t f", p=NT)
            sp.dma_start(xn[0:112, :, :], xv[0:112, :, :]).then_inc(S("x_loaded"), 16)
            sp.dma_start(xn[112:NT, :, :], xv[112:NT, :, :]).then_inc(S("x_loaded"), 16)
            sp.wait_ge(S("epad"), 1)
            full = (EB - 1) * P
            rest = E // P - full
            for n, v in enumerate((src, dst, typ)):
                sp.dma_start(ei[:, n, 0:EB - 1, :], v[0:full * P].rearrange("(b t e) -> t b e", t=P, e=P)).then_inc(S("edges_loaded"), 16)
                sp.dma_start(ei[0:rest, n, EB - 1, :], v[full * P:(full + rest) * P].rearrange("(t e) -> t e", e=P)).then_inc(S("edges_loaded"), 16)
                sp.dma_start(ei[rest:rest + 1, n, EB - 1, 0:E % P], v[(full + rest) * P:E].rearrange("(t e) -> t e", t=1)).then_inc(S("edges_loaded"), 16)
            for n, m in enumerate(("q", "k", "v")):
                sp.dma_start(wstage[:, n, :, :], a["L0_mix_W" + m].rearrange("(b p) f -> p b f", p=P)).then_inc(S(f"w{m}_loaded"), 16)
            for t in range(T):
                sp.wait_ge(S("xlo_ready"), t + 1)
                sp.wait_ge(S("xhi_ready"), t + 1)
                sp.dma_start(xg[t * NT:(t + 1) * NT, :], xgst[:, t % 2, :]).then_inc(xg_stored[t % 2], 16)
            for n, v in (("bq", "L0_mix_bq"), ("bk", "L0_mix_bk"), ("bv", "L0_mix_bv"),
                         ("self_b", "L0_gnn_self_b"), ("ln1_w", "L0_gnn_ln1_w"), ("ln1_b", "L0_gnn_ln1_b")):
                sp.dma_start(bcast[n][:, :], a[v].rearrange("(o f) -> o f", o=1).broadcast_to([NT, D])).then_inc(S("biases_loaded"), 16)
            for r in range(R):
                sp.dma_start(relb[r * GW:(r + 1) * GW, :], a["L0_gnn_rel_b"][r:r + 1, :].broadcast_to([GW, D])).then_inc(S("biases_loaded"), 16)
            sp.dma_start(selfW[:, :, :], a["L0_gnn_self_W"].rearrange("(c p) f -> p c f", p=P)).then_inc(S("selfW_loaded"), 16)
            sp.dma_start(b1c[:, :], a["L0_gnn_b1"].rearrange("(c p) -> p c", p=P), allow_slow_non_contiguous=True).then_inc(S("biases_loaded"), 16)
            sp.wait_ge(S("wT_ps"), 3 * C)
            sp.wait_ge(S("bound_int"), 1)
            sp.wait_ge(S("edge_out"), 2)
            sp.wait_ge(S("consts_vec"), N_CONSTS)
            for k in range(2):
                sp.wait_ge(xg_stored[k], 16 * T // 2)
            sp.dma_start(relW[:, :, :], a["L0_gnn_rel_W"].rearrange("r (c p) f -> p (r c) f", p=P)).then_inc(S("relW_loaded"), 16)

            def load(p, u, sl):
                sp.wait_ge(p.s(p.raw_free, sl), p.prev(p.raw_free, u))
                dst_ap = p.raw[sl][:, 0:p.K * P]
                if not p.transposed:
                    dst_ap = dst_ap.rearrange("p (k f) -> p k f", k=p.K)
                sp.dma_start(dst_ap, p.src(u, sl)).then_inc(p.s("loaded", sl), 16)

            def load_pass(p):
                with sp.Fori(0, p.U) as u:
                    for sl in range(2):
                        load(p, u, sl)

            def row(v):
                return a[v].rearrange("(o f) -> o f", o=1).broadcast_to([NT, D])

            sp.dma_start(b2[:, :], row("L0_gnn_b2")).then_inc(S("b2_loaded"), 16)
            load_pass(W1)
            load_pass(W2)
            sp.wait_ge(S("pair_ready"), W1.U)
            load_pass(WP)
            for sl in range(2):
                sp.wait_ge(W2.s("wlo", sl), W2.cur("wlo", W2.U - 1))
            sp.dma_start(yx[0:112, :, :], xv[0:112, :, :]).then_inc(S("x_again"), 16)
            sp.dma_start(yx[112:NT, :, :], xv[112:NT, :, :]).then_inc(S("x_again"), 16)
            for sl in range(2):
                sp.wait_ge(W2.s("mm", sl), W2.cur("mm", W2.U - 1))
            for n in bcast2:
                sp.dma_start(bcast2[n][:, :], row("L0_mix_bp" if n == "bp" else "L0_gnn_" + n)).then_inc(S("bias2_loaded"), 16)
            load_pass(GU)
            load(WD, 0, 0)
            for sl in range(2):
                sp.wait_ge(GU.s("mm", sl), GU.cur("mm", GU.U - 1))
            load(WD, 0, 1)
            for u in range(1, WD.U):
                for sl in range(2):
                    load(WD, u, sl)
            ov = out.rearrange("(t p) f -> p t f", p=NT)
            for o in range(2 * WD.U):
                sp.wait_ge(WD.s("backed", o % 2), WD.cur("backed", o // 2))
                sp.dma_start(ov[0:112, :, o * P:(o + 1) * P], yx[0:112, :, o * P:(o + 1) * P]).then_inc(S("out_stored"), 16)
                sp.dma_start(ov[112:NT, :, o * P:(o + 1) * P], yx[112:NT, :, o * P:(o + 1) * P]).then_inc(S("out_stored"), 16)
            sp.wait_ge(S("out_stored"), 16 * 4 * WD.U)


        @block.gpsimd
        def _(pool):
            pool.sem_inc(S("plo"), 2)
            pass_credit(pool, ["quant"])
            nc.gpsimd.memset(ident[:, :], 0.0).then_inc(S("consts_mem"), 1)
            nc.gpsimd.memset(bmask[:, :], 0.0).then_inc(S("consts_mem"), 1)
            pool.wait_ge(S("consts_mem"), 2)
            nc.gpsimd.affine_select(out=ident[:, :], in_=ident[:, :], compare_op=ALU.not_equal, fill=1.0, base=0,
                                    pattern=[[-1, P]], channel_multiplier=1).then_inc(S("consts_iota"), 1)
            nc.gpsimd.iota(gbi[:, 0:G], pattern=[[NT, T], [GW, 4]], base=0, channel_multiplier=0).then_inc(S("consts_iota"), 1)
            nc.gpsimd.memset(gbi[:, G:G + 1], N).then_inc(S("consts_iota"), 1)
            nc.gpsimd.iota(tni[:, :], pattern=[[P, EB]], base=0, channel_multiplier=1).then_inc(S("consts_iota"), 1)
            nc.gpsimd.iota(ikey[:, :], pattern=[[KEY, R], [1, GW]], base=0, channel_multiplier=0).then_inc(S("consts_iota"), 1)
            nc.gpsimd.iota(gmi[:, :, :], pattern=[[-1, 4], [0, GW]], base=0, channel_multiplier=1).then_inc(S("consts_iota"), 1)

            pool.wait_ge(S("bound_int"), 1)
            pool.wait_ge(S("edge_out"), 2)
            for k in range(2):
                pool.wait_ge(xg_stored[k], 16 * T // 2)
            n = pool.alloc_register("gather_round")
            pool.reg_mov(n, 0)
            with pool.Fori(0, G) as g:
                lo = pool.value_load(bounds[0:1, bass.ds(g, 1)], min_val=0, max_val=ETILES)
                hi = pool.value_load(bounds[0:1, bass.ds(g + (G + 1), 1)], min_val=0, max_val=ETILES)
                with pool.Fori(lo, hi, ROUND) as tb:
                    m = pool.snap(n, min_val=0, max_val=G * 33)
                    for h in range(2):
                        pool.wait_ge(S("slots_used"), m * ROUND + HALF * (h + 1))
                        nc.gpsimd.tensor_copy(idx[:, h, :], srcT[:, bass.ds(tb + HALF * h, HALF)]).then_inc(S("idx_ready"), 1)
                        pool.wait_ge(S("idx_ready"), m * 2 + (h + 1))
                        pool.sem_inc(S("pool_passed"), 1)
                        for k in range(HALF):
                            slot = HALF * h + k
                            nc.gpsimd.indirect_dma_start(
                                out=ring[:, slot, :], out_offset=None, in_=xg[:, :],
                                in_offset=bass.IndirectOffsetOnAxis(ap=idx[:, h, k:k + 1], axis=0)).then_inc(gathered[slot], 16)
                    pool.reg_add(n, n, 1)

            G_ = nc.gpsimd
            pool.wait_ge(S("b2_loaded"), 16)
            pool.wait_ge(S("x1c_ps"), T)
            for t in range(T):
                G_.tensor_tensor(xn[:, t, :], xn[:, t, :], b2[:, :], ALU.add).then_inc(S("b2_added"), 1)
            with pool.Fori(0, W1.U) as u:
                for sl in range(2):
                    for ch, (n0, n1) in enumerate(CH):
                        g = (bass.ds(2 * u + sl, 1), slice(n0, n1))
                        pool.wait_ge(S("phi"), 6 * u + (3 * sl + ch + 1))
                        G_.tensor_tensor(gl[:, g[0], g[1]].rearrange("p o n -> p (o n)"), tmpA[(3 * sl + ch) % 2][:, 0:n1 - n0],
                                         f32(gh[:, g[0], g[1]]).rearrange("p o n -> p (o n)"), ALU.subtract).then_inc(S("plo"), 1)
            for pr in range(C):
                pool.wait_ge(S("attn_hi"), pr + 1)
                G_.tensor_tensor(x1l[:, pr, :], qT[:, pr, :], f32(x1h[:, pr, :]), ALU.subtract).then_inc(S("attn_lo"), 1)
            pool.wait_ge(S("bias2_loaded"), 48)
            G_.tensor_tensor(bcast2["bp"][:, :], bcast2["bp"][:, :], bcast2["ln2_b"][:, :], ALU.add).then_inc(S("bias_sum"), 1)
            pool.wait_ge(S("bias_sum"), 1)

            def quantised(p, u, sl):
                pool.wait_ge(S("quant_step"), quant_at(p, u, sl, QSTEPS))
                w, wq = p.raw[sl][:, 0:p.K * P], p.q[sl][:, 0:p.K * P]
                G_.tensor_tensor(wq, wq, w, ALU.add).then_inc(p.s("quant", sl), 1)

            def ln2_affine(t0, t1_):
                for t in range(t0, t1_):
                    pool.wait_ge(S("ln2_rows"), t + 1)
                    G_.tensor_tensor(xn[:, t, :], xn[:, t, :], bcast2["ln2_w"][:, :], ALU.mult).then_inc(S("ln2_scaled"), 1)
                    pool.wait_ge(S("ln2_scaled"), t + 1)
                    G_.tensor_tensor(xn[:, t, :], xn[:, t, :], bcast2["bp"][:, :], ALU.add).then_inc(S("ln2_ready"), 1)

            ln2_affine(0, LN2_HALF)
            quantised(GU, 0, 0)
            ln2_affine(LN2_HALF, T)
            quantised(GU, 0, 1)

            def gateup(u, last):
                if not last:
                    quantised(GU, u + 1, 0)
                    quantised(GU, u + 1, 1)
                else:
                    quantised(WD, 0, 0)
                for ch, (n0, n1) in enumerate(CH):
                    pool.wait_ge(S("sil"), 3 * u + (ch + 1))
                    G_.tensor_tensor(hl[:, bass.ds(u, 1), n0:n1].rearrange("p o n -> p (o n)"), sg[ch][:, 0:n1 - n0],
                                     f32(hh[:, bass.ds(u, 1), n0:n1]).rearrange("p o n -> p (o n)"), ALU.subtract).then_inc(S("plo"), 1)

            with pool.Fori(0, GU.U - 1) as u:
                gateup(u, False)
            gateup(GU.U - 1, True)
            quantised(WD, 0, 1)
            for u in range(1, WD.U):
                for sl in range(2):
                    quantised(WD, u, sl)

        @block.scalar
        def _(act):
            start_credit(act, ["xs_ready", "xT_ready", "q_exp", "k_exp", "qT_saved", "S_saved", "ST_saved", "sd_ready"])
            pass_credit(act, ["whi", "outT", "used"])
            act.wait_ge(S("ln0_stats"), T + 1)
            nc.scalar.activation(lnsd[:, :], lnmv[:, :, 1], ACT.Sqrt, bias=epsc[0:NT, 0:1]).then_inc(S("ln0_sd"), 1)

            def save_w(n, c):
                act.wait_ge(S("wT_ps"), n * C + c + 1)
                nc.scalar.copy(wqkv[:, c, n, :], bank[(n * C + c) % 4][:, :]).then_inc(S("wT_saved"), 1)

            for n in range(2):
                for c in range(C):
                    save_w(n, c)
            for t in range(T):
                act.wait_ge(S("xn_rows"), t + 1)
                if t >= 2:
                    act.wait_ge(xg_stored[t % 2], 16 * (t // 2))
                nc.scalar.activation(xgst[:, t % 2, 0:D], xn[:, t, :], ACT.Identity, scale=XSCALE).then_inc(S("xhi_ready"), 1)
            for c in range(C):
                save_w(2, c)

            def copy_rows(t):
                nc.scalar.copy(xs[:, :], xn[:, bass.ds(t, 1), :].rearrange("p o f -> p (o f)")).then_inc(S("xs_ready"), 1)

            def tail_sd(i):
                act.wait_ge(S("var_ready"), cur("var_ready", i))
                nc.scalar.activation(sd[:, :], mv[:, 1:2], ACT.Sqrt, bias=epsc[0:NT, 0:1]).then_inc(S("sd_ready"), 1)

            def tile(i, first):
                def save_S(j):
                    act.wait_ge(S("group_done"), cur("group_done", i, j + 1))
                    if j == 0:
                        act.wait_ge(S("cnt_ready"), prev("cnt_ready", i))
                    nc.scalar.copy(cntb[:, j:j + 1], CNT).then_inc(S("S_saved"), 1)
                    nc.scalar.activation(S_sb[:, j % 2, :], SPS[:, :], ACT.Copy, scale=1.0 / XSCALE).then_inc(S("S_saved"), 1)

                def save_ST(j):
                    act.wait_ge(S("ST_ps"), cur("ST_ps", i, j + 1))
                    nc.scalar.copy(ST[:, :, :, GW * j:GW * (j + 1)],
                                   SUMT[j][:, :].rearrange("p (c t d) -> p c t d", c=C, t=R)).then_inc(S("ST_saved"), 1)

                save_S(0)
                save_S(1)
                act.wait_ge(S("xnT_ps"), cur("xnT_ps", i))
                act.wait_ge(S("self_ps"), prev("self_ps", i))
                nc.scalar.copy(xT[:, :, :], bview(TP, C, NT)).then_inc(S("xT_ready"), 1)
                if not first:
                    act.wait_ge(S("rel_done"), cur("rel_done", i - 1))
                save_ST(0)
                save_ST(1)
                if not first:
                    tail_sd(i - 1)
                save_S(2)
                act.wait_ge(S("q_shift"), cur("q_shift", i))
                nc.scalar.activation(qf[:, :], qf[:, :], ACT.Exp).then_inc(S("q_exp"), 1)
                act.wait_ge(S("k_shift"), cur("k_shift", i))
                nc.scalar.activation(kf[:, :], kf[:, :], ACT.Exp).then_inc(S("k_exp"), 1)
                save_ST(2)
                save_S(3)
                act.wait_ge(S("qT_ps"), cur("qT_ps", i))
                nc.scalar.copy(qT[:, :, bass.ds(i * NT, NT)], bview(TP, C, NT)).then_inc(S("qT_saved"), 1)
                save_ST(3)

            copy_rows(0)
            tile(0, True)
            with act.Fori(1, T) as i:
                copy_rows(i)
                tile(i, False)
            tail_sd(T - 1)

            act.wait_ge(S("x1_ready"), cur("x1_ready", T - 1))
            act.wait_ge(S("ctx_bd_ready"), 1)
            act.wait_ge(S("rel_done"), cur("rel_done", T - 1))
            for t in range(T):
                act.wait_ge(S("x1c_ps"), t + 1)
                nc.scalar.copy(x1h[:, :, t * NT:(t + 1) * NT], bview(XB[t % 4], C, NT)).then_inc(S("x1c_hi"), 1)

            def weights_hi(p, u, sl):
                for ci, (k0, k1) in enumerate(p.chunks):
                    if p.transposed:
                        act.wait_ge(p.s("wT", sl), p.cur("wT", u, ci + 1))
                        source = TB[tb_of(p, sl, ci)][:, 0:(k1 - k0) * P]
                    else:
                        act.wait_ge(p.s("loaded", sl), p.cur("loaded", u))
                        source = p.raw[sl][:, 0:p.K * P]
                    if ci == 0:
                        act.wait_ge(p.s("mm", sl), p.prev("mm", u))
                    nc.scalar.copy(p.h[sl][:, k0 * P:k1 * P], source).then_inc(p.s("whi", sl), 1)

            def results(p, u, sl):
                for ch, (n0, n1) in enumerate(CH):
                    w = n1 - n0
                    if p.mode == "gelu":
                        act.wait_ge(p.s("mm", sl), p.cur("mm", u, ch + 1))
                        b = (3 * sl + ch) % 2
                        act.wait_ge(S("plo"), 6 * u + 3 * sl + ch + 1 )
                        act.sem_inc(S("act_passed"), 1)
                        nc.scalar.activation(tmpA[b][:, 0:w], MB[sl][ch][:, 0:w], ACT.Gelu,
                                             bias=b1c[:, bass.ds(2 * u + sl, 1)]).then_inc(p.s("used", sl), 1)
                        act.wait_ge(p.s("used", sl), p.cur("used", u, ch + 1))
                        nc.scalar.copy(gh[:, bass.ds(2 * u + sl, 1), n0:n1].rearrange("p o n -> p (o n)"), tmpA[b][:, 0:w]).then_inc(S("phi"), 1)
                    elif p.mode == "gateup":
                        if sl == 0:
                            act.wait_ge(p.s("mm", 0), p.cur("mm", u, ch + 1))
                            act.wait_ge(S("plo"), 3 * u + (PLO_W1 - 2 + ch))
                            nc.scalar.activation(sg[ch][:, 0:w], MB[0][ch][:, 0:w], ACT.Silu).then_inc(p.s("used", 0), 1)
                        else:
                            act.wait_ge(p.s("used", 1), p.cur("used", u, ch + 1))
                            nc.scalar.copy(hh[:, bass.ds(u, 1), n0:n1].rearrange("p o n -> p (o n)"), sg[ch][:, 0:w]).then_inc(S("sil"), 1)
                    else:
                        act.wait_ge(p.s("mm", sl), p.cur("mm", u, ch + 1))
                        if ch == 0:
                            if sl == 0:
                                act.wait_ge(p.s("backT", 1), p.prev("backT", u))
                            else:
                                act.wait_ge(p.s("backT", 0), p.cur("backT", u))
                        nc.scalar.copy(p.outT[:, n0:n1], MB[sl][ch][:, 0:w]).then_inc(p.s("outT", sl), 1)

            def no_work(u, sl):
                pass

            def run(p, beside=no_work):
                weights_hi(p, 0, 0)

                def body(u, last):
                    weights_hi(p, u, 1)
                    beside(u, 0)
                    results(p, u, 0)
                    if not last:
                        weights_hi(p, u + 1, 0)
                    beside(u, 1)
                    results(p, u, 1)
                if p.U > 2:
                    with act.Fori(0, p.U - 1) as u:
                        body(u, False)
                else:
                    body(0, False)
                body(p.U - 1, True)

            def pair_operands(u, sl):
                if sl == 0:
                    act.wait_ge(S("attn_ps"), 3 * u + 3)
                    nc.scalar.copy(pair[:, 0, :], ksumbd[:, bass.ds(u, 1), :].rearrange("p o f -> p (o f)"))
                    nc.scalar.copy(pair[:, 1, :], ctxbd[:, bass.ds(u, 1), :].rearrange("p o f -> p (o f)")).then_inc(S("pair_ready"), 1)

            def attention_hi(u, sl):
                if (u, sl) == (0, 0):
                    act.wait_ge(S("attn_full"), 3 * C + 1)
                    for k in range(2):
                        act.wait_ge(W1.s("mm", k), W1.cur("mm", W1.U - 1))
                nc.scalar.copy(x1h[:, 2 * u + sl, :], qT[:, 2 * u + sl, :]).then_inc(S("attn_hi"), 1)

            def ln2_rows(u, sl):
                if (u, sl) == (0, 0):
                    act.wait_ge(S("ln2_stats"), T)
                    nc.scalar.activation(lnsd[:, :], lnmv[:, :, 1], ACT.Sqrt, bias=epsc[0:NT, 0:1]).then_inc(S("ln2_sd"), 1)
                if u == 0:
                    act.wait_ge(S("ln2_shift"), 1)
                    for t in range(LN2_HALF * sl, LN2_HALF * (sl + 1)):
                        nc.scalar.activation(xn[:, t, :], xn[:, t, :], ACT.Identity, bias=lnsh[:, t:t + 1],
                                             scale=lnrs[:, t:t + 1]).then_inc(S("ln2_rows"), 1)

            act.wait_ge(S("biases_loaded"), 16 * 11)
            run(W1, pair_operands)
            run(W2, attention_hi)
            run(WP, ln2_rows)
            act.wait_ge(S("ln3_stats"), T)
            nc.scalar.activation(lnsd[:, :], lnmv[:, :, 1], ACT.Sqrt, bias=epsc[0:NT, 0:1]).then_inc(S("ln3_sd"), 1)
            for t in range(T):
                act.wait_ge(S("n3c_ps"), t + 1)
                nc.scalar.copy(nh[:, :, t * NT:(t + 1) * NT], bview(XB[t % 4], C, NT)).then_inc(S("n3c_hi"), 1)
            run(GU)
            run(WD)

        @block.tensor
        def _(pe):
            pe.sem_inc(S("attn_ps"), 3)
            start_credit(pe, ["xnT_ps", "q_ps", "k_ps", "v_ps", "self_ps", "qT_ps", "ctx_done", "group_done", "ST_ps", "rel_done"])
            pe.sem_inc(S("slots_used"), ROUND)
            pass_credit(pe, ["mm", "wT", "backT"])
            pe.wait_ge(S("consts_iota"), 1)

            def weights_T(n):
                pe.wait_ge(S(f"w{'qkv'[n]}_loaded"), 16)
                for c in range(C):
                    k = n * C + c
                    if k >= 4:
                        pe.wait_ge(S("wT_saved"), k - 3)
                    transposes(bank[k % 4], lambda b: wstage[:, n, b, c * P:(c + 1) * P], C, P, P, P).then_inc(S("wT_ps"), 1)

            weights_T(0)
            weights_T(1)
            pe.wait_ge(S("edge_prep"), 2)
            transposes(bank[4], lambda b: ekey[:, b, :], EB, P, P, P)
            transposes(bank[5], lambda b: esrc[:, b, :], EB, P, P, P).then_inc(S("edge_T"), 1)
            pe.wait_ge(S("bound_val"), N_BOUND)
            W2G = 2 * (G + 1)
            transposes(bank[6], lambda b: gv[:, b, :, :].rearrange("p a g -> p (a g)"), EB, P, W2G, P).then_inc(S("bound_T"), 1)
            pe.wait_ge(S("bound_max"), 1)
            nc.tensor.transpose(bank[7][0:1, 0:W2G], gm[:, 0:1], ident[0:W2G, 0:W2G]).then_inc(S("bound_T"), 1)
            weights_T(2)
            pe.wait_ge(S("consts_vec"), N_CONSTS)
            pe.wait_ge(S("bound_int"), 1)
            for b in CTX:
                nc.tensor.matmul(b[:, :], zero16[:, 0:P], zero16[:, :], start=True, stop=True, skip_group_check=True)
            pe.wait_ge(S("edge_out"), 2)
            pe.wait_ge(S("wT_saved"), 3 * C)

            n = pe.alloc_register("agg_round")
            pe.reg_mov(n, 0)
            def relations(i, r0, r1):
                for r in range(r0, r1):
                    for c in range(C):
                        nc.tensor.matmul(AGG[0:NT, :], ST[:, c, r, 0:NT], relW[:, r * C + c, :], start=r + c == 0, stop=False)

            def relation_biases(i):
                pe.wait_ge(S("A_ready"), cur("A_ready", i))
                av = A[:, :, :].rearrange("p g d -> p (g d)")[:, 0:NT]
                nc.tensor.matmul(AGG[0:NT, :], av, relb[:, :], start=False, stop=True)
                nc.tensor.matmul(DEG, av, ones[:, :], start=True, stop=True, skip_group_check=True).then_inc(S("rel_done"), 1)

            def tile(i, first):
                def neighbours(j):
                    lo = pe.value_load(bounds[0:1, bass.ds(i * 4 + j, 1)], min_val=0, max_val=ETILES)
                    hi = pe.value_load(bounds[0:1, bass.ds(i * 4 + (j + G + 1), 1)], min_val=0, max_val=ETILES)
                    pe.wait_ge(S("S_saved"), 2 * (i * 4 + j) + 8)
                    nc.tensor.matmul(SPS[:, :], zero16[:, 0:P], zero16[:, :], start=True, stop=False, skip_group_check=True)
                    if j == 0:
                        pe.wait_ge(S("qT_saved"), prev("qT_saved", i))
                    if j == 2:
                        pe.wait_ge(S("xT_ready"), cur("xT_ready", i))
                        if not first:
                            pe.wait_ge(S("y_ready"), cur("y_ready", i - 1))
                    nc.tensor.matmul(CNT, zero16[:, 0:P], zero16[:, 0:1], start=True, stop=False, skip_group_check=True)
                    with pe.Fori(lo, hi, ROUND) as tb:
                        m = pe.snap(n, min_val=0, max_val=G * 33)
                        for h in range(2):
                            pe.wait_ge(S("oh_ready"), m * 2 + (h + 3))
                            for k in range(HALF):
                                slot = HALF * h + k
                                pe.wait_ge(gathered[slot], m * 16 + 16)
                                nc.tensor.matmul(SPS[:, :], oh[:, h, k, :], ring[:, slot, 0:D], start=False, stop=False, skip_group_check=True)
                                nc.tensor.matmul(SPS[:, :], oh[:, h, k, :], ring[:, slot, D:2 * D], start=False, stop=False, skip_group_check=True)
                                nc.tensor.matmul(CNT, oh[:, h, k, :], one16[:, 0:1], start=False, stop=False,
                                                 skip_group_check=True).then_inc(S("slots_used"), 1)
                        pe.reg_add(n, n, 1)
                    nc.tensor.matmul(MARK, zero16[:, 0:P], zero16[:, 0:1], start=False, stop=True,
                                     skip_group_check=True).then_inc(S("group_done"), 1)

                def sums_T(j):
                    pe.wait_ge(S("S_saved"), 2 * (i * 4 + j) + 10)
                    transposes(SUMT[j], lambda c: S_sb[:, j % 2, c * P:(c + 1) * P], C, P, P, P).then_inc(S("ST_ps"), 1)

                def project(b, w, name):
                    for c in range(C):
                        last = nc.tensor.matmul(b[0:NT, :], xT[:, c, :], w(c), start=c == 0, stop=c == C - 1)
                    last.then_inc(S(name), 1)

                neighbours(0)
                if not first:
                    relations(i - 1, 0, R // 2)
                neighbours(1)
                pe.wait_ge(S("S_saved"), 2 * (i * 4 + 1) + 10)
                pe.wait_ge(S("xs_ready"), cur("xs_ready", i))
                transposes(TP, lambda c: xs[:, c * P:(c + 1) * P], C, NT, P, NT).then_inc(S("xnT_ps"), 1)
                if not first:
                    relations(i - 1, R // 2, R)
                    pe.wait_ge(S("xT_ready"), cur("xT_ready", i))
                    relation_biases(i - 1)
                pe.wait_ge(S("ST_saved"), prev("ST_saved", i))
                sums_T(0)
                pe.wait_ge(S("self_added"), prev("self_added", i))
                sums_T(1)
                neighbours(2)
                pe.wait_ge(S("xT_ready"), cur("xT_ready", i))
                pe.wait_ge(S("v_biased"), prev("v_biased", i))
                project(QK[0], lambda c: wqkv[:, c, 0, :], "q_ps")
                pe.wait_ge(S("ST_saved"), cur("ST_saved", i, 2))
                project(QK[1], lambda c: wqkv[:, c, 1, :], "k_ps")
                sums_T(2)
                neighbours(3)
                pe.wait_ge(S("q_biased"), cur("q_biased", i))
                project(QK[0], lambda c: wqkv[:, c, 2, :], "v_ps")
                pe.wait_ge(S("q_soft"), cur("q_soft", i))
                pe.wait_ge(S("S_saved"), 2 * (i * 4 + 3) + 10)
                transposes(TP, lambda c: qf[:, c * P:(c + 1) * P], C, NT, P, NT).then_inc(S("qT_ps"), 1)
                pe.wait_ge(S("k_biased"), cur("k_biased", i))
                project(QK[1], lambda c: selfW[:, c, :], "self_ps")
                pe.wait_ge(S("k_soft"), cur("k_soft", i))
                pe.wait_ge(S("v_biased"), cur("v_biased", i))
                for pr in range(4):
                    last = nc.tensor.matmul(CTX[pr // 2][:, 130 * (pr % 2):130 * (pr % 2) + 130], kf[:, pr * P:(pr + 1) * P], vf[:, pr, :],
                                            start=False, stop=True, skip_group_check=True)
                last.then_inc(S("ctx_done"), 1)
                pe.wait_ge(S("ST_saved"), cur("ST_saved", i, 3))
                sums_T(3)

            pe.wait_ge(S("selfW_loaded"), 16)
            tile(0, True)
            pe.wait_ge(S("relW_loaded"), 16)
            pe.wait_ge(S("biases_loaded"), 16 * 11)
            with pe.Fori(1, T) as i:
                pe.wait_ge(S("ST_saved"), prev("ST_saved", i))
                tile(i, False)
            pe.wait_ge(S("ST_saved"), cur("ST_saved", T - 1, 4))
            relations(T - 1, 0, R)
            relation_biases(T - 1)

            def to_columns(name, ready):
                for t in range(T):
                    ready(t)
                    if t >= 4:
                        pe.wait_ge(S(name + "_hi"), t - 3)
                        pe.wait_ge(S(name + "_lo"), t - 3)
                    transposes(XB[t % 4], lambda c: xn[:, t, c * P:(c + 1) * P], C, NT, P, NT).then_inc(S(name + "_ps"), 1)
                for part in ("_hi", "_lo"):
                    pe.wait_ge(S(name + part), T)

            pe.wait_ge(S("v_biased"), cur("v_biased", T - 1))
            pe.wait_ge(S("self_added"), cur("self_added", T - 1))
            to_columns("x1c", lambda t: pe.wait_ge(S("x1_ready"), cur("x1_ready", t)))
            pe.wait_ge(S("ctx_bd_ready"), 1)

            def weights_T2(p, u, sl):
                if not p.transposed:
                    return
                w = p.q if p.q else p.raw
                pe.wait_ge(p.s("quant", sl), p.cur("quant", u)) if p.q else pe.wait_ge(p.s("loaded", sl), p.cur("loaded", u))
                total = len(p.chunks)
                for ci, (k0, k1) in enumerate(p.chunks):
                    b = sl * total + ci
                    back = b - 2
                    if back >= 0:
                        osl, oci, ou = back // total, back % total, u
                        pe.wait_ge(p.s("whi", osl), p.cur("whi", ou, oci + 1))
                        pe.wait_ge(p.s("wlo", osl), p.cur("wlo", ou, oci + 1))
                    else:
                        osl, oci = (back + 2 * total) // total, (back + 2 * total) % total
                        pe.wait_ge(p.s("whi", osl), p.cur("whi", u, oci + 1 - total))
                        pe.wait_ge(p.s("wlo", osl), p.cur("wlo", u, oci + 1 - total))
                    if p.back:
                        pe.wait_ge(p.s("backed", sl), p.prev("backed", u))
                    last = transposes(TB[b % 2], lambda c: w[sl][:, (k0 + c) * P:(k0 + c + 1) * P], k1 - k0, P, P, P)
                    last.then_inc(p.s("wT", sl), 1)

            def attention(u, ch):
                n0, n1 = CH[ch]
                if ch == 0:
                    pe.wait_ge(S("pair_ready"), u + 1)
                pe.wait_ge(S("attn_nd"), 3 * u + (ch + 1))
                q = qT[:, bass.ds(u, 1), n0:n1].rearrange("p o n -> p (o n)")
                nc.tensor.matmul(TB[0][:, 0:n1 - n0], pair[:, 0, :], q, start=True, stop=True)
                nc.tensor.matmul(TB[1][:, 0:n1 - n0], pair[:, 1, :], q, start=True, stop=True).then_inc(S("attn_ps"), 1)

            def products(p, u, sl):
                for ch, (n0, n1) in enumerate(CH):
                    w = n1 - n0
                    if ch == 0:
                        pe.wait_ge(p.s("whi", sl), p.cur("whi", u))
                        pe.wait_ge(p.s("wlo", sl), p.cur("wlo", u))
                    done = "outT" if p.back else "used"
                    pe.wait_ge(p.s(done, sl), p.cur(done, u, ch - 2))
                    k = 0
                    for kc in range(p.K):
                        ws = slice(kc * P, (kc + 1) * P)
                        for wgt, mov in ((p.h, p.act[0]), (p.h, p.act[1]), (p.l, p.act[0])):
                            last = nc.tensor.matmul(MB[sl][ch][:, 0:w], wgt[sl][:, ws], mov[:, kc, n0:n1],
                                                    start=k == 0, stop=k == 3 * p.K - 1)
                            k += 1
                    last.then_inc(p.s("mm", sl), 1)
                    if p.mode == "gelu" and (sl, ch) in ATTN_AT:
                        attention(u, ATTN_AT.index((sl, ch)))

            def back(p, u, sl, ahead):
                if not p.back:
                    return
                pe.wait_ge(p.s("outT", sl), p.cur("outT", u))
                for q, (t0, t1_) in enumerate(BACK):
                    total = len(p.chunks)
                    if q < 2 and p.transposed:
                        for osl in range(2):
                            at_u = u + 1 if ahead and osl == 0 else u
                            pe.wait_ge(p.s("whi", osl), p.cur("whi", at_u))
                            pe.wait_ge(p.s("wlo", osl), p.cur("wlo", at_u))
                    if sl == 0:
                        pe.wait_ge(p.s("backed", 1), p.prev("backed", u))
                    else:
                        pe.wait_ge(p.s("backed", 0), p.cur("backed", u))
                    if q == 2:
                        pe.wait_ge(p.s("backed", sl), p.cur("backed", u, 1))
                    for t in range(t0, t1_):
                        last = nc.tensor.transpose(TB[q % 2][0:NT, (t - t0) * P:(t - t0 + 1) * P],
                                                   p.outT[:, t * NT:(t + 1) * NT], ident[:, :])
                    last.then_inc(p.s("backT", sl), 1)

            def run(p):
                weights_T2(p, 0, 0)

                def body(u, last):
                    weights_T2(p, u, 1)
                    products(p, u, 0)
                    back(p, u, 0, False)
                    if not last:
                        weights_T2(p, u + 1, 0)
                    products(p, u, 1)
                    back(p, u, 1, not last)
                with pe.Fori(0, p.U - 1) as u:
                    body(u, False)
                body(p.U - 1, True)

            run(W1)
            pe.wait_ge(S("phi"), 3 * 2 * W1.U)
            pe.wait_ge(S("plo"), PLO_W1)
            pe.wait_ge(S("attn_nd"), 3 * C + 1)
            run(W2)
            for sl in range(2):
                pe.wait_ge(W2.s("backed", sl), W2.cur("backed", W2.U - 1))
            pe.wait_ge(S("attn_hi"), C)
            pe.wait_ge(S("attn_lo"), C)
            run(WP)
            to_columns("n3c", lambda t: pe.wait_ge(S("n3_rows"), t + 1))
            run(GU)
            pe.wait_ge(S("sil"), 3 * GU.U)
            pe.wait_ge(S("plo"), PLO_W1 + 3 * GU.U)
            run(WD)

        @block.vector
        def _(dve):
            V = nc.vector
            start_credit(dve, ["q_biased", "k_biased", "v_biased", "self_added", "q_shift", "k_shift", "q_soft", "k_soft",
                               "cnt_ready", "A_ready", "y_ready", "var_ready", "x1_ready", "soft_step", "tail_step"])
            dve.sem_inc(S("oh_ready"), 2)
            dve.sem_inc(S("attn_nd"), 1)
            dve.sem_inc(S("attn_full"), 1)
            dve.sem_inc(S("quant_step"), QSTEPS)
            pass_credit(dve, ["wlo", "backed"])

            V.memset(epsc[:, :], EPS)
            V.memset(ei[:, 0, EB - 1, :], 0)
            V.memset(ei[:, 2, EB - 1, :], 0)
            V.memset(ei[:, 1, EB - 1, :], int(NO_DST)).then_inc(S("epad"), 1)

            def const(ins):
                ins.then_inc(S("consts_vec"), 1)

            const(V.memset(zero16[:, :], 0.0))
            const(V.memset(one16[:, :], 1.0))
            const(V.memset(ones[:, :], 1.0))
            const(V.memset(cntb[:, :], 0.0))
            dve.wait_ge(S("consts_iota"), 6)
            const(V.tensor_copy(gb[:, :], gbi[:, :]))
            const(V.tensor_copy(iotaK[:, :], ikey[:, :]))
            const(V.tensor_copy(gmask[:, :, :], gmi[:, :, :]))
            dve.wait_ge(S("consts_vec"), 7)
            for q in range(4):
                quad = gmask[GW * q:GW * (q + 1), :, :]
                last = V.tensor_scalar(quad, quad, float(GW * q), None, ALU.is_equal)
            const(last)
            dve.wait_ge(S("consts_mem"), 2)
            V.memset(bmask[0:DH, 0:DH], 1.0)
            const(V.memset(bmask[DH:P, DH:P], 1.0))
            V.memset(vf[:, :, P:130], 1.0)

            dve.wait_ge(S("x_loaded"), 32)
            for t in range(T):
                V.bn_stats(lnst[:, t, :], xn[:, t, :]).then_inc(S("ln0_stats"), 1)
            dve.wait_ge(S("ln0_stats"), T)
            for t in range(T):
                last = V.bn_aggr(lnmv[:, t, :], lnst[:, t, :])
            last.then_inc(S("ln0_stats"), 1)

            dve.wait_ge(S("edges_loaded"), 16 * 9)
            V.scalar_tensor_tensor(ekey[:, :, :], ei[:, 2, :, :], float(KEY), ei[:, 1, :, :], ALU.mult, ALU.add).then_inc(S("edge_prep"), 1)
            V.tensor_copy(esrc[:, :, :], ei[:, 0, :, :]).then_inc(S("edge_prep"), 1)
            bv = [0]

            def bound(ins, wait=True):
                bv[0] += 1
                ins.then_inc(S("bound_val"), 1)
                if wait:
                    dve.wait_ge(S("bound_val"), bv[0])

            bound(V.tensor_reduce(emin[:, :], ei[:, 1, :, :], AX.X, ALU.min), False)
            bound(V.tensor_reduce(emax[:, :], ei[:, 1, :, :], AX.X, ALU.max), False)
            bound(V.tensor_copy(tn[:, :], tni[:, :]))
            bound(V.tensor_scalar(emin[:, :], emin[:, :], 1.0 - GW, None, ALU.add), False)
            bound(V.tensor_scalar(tnr[:, :], tn[:, :], -1.0, 400.0, ALU.mult, ALU.add))
            for b in range(EB):
                bound(V.tensor_scalar(ga[:, :], gb[:, :], emin[:, b:b + 1], None, ALU.is_ge))
                bound(V.scalar_tensor_tensor(ga[:, :], gb[:, :], emax[:, b:b + 1], ga[:, :], ALU.is_le, ALU.mult))
                bound(V.tensor_scalar(gv[:, b, 0, :], ga[:, :], tnr[:, b:b + 1], None, ALU.mult), False)
                bound(V.scalar_tensor_tensor(gv[:, b, 1, :], ga[:, :], tn[:, b:b + 1], ga[:, :], ALU.mult, ALU.add))
            assert bv[0] == N_BOUND
            dve.wait_ge(S("ln0_sd"), 1)
            V.reciprocal(lnrs[:, :], lnsd[:, :]).then_inc(S("ln0_rs"), 1)
            dve.wait_ge(S("ln0_rs"), 1)
            for t in range(T):
                V.tensor_scalar(xn[:, t, :], xn[:, t, :], lnmv[:, t, 0:1], lnrs[:, t:t + 1], ALU.subtract, ALU.mult).then_inc(S("xn_rows"), 1)
            dve.wait_ge(S("edge_T"), 1)
            V.tensor_copy(keyT[:, :], bank[4][:, 0:EB * P]).then_inc(S("edge_out"), 1)
            V.tensor_copy(srcT[:, :], bank[5][:, 0:EB * P]).then_inc(S("edge_out"), 1)
            dve.wait_ge(S("bound_T"), 1)
            V.reduce_max(gm[:, :], bank[6][0:2 * (G + 1), 0:EB * P], AX.X).then_inc(S("bound_max"), 1)
            dve.wait_ge(S("bound_T"), 2)
            V.tensor_scalar(gr[:, :], bank[7][0:1, 0:2 * (G + 1)], -1.0, 400.0, ALU.mult, ALU.add).then_inc(S("bound_row"), 1)
            dve.wait_ge(S("bound_row"), 1)
            V.tensor_scalar(bounds[:, 0:G + 1], gr[:, 0:G + 1], float(ETILES - 1), None, ALU.min)
            V.tensor_copy(bounds[:, G + 1:], bank[7][0:1, G + 1:2 * (G + 1)]).then_inc(S("bound_int"), 1)
            for t in range(T):
                dve.wait_ge(S("xhi_ready"), t + 1)
                V.scalar_tensor_tensor(xgst[:, t % 2, D:2 * D], xn[:, t, :], XSCALE, xgst[:, t % 2, 0:D],
                                       ALU.mult, ALU.subtract).then_inc(S("xlo_ready"), 1)

            n = dve.alloc_register("onehot_round")
            dve.reg_mov(n, 0)

            def onehots(g):
                lo = dve.value_load(bounds[0:1, bass.ds(g, 1)], min_val=0, max_val=ETILES)
                hi = dve.value_load(bounds[0:1, bass.ds(g + (G + 1), 1)], min_val=0, max_val=ETILES)
                m = dve.snap(n, min_val=0, max_val=G * 33)
                dve.wait_ge(S("oh_ready"), m * 2 + 2)
                V.tensor_scalar(iotaG[:, :], iotaK[:, :], gb[:, bass.ds(g, 1)], None, ALU.add).then_inc(S("iotaG_ready"), 1)
                with dve.Fori(lo, hi, ROUND) as tb:
                    m = dve.snap(n, min_val=0, max_val=G * 33)
                    for h in range(2):
                        dve.wait_ge(S("slots_used"), m * ROUND + HALF * (h + 1))
                        dve.wait_ge(S("iotaG_ready"), g + 1)
                        V.tensor_tensor(oh[:, h, :, :], iotaG[:, :].rearrange("p (o c) -> p o c", o=1).broadcast_to([P, HALF, P]),
                                        keyT[:, bass.ds(tb + HALF * h, HALF)].rearrange("p (k o) -> p k o", o=1).broadcast_to([P, HALF, P]),
                                        ALU.is_equal).then_inc(S("oh_ready"), 1)
                    dve.reg_add(n, n, 1)

            dve.wait_ge(S("edge_out"), 2)
            dve.wait_ge(S("bound_int"), 1)
            for k in range(2):
                dve.wait_ge(xg_stored[k], 16 * T // 2)
            dve.wait_ge(S("wT_ps"), 3 * C)
            dve.wait_ge(S("biases_loaded"), 16 * 11)
            onehots(0)

            def heads(v):
                return v[:, :].rearrange("p (h e) -> p h e", h=HEADS)

            def over(v):
                return v[:, :].rearrange("p (h o) -> p h o", o=1).broadcast_to([NT, HEADS, DH])

            def tail(i):
                dve.wait_ge(S("rel_done"), cur("rel_done", i))
                V.tensor_scalar(rdeg[:, :], DEG[:, 0:1], 1.0, None, ALU.max).then_inc(S("tail_step"), 1)
                dve.wait_ge(S("tail_step"), cur("tail_step", i, 2))
                V.reciprocal(rdeg[:, :], rdeg[:, :]).then_inc(S("tail_step"), 1)
                dve.wait_ge(S("tail_step"), cur("tail_step", i, 3))
                V.scalar_tensor_tensor(y1[:, :], AGG[0:NT, :], rdeg[:, 0:1], t1[:, :], ALU.mult, ALU.add).then_inc(S("y_ready"), 1)
                dve.wait_ge(S("y_ready"), cur("y_ready", i))
                V.bn_stats(st6[:, :], y1[:, :]).then_inc(S("tail_step"), 1)
                dve.wait_ge(S("tail_step"), cur("tail_step", i, 4))
                dve.sem_inc(S("dve_passed"), 1)
                V.bn_aggr(mv[:, :], st6[:, :]).then_inc(S("var_ready"), 1)
                dve.wait_ge(S("sd_ready"), cur("sd_ready", i))
                V.reciprocal(rs[:, :], sd[:, :]).then_inc(S("tail_step"), 1)
                dve.wait_ge(S("tail_step"), cur("tail_step", i, 5))
                V.tensor_scalar(y1[:, :], y1[:, :], mv[:, 0:1], rs[:, 0:1], ALU.subtract, ALU.mult).then_inc(S("tail_step"), 1)
                dve.wait_ge(S("tail_step"), cur("tail_step", i, 6))
                V.tensor_tensor(y1[:, :], y1[:, :], bcast["ln1_w"][:, :], ALU.mult).then_inc(S("tail_step"), 1)
                dve.wait_ge(S("tail_step"), cur("tail_step", i, 7))
                V.tensor_tensor(xn[:, bass.ds(i, 1), :].rearrange("p o f -> p (o f)"), y1[:, :], bcast["ln1_b"][:, :],
                                ALU.add).then_inc(S("x1_ready"), 1)

            def tile(i, first):
                def shifted(b, name, z, mx, k):
                    dve.wait_ge(S(name + "_ps"), cur(name + "_ps", i))
                    V.tensor_tensor(z[:, :], b[0:NT, :], bcast["b" + name][:, :], ALU.add).then_inc(S(name + "_biased"), 1)
                    dve.wait_ge(S(name + "_biased"), cur(name + "_biased", i))
                    V.reduce_max(mx[:, :], heads(z), AX.X).then_inc(S("soft_step"), 1)
                    dve.wait_ge(S("soft_step"), cur("soft_step", i, k))
                    V.tensor_tensor(heads(z), heads(z), over(mx), ALU.subtract).then_inc(S(name + "_shift"), 1)

                def normed(name, z, sm, k):
                    dve.wait_ge(S(name + "_exp"), cur(name + "_exp", i))
                    V.reduce_sum(sm[:, :], heads(z), AX.X).then_inc(S("soft_step"), 1)
                    dve.wait_ge(S("soft_step"), cur("soft_step", i, k))
                    V.reciprocal(sm[:, :], sm[:, :]).then_inc(S("soft_step"), 1)
                    dve.wait_ge(S("soft_step"), cur("soft_step", i, k + 1))
                    V.tensor_tensor(heads(z), heads(z), over(sm), ALU.mult).then_inc(S(name + "_soft"), 1)

                onehots(i * 4 + 1)
                onehots(i * 4 + 2)
                if not first:
                    tail(i - 1)
                onehots(i * 4 + 3)
                dve.wait_ge(S("qT_ps"), prev("qT_ps", i))
                shifted(QK[0], "q", qf, mxq, 1)
                dve.wait_ge(S("ctx_done"), prev("ctx_done", i))
                shifted(QK[1], "k", kf, mxk, 2)
                normed("q", qf, smq, 3)
                normed("k", kf, smk, 5)
                onehots(i * 4 + 4)
                dve.wait_ge(S("v_ps"), cur("v_ps", i))
                V.tensor_tensor(vf[:, :, 0:P], QK[0][0:NT, :].rearrange("p (a b) -> p a b", a=4),
                                bcast["bv"][:, :].rearrange("p (a b) -> p a b", a=4), ALU.add).then_inc(S("v_biased"), 1)
                dve.wait_ge(S("self_ps"), cur("self_ps", i))
                V.tensor_tensor(t1[:, :], QK[1][0:NT, :], bcast["self_b"][:, :], ALU.add).then_inc(S("self_added"), 1)
                dve.wait_ge(S("self_added"), cur("self_added", i))
                V.tensor_tensor(t1[:, :], t1[:, :], xn[:, bass.ds(i, 1), :].rearrange("p o f -> p (o f)"), ALU.add).then_inc(S("tail_step"), 1)
                dve.wait_ge(S("S_saved"), cur("S_saved", i, 8))
                V.transpose(cntT[:, :], cntb[:, :]).then_inc(S("cnt_ready"), 1)
                dve.wait_ge(S("cnt_ready"), cur("cnt_ready", i))
                V.tensor_tensor(A[:, :, :], gmask[:, :, :], cntT[:, :].rearrange("p (o d) -> p o d", o=1).broadcast_to([P, 4, GW]),
                                ALU.mult).then_inc(S("A_ready"), 1)

            tile(0, True)
            with dve.Fori(1, T) as i:
                tile(i, False)
            tail(T - 1)

            dve.wait_ge(S("ctx_done"), cur("ctx_done", T - 1))
            for pr in range(4):
                o = 130 * (pr % 2)
                V.tensor_tensor(ctxbd[:, pr, :], CTX[pr // 2][:, o:o + P], bmask[:, :], ALU.mult)
                last = V.tensor_scalar(ksumbd[:, pr, :], bmask[:, :], CTX[pr // 2][:, o + P:o + P + 1], None, ALU.mult)
            last.then_inc(S("ctx_bd_ready"), 1)

            def columns_lo(name, hi, lo, t):
                dve.wait_ge(S(name + "_hi"), t + 1)
                nodes = slice(t * NT, (t + 1) * NT)
                V.tensor_tensor(lo[:, :, nodes], bview(XB[t % 4], C, NT), f32(hi[:, :, nodes]), ALU.subtract).then_inc(S(name + "_lo"), 1)

            dve.wait_ge(S("x1_ready"), cur("x1_ready", T - 1))
            for t in range(T):
                columns_lo("x1c", x1h, x1l, t)

            def weights_lo(p, u, sl):
                for ci, (k0, k1) in enumerate(p.chunks):
                    dve.wait_ge(p.s("whi", sl), p.cur("whi", u, ci + 1))
                    source = TB[tb_of(p, sl, ci)][:, 0:(k1 - k0) * P] if p.transposed else p.raw[sl][:, 0:p.K * P]
                    V.tensor_tensor(p.l[sl][:, k0 * P:k1 * P], source, f32(p.h[sl][:, k0 * P:k1 * P]), ALU.subtract).then_inc(p.s("wlo", sl), 1)

            def quantise(p, u, sl):
                step = S("quant_step")
                at_step = lambda k: quant_at(p, u, sl, k)
                w, wq, K = p.raw[sl], p.q[sl], p.K
                groups = [(k, slice(k * P, (k + 1) * P)) for k in range(K)]
                dve.wait_ge(p.s("loaded", sl), p.cur("loaded", u))
                dve.wait_ge(p.s("wT", sl), p.prev("wT", u))
                dve.wait_ge(step, at_step(0))
                V.tensor_reduce(qs[:, 0, 0:K], w[:, 0:K * P].rearrange("p (k f) -> p k f", k=K), AX.X, ALU.add,
                                apply_absolute_value=True).then_inc(step, 1)
                dve.wait_ge(step, at_step(1))
                V.tensor_scalar(qs[:, 1, 0:K], qs[:, 0, 0:K], 1.0 / P, EPS, ALU.mult, ALU.add).then_inc(step, 1)
                dve.wait_ge(step, at_step(2))
                for n, m in enumerate((0.5, -0.5, -1.0)):
                    V.tensor_scalar(qs[:, 2 + n, 0:K], qs[:, 1, 0:K], m, None, ALU.mult).then_inc(step, 1)
                dve.wait_ge(step, at_step(5))
                for k, g in groups:
                    last = V.tensor_scalar(wq[:, g], w[:, g], qs[:, 2, k:k + 1], None, ALU.is_gt)
                last.then_inc(step, 1)
                dve.wait_ge(step, at_step(6))
                for k, g in groups:
                    last = V.scalar_tensor_tensor(wq[:, g], w[:, g], qs[:, 3, k:k + 1], wq[:, g], ALU.is_lt, ALU.subtract)
                last.then_inc(step, 1)
                dve.wait_ge(step, at_step(7))
                for k, g in groups:
                    last = V.scalar_tensor_tensor(wq[:, g], wq[:, g], qs[:, 4, k:k + 1], w[:, g], ALU.mult, ALU.subtract)
                last.then_inc(step, 1)

            def attention(u, ch):
                n0, n1 = CH[ch]
                w = n1 - n0
                dve.wait_ge(S("attn_ps"), 3 * u + (3 + ch + 1))
                dve.wait_ge(S("attn_full"), 3 * u + (ch + 1))
                V.reciprocal(at[:, 0:w], TB[0][:, 0:w]).then_inc(S("attn_rd"), 1)
                dve.wait_ge(S("attn_rd"), 3 * u + (ch + 1))
                V.tensor_tensor(at[:, 0:w], TB[1][:, 0:w], at[:, 0:w], ALU.mult).then_inc(S("attn_nd"), 1)
                dve.wait_ge(S("attn_nd"), 3 * u + (ch + 2))
                q = qT[:, bass.ds(u, 1), n0:n1].rearrange("p o n -> p (o n)")
                V.tensor_tensor(q, q, at[:, 0:n1 - n0], ALU.add).then_inc(S("attn_full"), 1)

            def results(p, u, sl):
                if p.mode == "gelu":
                    for ch in ((0,), (1, 2))[sl]:
                        attention(u, ch)
                elif p.mode == "gateup":
                    if sl == 0:
                        return
                    for ch, (n0, n1) in enumerate(CH):
                        w = n1 - n0
                        dve.wait_ge(p.s("used", 0), p.cur("used", u, ch + 1))
                        dve.wait_ge(p.s("mm", 1), p.cur("mm", u, ch + 1))
                        V.tensor_tensor(sg[ch][:, 0:w], MB[1][ch][:, 0:w], sg[ch][:, 0:w], ALU.mult).then_inc(p.s("used", 1), 1)
                else:
                    rows = xn if p.mode == "w2" else yx
                    for q, (t0, t1_) in enumerate(BACK):
                        dve.wait_ge(p.s("backT", sl), p.cur("backT", u, q + 1))
                        r = rows[:, t0:t1_, bass.ds((2 * u + sl) * P, P)]
                        V.tensor_tensor(r, r, TB[q % 2][0:NT, 0:(t1_ - t0) * P].rearrange("p (t f) -> p t f", f=P),
                                        ALU.add).then_inc(p.s("backed", sl), 1)

            def no_work(u, sl):
                pass

            def run(p, beside=no_work):
                weights_lo(p, 0, 0)

                def body(u, last):
                    weights_lo(p, u, 1)
                    if p.q and not last:
                        quantise(p, u + 1, 0)
                    beside(u, 0)
                    results(p, u, 0)
                    if not last:
                        weights_lo(p, u + 1, 0)
                        if p.q:
                            quantise(p, u + 1, 1)
                    beside(u, 1)
                    results(p, u, 1)
                if p.U > 2:
                    with dve.Fori(0, p.U - 1) as u:
                        body(u, False)
                else:
                    body(0, False)
                body(p.U - 1, True)

            lc = [0]

            def step(ins, wait=False):
                lc[0] += 1
                ins.then_inc(S("ln2_step"), 1)
                if wait:
                    dve.wait_ge(S("ln2_step"), lc[0])

            def add_ln2(t0, t1_):
                for t in range(t0, t1_):
                    dve.wait_ge(S("ln2_ready"), t + 1)
                    V.tensor_tensor(yx[:, t, :], yx[:, t, :], xn[:, t, :], ALU.add).then_inc(S("ln2_done"), 1)

            def beside_wp(u, sl):
                if (u, sl) == (0, 0):
                    for k in range(2):
                        dve.wait_ge(W2.s("backed", k), W2.cur("backed", W2.U - 1))
                    for t in range(T):
                        step(V.bn_stats(lnst[:, t, :], xn[:, t, :]), t == T - 1)
                    for t in range(T):
                        V.bn_aggr(lnmv[:, t, :], lnst[:, t, :]).then_inc(S("ln2_stats"), 1)
                    dve.wait_ge(S("ln2_sd"), 1)
                    step(V.reciprocal(lnrs[:, :], lnsd[:, :]), True)
                    V.scalar_tensor_tensor(lnsh[:, :], lnmv[:, :, 0], -1.0, lnrs[:, :], ALU.mult, ALU.mult).then_inc(S("ln2_shift"), 1)
                    dve.wait_ge(S("x_again"), 32)
                elif (u, sl) == (0, 1):
                    quantise(GU, 0, 0)
                elif (u, sl) == (1, 0):
                    for k in range(2):
                        dve.wait_ge(WP.s("backed", k), WP.cur("backed", 0))
                    add_ln2(0, LN2_HALF)
                    quantise(GU, 0, 1)
                else:
                    dve.wait_ge(WP.s("backed", 0), WP.cur("backed", 1))
                    add_ln2(LN2_HALF, T)
                    dve.wait_ge(S("ln2_done"), T)

            def beside_gu(u, sl):
                if sl == 0 and isinstance(u, int):
                    quantise(WD, 0, 0)

            run(W1)
            dve.wait_ge(S("b2_added"), T)
            run(W2)
            run(WP, beside_wp)

            for k in range(2):
                dve.wait_ge(WP.s("backed", k), WP.cur("backed", WP.U - 1))
            for t in range(T):
                step(V.bn_stats(lnst[:, t, :], yx[:, t, :]), t == T - 1)
            for t in range(T):
                V.bn_aggr(lnmv[:, t, :], lnst[:, t, :]).then_inc(S("ln3_stats"), 1)
            dve.wait_ge(S("ln3_sd"), 1)
            step(V.reciprocal(lnrs[:, :], lnsd[:, :]), True)

            def n3_rows(t):
                V.tensor_scalar(xn[:, t, :], yx[:, t, :], lnmv[:, t, 0:1], lnrs[:, t:t + 1],
                                ALU.subtract, ALU.mult).then_inc(S("n3_rows"), 1)

            for t in range(3):
                n3_rows(t)
            for t in range(T):
                if t + 3 < T:
                    n3_rows(t + 3)
                columns_lo("n3c", nh, nl, t)
            run(GU, beside_gu)
            for sl in range(2):
                dve.wait_ge(GU.s("mm", sl), GU.cur("mm", GU.U - 1))
            quantise(WD, 0, 1)
            run(WD)


INPUTS = ("x", "src", "dst", "edge_type_4", "L0_gnn_self_W", "L0_gnn_self_b", "L0_gnn_rel_W", "L0_gnn_rel_b", "L0_gnn_ln1_w",
          "L0_gnn_ln1_b", "L0_gnn_W1", "L0_gnn_b1", "L0_gnn_W2", "L0_gnn_b2", "L0_gnn_ln2_w", "L0_gnn_ln2_b", "L0_mix_Wq",
          "L0_mix_bq", "L0_mix_Wk", "L0_mix_bk", "L0_mix_Wv", "L0_mix_bv", "L0_mix_Wp", "L0_mix_bp", "L0_ffn_w_gate",
          "L0_ffn_w_up", "L0_ffn_w_down")


def kernel(**inputs):
    import concourse.bacc as bacc
    from concourse.bass_utils import run_bass_kernel_spmd

    nc = bacc.Bacc("TRN2", target_bir_lowering=False, num_devices=1)
    arrays, aps = {}, {}
    for name in INPUTS:
        v = np.ascontiguousarray(inputs[name])
        arrays[name] = v
        aps[name] = nc.dram_tensor(name, v.shape, mybir.dt.from_np(v.dtype), kind="ExternalInput").ap()
    out = nc.dram_tensor("out", (N, D), F32, kind="ExternalOutput").ap()
    program(nc, aps, out)
    r = run_bass_kernel_spmd(nc, [arrays], core_ids=[0])
    return r.results[0]["out"]
```

```python
from contextlib import ExitStack

import numpy as np
import concourse.bass as bass
from concourse import mybir

F32, F32R, F16, I32 = mybir.dt.float32, mybir.dt.float32r, mybir.dt.float16, mybir.dt.int32
ALU, ACT, AX = mybir.AluOpType, mybir.ActivationFunctionType, mybir.AxisListType

EPS = 1e-5
N, D, E, R, HEADS = 1250, 512, 40000, 4, 8
P = 128
T, NT = 10, 125
C = D // P
DH = D // HEADS
FF1, FFN = 2 * D, 1408
K1, KF = FF1 // P, FFN // P
GROUPS_PER_TILE, GW = 4, 32
G = T * GROUPS_PER_TILE
ETILES = (E + P - 1) // P
EB = (ETILES + P - 1) // P
ROUND, HALF = 10, 5
KEY = 2048
NO_DST = 4095.0
XSCALE = 1024.0
CH = [(0, 418), (418, 834), (834, 1250)]
CHW = 418


def program(nc, a, out):
    x, src, dst, typ = a["x"], a["src"], a["dst"], a["edge_type_4"]
    xg = nc.dram_tensor("xn_parts", (N, 2 * D), F16).ap()

    top = ExitStack()
    with top:
        def sem(name):
            return top.enter_context(nc.semaphore(name))

        def tensors(stack):
            return lambda name, shape, dt=F32: stack.enter_context(nc.sbuf_tensor(name, shape, dt))

        bank = [top.enter_context(nc.psum_tensor(f"bank{i}", [P, 512], F32)) for i in range(8)]

        sb = tensors(top)
        ident = sb("ident", [P, P])
        epsc = sb("epsc", [P, 1])
        bmask = sb("bmask", [P, P])
        st = ExitStack()
        sb = tensors(st)
        ctxbd = sb("ctxbd", [P, 4, P])
        ksumbd = sb("ksumbd", [P, 4, P])
        st.close()
        sb = tensors(top)
        wrawP = [sb(f"wrawP{s}", [P, C * P]) for s in range(2)]
        pair = sb("pair", [P, 2, P])
        b1c = sb("b1c", [P, K1])
        lnst = sb("lnst", [NT, T, 6])
        lnst4 = sb("lnst4", [NT, T, C, 6])
        lnmv = sb("lnmv", [NT, T, 2])
        lnsd = sb("lnsd", [NT, T])
        lnrs = sb("lnrs", [NT, T])
        st = ExitStack()
        sb = tensors(st)
        wrawA = [sb(f"wrawA{s}", [P, K1 * P]) for s in range(2)]
        tmpA = [sb(f"tmpA{s}", [P, CHW]) for s in range(2)]
        at = sb("at", [P, CHW])
        b2 = sb("b2", [NT, D])
        st.close()
        st = ExitStack()
        sb = tensors(st)
        wqkvl = [sb(f"wqkvl{c}", [P, 3, D], F32R) for c in range(C - 1)]
        xs = sb("xs", [NT, D])
        st.close()
        sb = tensors(top)
        yx = sb("yx", [NT, T, D])
        qs = sb("qs", [P, 5, KF])

        low = ExitStack()
        sb = tensors(low)
        xn = sb("xn", [NT, T, D])
        qT = sb("qT", [P, C, N])

        st = ExitStack()
        sb = tensors(st)
        wstage = sb("wstage", [P, 3, C, D])
        ei = sb("ei", [P, 3, EB, P], I32)
        ekey = sb("ekey", [P, EB, P])
        esrc = sb("esrc", [P, EB, P])
        emin = sb("emin", [P, EB])
        emax = sb("emax", [P, EB])
        gbi = sb("gbi", [P, G + 1], I32)
        tni = sb("tni", [P, EB], I32)
        tn = sb("tn", [P, EB])
        tnr = sb("tnr", [P, EB])
        ga = sb("ga", [P, G + 1])
        gv = sb("gv", [P, EB, 2, G + 1])
        gm = sb("gm", [2 * (G + 1), 1])
        gr = sb("gr", [1, 2 * (G + 1)])
        ikey = sb("ikey", [P, P], I32)
        gmi = sb("gmi", [P, 4, GW], I32)
        xgst = sb("xgst", [NT, T, 2 * D], F16)
        st.close()

        st = ExitStack()
        sb = tensors(st)
        ST = sb("ST", [P, C, R, P])
        S_sb = sb("S_sb", [P, 2, D])
        t1 = sb("t1", [NT, D])
        qf = sb("qf", [NT, D])
        kf = sb("kf", [NT, D])
        relW = sb("relW", [P, R * C, D])
        vf = sb("vf", [NT, 4, 130])
        ring = sb("ring", [P, ROUND, 2 * D], F16)
        wqkvh = sb("wqkvh", [P, C, 3, D], F32R)
        wqkvl.append(sb("wqkvl3", [P, 3, D], F32R))
        selfW = sb("selfW", [P, C, D])
        bcast = {n: sb("b_" + n, [NT, D]) for n in ("bq", "bk", "bv", "self_b", "ln1_w", "ln1_b")}
        relb = sb("relb", [P, D])
        xT = sb("xT", [P, C, NT])
        xTh = sb("xTh", [P, C, NT], F32R)
        xTl = sb("xTl", [P, C, NT], F32R)
        oh = sb("oh", [P, 2, HALF, P], F16)
        keyT = sb("keyT", [P, EB * P])
        srcT = sb("srcT", [P, EB * P], I32)
        idx = sb("idx", [P, 2, HALF], I32)
        gb = sb("gb", [P, G + 1])
        bounds = sb("bounds", [1, 2 * (G + 1)], I32)
        iotaK = sb("iotaK", [P, P])
        iotaG = sb("iotaG", [P, P])
        gmask = sb("gmask", [P, 4, GW])
        cntb = sb("cntb", [P, GW])
        cntT = sb("cntT", [P, GW])
        A = sb("A", [P, 4, GW])
        zero16 = sb("zero16", [P, D], F16)
        one16 = sb("one16", [P, 2], F16)
        ones = sb("ones", [P, 2])
        mxq = sb("mxq", [NT, HEADS])
        mxk = sb("mxk", [NT, HEADS])
        smq = sb("smq", [NT, HEADS])
        smk = sb("smk", [NT, HEADS])
        rdeg = sb("rdeg", [NT, 1])
        st6 = sb("st6", [NT, 6])
        mv = sb("mv", [NT, 2])
        sd = sb("sd", [NT, 1])
        rs = sb("rs", [NT, 1])
        st.close()

        st = ExitStack()
        sb = tensors(st)
        x1h = sb("x1h", [P, C, N], F32R)
        x1l = sb("x1l", [P, C, N], F32R)
        up = ExitStack()
        sb = tensors(up)
        gh = sb("gh", [P, K1, N], F32R)
        gl = sb("gl", [P, K1, N], F32R)
        whA = [sb(f"whA{s}", [P, K1 * P], F32R) for s in range(2)]
        wlA = [sb(f"wlA{s}", [P, K1 * P], F32R) for s in range(2)]
        outTA = sb("outTA", [P, N])
        up.close()
        sb = tensors(st)
        bcast2 = {n: sb("c_" + n, [NT, D]) for n in ("ln2_w", "ln2_b", "bp")}
        st.close()
        low.close()

        st = ExitStack()
        sb = tensors(st)
        hh = sb("hh", [P, KF, N], F32R)
        hl = sb("hl", [P, KF, N], F32R)
        up = ExitStack()
        sb = tensors(up)
        wrawF = [sb(f"wrawF{s}", [P, C * P]) for s in range(2)]
        wqF = [sb(f"wqF{s}", [P, C * P]) for s in range(2)]
        whF, wlF = [sb("whF0", [P, C * P], F32R)], [sb("wlF0", [P, C * P], F32R)]
        whF.append(sb("whF1", [P, C * P], F32R))
        wlF.append(sb("wlF1", [P, C * P], F32R))
        sg = [sb(f"sg{s}", [P, CHW]) for s in range(3)]
        nh = sb("nh", [P, C, N], F32R)
        nl = sb("nl", [P, C, N], F32R)
        wrawD0 = sb("wrawD0", [P, KF * P])
        wqD0 = sb("wqD0", [P, KF * P])
        up.close()
        sb = tensors(st)
        whD, wlD = [sb("whD0", [P, KF * P], F32R)], [sb("wlD0", [P, KF * P], F32R)]
        outTD = sb("outTD", [P, N])
        whD.append(sb("whD1", [P, KF * P], F32R))
        wlD.append(sb("wlD1", [P, KF * P], F32R))
        wrawD = [wrawD0, sb("wrawD1", [P, KF * P])]
        wqD = [wqD0, sb("wqD1", [P, KF * P])]
        st.close()

        N_CONSTS = 9
        QSTEPS = 8
        N_BOUND = 5 + 4 * EB

        s = {}

        def S(name):
            if name not in s:
                s[name] = sem(name)
            return s[name]

        xg_stored = [S("xg_stored0"), S("xg_stored1")]
        gathered = [S(f"gathered{k}") for k in range(ROUND)]

        PER_TILE = dict(
            xs_ready=1, xnT_ps=1, xT_ready=2, xTl_ready=1, q_ps=1, k_ps=1, v_ps=1, self_ps=1,
            q_biased=1, k_biased=1, v_biased=1, self_added=1, q_shift=1, k_shift=1, q_exp=1, k_exp=1,
            q_soft=1, k_soft=1, qT_ps=1, qT_saved=1, ctx_done=1,
            group_done=4, S_saved=8, ST_ps=4, ST_saved=4, cnt_ready=1, A_ready=1, rel_done=1, y_ready=1,
            var_ready=1, sd_ready=1, x1_ready=1, soft_step=6, tail_step=7)

        def cur(name, i, k=1):
            return PER_TILE[name] * (i + 1) + k

        def prev(name, i):
            return PER_TILE[name] * (i + 1)

        def start_credit(eng, names):
            for n in names:
                eng.sem_inc(S(n), PER_TILE[n])

        def transposes(dst_bank, src_of, n, rows, cols, width):
            for c in range(n):
                last = nc.tensor.transpose(dst_bank[0:cols, c * width:c * width + rows], src_of(c), ident[0:rows, 0:rows])
            return last

        def bview(b, n, w):
            return b[:, 0:n * w].rearrange("p (c w) -> p c w", c=n)

        TS, QK, SPS, AGG, CTX = bank[1], (bank[2], bank[3]), bank[4], bank[5], (bank[6], bank[7])
        TP = bank[0]
        SUMT = (TS, bank[3], TS, TS)
        CNT = bank[0][:, 504:505]
        DEG = bank[0][0:NT, 506:508]
        MARK = bank[0][:, 508:509]

        CREDIT = 4
        PASS_COUNTS = dict(loaded=0) | {k: CREDIT for k in ("whi", "wlo", "mm", "wT", "quant", "outT", "backT", "backed", "used")}

        class Pass:
            def __init__(self, name, U, K, src, raw, h, l, act, mode, q=None, outT=None):
                self.name, self.U, self.K, self.src, self.raw, self.h, self.l = name, U, K, src, raw, h, l
                self.act, self.mode, self.q, self.outT = act, mode, q, outT
                self.transposed = mode in ("gateup", "down", "mix")
                self.chunks = [(k, min(k + 4, K)) for k in range(0, K, 4)] if self.transposed else [(0, K)]
                self.back = mode in ("down", "mix", "w2")
                self.raw_free = "quant" if q else "wT" if self.transposed else "wlo"
                n = len(self.chunks)
                self.per = dict(loaded=16, whi=n, wlo=n, mm=3)
                self.per |= dict(wT=n) if self.transposed else {}
                self.per |= dict(quant=1) if q else {}
                self.per |= dict(outT=3, backT=3, backed=3) if self.back else dict(used=3)
                self.base = dict(PASS_COUNTS) | dict(loaded=0)
                for k, m in self.per.items():
                    PASS_COUNTS[k] += m * U

            def s(self, what, slot):
                return S(f"{self.name}_loaded{slot}" if what == "loaded" else f"pass_{what}{slot}")

            def cur(self, what, u, k=None):
                m = self.per[what]
                return u * m + (self.base[what] + (m if k is None else k))

            def prev(self, what, u):
                return u * self.per[what] + self.base[what]

        w1_src = lambda u, sl: a["L0_gnn_W1"].rearrange("(c p) f -> p c f", p=P)[:, :, bass.ds((2 * u + sl) * P, P)]
        w2_src = lambda u, sl: a["L0_gnn_W2"].rearrange("(c p) f -> p c f", p=P)[:, :, bass.ds((2 * u + sl) * P, P)]
        wp_src = lambda u, sl: a["L0_mix_Wp"][bass.ds((2 * u + sl) * P, P), :]
        gu_src = lambda u, sl: a[("L0_ffn_w_gate", "L0_ffn_w_up")[sl]][bass.ds(u * P, P), :]
        wd_src = lambda u, sl: a["L0_ffn_w_down"][bass.ds((2 * u + sl) * P, P), :]
        W1 = Pass("w1", 4, C, w1_src, wrawA, whA, wlA, (x1h, x1l), "gelu")
        W2 = Pass("w2", 2, K1, w2_src, wrawA, whA, wlA, (gh, gl), "w2", outT=outTA)
        WP = Pass("wp", 2, C, wp_src, wrawP, whA, wlA, (x1h, x1l), "mix", outT=outTA)
        GU = Pass("gu", KF, C, gu_src, wrawF, whF, wlF, (nh, nl), "gateup", q=wqF)
        WD = Pass("wd", 2, KF, wd_src, wrawD, whD, wlD, (hh, hl), "down", q=wqD, outT=outTD)
        TB = (bank[6], bank[7])
        XB = bank[3:6]
        MB = ((bank[0], bank[1], bank[2]), (bank[3], bank[4], bank[5]))

        PLO_W1 = 2 + 3 * 2 * W1.U
        ATTN_AT = [(0, 1), (1, 0), (1, 2)]

        def quant_at(p, u, sl, k):
            tiles_before = 2 * (p.base["quant"] - CREDIT)
            return u * (2 * QSTEPS) + ((tiles_before + sl + 1) * QSTEPS + k)

        def f32(v):
            return v.bitcast(F32)

        def pass_credit(eng, whats):
            for w in whats:
                for sl in range(2):
                    eng.sem_inc(S(f"pass_{w}{sl}"), CREDIT)

        CHAIN = [(p, u, sl) for p in (W2, WP) for u in range(p.U) for sl in range(2)]
        DOWN = [(WD, u, sl) for u in range(WD.U) for sl in range(2)]
        BACK = [(0, 4), (4, 8), (8, 10)]

        def tb_of(p, sl, ci):
            return (sl * len(p.chunks) + ci) % 2

        block = top.enter_context(nc.Block())

        @block.sync
        def _(sp):
            xv = x.rearrange("(t p) f -> p t f", p=NT)
            for h in range(2):
                ts = slice(h * T // 2, (h + 1) * T // 2)
                sp.dma_start(xn[0:112, ts, :], xv[0:112, ts, :]).then_inc(S(f"x_loaded{h}"), 16)
                sp.dma_start(xn[112:NT, ts, :], xv[112:NT, ts, :]).then_inc(S(f"x_loaded{h}"), 16)
            sp.wait_ge(S("epad"), 1)
            full = (EB - 1) * P
            rest = E // P - full
            for n, v in enumerate((src, dst, typ)):
                sp.dma_start(ei[:, n, 0:EB - 1, :], v[0:full * P].rearrange("(b t e) -> t b e", t=P, e=P)).then_inc(S("edges_loaded"), 16)
                sp.dma_start(ei[0:rest, n, EB - 1, :], v[full * P:(full + rest) * P].rearrange("(t e) -> t e", e=P)).then_inc(S("edges_loaded"), 16)
                sp.dma_start(ei[rest:rest + 1, n, EB - 1, 0:E % P], v[(full + rest) * P:E].rearrange("(t e) -> t e", t=1)).then_inc(S("edges_loaded"), 16)
            for n, m in enumerate(("q", "k", "v")):
                sp.dma_start(wstage[:, n, :, :], a["L0_mix_W" + m].rearrange("(b p) f -> p b f", p=P)).then_inc(S(f"w{m}_loaded"), 16)
            for n, v in (("bq", "L0_mix_bq"), ("bk", "L0_mix_bk"), ("bv", "L0_mix_bv"),
                         ("self_b", "L0_gnn_self_b"), ("ln1_w", "L0_gnn_ln1_w"), ("ln1_b", "L0_gnn_ln1_b")):
                sp.dma_start(bcast[n][:, :], a[v].rearrange("(o f) -> o f", o=1).broadcast_to([NT, D])).then_inc(S("biases_loaded"), 16)
            for r in range(R):
                sp.dma_start(relb[r * GW:(r + 1) * GW, :], a["L0_gnn_rel_b"][r:r + 1, :].broadcast_to([GW, D])).then_inc(S("biases_loaded"), 16)
            sp.dma_start(selfW[:, :, :], a["L0_gnn_self_W"].rearrange("(c p) f -> p c f", p=P)).then_inc(S("selfW_loaded"), 16)
            sp.dma_start(b1c[:, :], a["L0_gnn_b1"].rearrange("(c p) -> p c", p=P), allow_slow_non_contiguous=True).then_inc(S("biases_loaded"), 16)
            for h in range(2):
                ts = slice(h * T // 2, (h + 1) * T // 2)
                sp.wait_ge(S("xlo_ready"), (h + 1) * T // 2)
                sp.wait_ge(S("xhi_ready"), (h + 1) * T // 2)
                sp.dma_start(xg.rearrange("(t p) f -> p t f", p=NT)[:, ts, :], xgst[:, ts, :]).then_inc(xg_stored[h], 16)
            sp.wait_ge(S("wT_ps"), 3 * C)
            sp.wait_ge(S("bound_int"), 1)
            sp.wait_ge(S("edge_out"), 2)
            sp.wait_ge(S("consts_vec"), N_CONSTS)
            for k in range(2):
                sp.wait_ge(xg_stored[k], 16)
            for r in range(R):
                sp.wait_ge(S("group_done"), cur("group_done", 0, r + 1))
                sp.dma_start(relW[:, r * C:(r + 1) * C, :], a["L0_gnn_rel_W"][r].rearrange("(c p) f -> p c f", p=P)).then_inc(S("relW_loaded"), 16)

            def load(p, u, sl):
                sp.wait_ge(p.s(p.raw_free, sl), p.prev(p.raw_free, u))
                dst_ap = p.raw[sl][:, 0:p.K * P]
                if not p.transposed:
                    dst_ap = dst_ap.rearrange("p (k f) -> p k f", k=p.K)
                sp.dma_start(dst_ap, p.src(u, sl)).then_inc(p.s("loaded", sl), 16)

            def load_pass(p):
                with sp.Fori(0, p.U) as u:
                    for sl in range(2):
                        load(p, u, sl)

            def row(v):
                return a[v].rearrange("(o f) -> o f", o=1).broadcast_to([NT, D])

            sp.wait_ge(S("v_ps"), cur("v_ps", T - 1))
            sp.wait_ge(S("rel_done"), cur("rel_done", T - 2))
            sp.dma_start(b2[:, :], row("L0_gnn_b2")).then_inc(S("b2_loaded"), 16)
            load_pass(W1)
            load_pass(W2)
            sp.wait_ge(S("pair_ready"), W1.U)
            for sl in range(2):
                load(WP, 0, sl)
            for sl in range(2):
                sp.wait_ge(W2.s("wlo", sl), W2.cur("wlo", W2.U - 1))
            sp.dma_start(yx[0:112, :, :], xv[0:112, :, :]).then_inc(S("x_again"), 16)
            sp.dma_start(yx[112:NT, :, :], xv[112:NT, :, :]).then_inc(S("x_again"), 16)
            for sl in range(2):
                sp.wait_ge(W2.s("mm", sl), W2.cur("mm", W2.U - 1))
            for n in bcast2:
                sp.dma_start(bcast2[n][:, :], row("L0_mix_bp" if n == "bp" else "L0_gnn_" + n)).then_inc(S("bias2_loaded"), 16)
            for sl in range(2):
                load(WP, 1, sl)
            load_pass(GU)
            load(WD, 0, 0)
            for sl in range(2):
                sp.wait_ge(GU.s("mm", sl), GU.cur("mm", GU.U - 1))
            load(WD, 0, 1)
            for u in range(1, WD.U):
                for sl in range(2):
                    load(WD, u, sl)
            ov = out.rearrange("(t p) f -> p t f", p=NT)
            for o in range(2 * WD.U):
                sp.wait_ge(WD.s("backed", o % 2), WD.cur("backed", o // 2))
                sp.dma_start(ov[0:112, :, o * P:(o + 1) * P], yx[0:112, :, o * P:(o + 1) * P]).then_inc(S("out_stored"), 16)
                sp.dma_start(ov[112:NT, :, o * P:(o + 1) * P], yx[112:NT, :, o * P:(o + 1) * P]).then_inc(S("out_stored"), 16)
            sp.wait_ge(S("out_stored"), 16 * 4 * WD.U)


        @block.gpsimd
        def _(pool):
            pool.sem_inc(S("plo"), 2)
            pass_credit(pool, ["quant"])
            nc.gpsimd.memset(ident[:, :], 0.0).then_inc(S("consts_mem"), 1)
            nc.gpsimd.memset(bmask[:, :], 0.0).then_inc(S("consts_mem"), 1)
            pool.wait_ge(S("consts_mem"), 2)
            nc.gpsimd.affine_select(out=ident[:, :], in_=ident[:, :], compare_op=ALU.not_equal, fill=1.0, base=0,
                                    pattern=[[-1, P]], channel_multiplier=1).then_inc(S("consts_iota"), 1)
            nc.gpsimd.iota(gbi[:, 0:G], pattern=[[NT, T], [GW, 4]], base=0, channel_multiplier=0).then_inc(S("consts_iota"), 1)
            nc.gpsimd.memset(gbi[:, G:G + 1], N).then_inc(S("consts_iota"), 1)
            nc.gpsimd.iota(tni[:, :], pattern=[[P, EB]], base=0, channel_multiplier=1).then_inc(S("consts_iota"), 1)
            nc.gpsimd.iota(ikey[:, :], pattern=[[KEY, R], [1, GW]], base=0, channel_multiplier=0).then_inc(S("consts_iota"), 1)
            nc.gpsimd.iota(gmi[:, :, :], pattern=[[-1, 4], [0, GW]], base=0, channel_multiplier=1).then_inc(S("consts_iota"), 1)

            pool.wait_ge(S("bound_int"), 1)
            pool.wait_ge(S("edge_out"), 2)
            for k in range(2):
                pool.wait_ge(xg_stored[k], 16)
            n = pool.alloc_register("gather_round")
            pool.reg_mov(n, 0)
            with pool.Fori(0, G) as g:
                lo = pool.value_load(bounds[0:1, bass.ds(g, 1)], min_val=0, max_val=ETILES)
                hi = pool.value_load(bounds[0:1, bass.ds(g + (G + 1), 1)], min_val=0, max_val=ETILES)
                with pool.Fori(lo, hi, ROUND) as tb:
                    m = pool.snap(n, min_val=0, max_val=G * 33)
                    for h in range(2):
                        pool.wait_ge(S("slots_used"), m * ROUND + HALF * (h + 1))
                        nc.gpsimd.tensor_copy(idx[:, h, :], srcT[:, bass.ds(tb + HALF * h, HALF)]).then_inc(S("idx_ready"), 1)
                        pool.wait_ge(S("idx_ready"), m * 2 + (h + 1))
                        pool.sem_inc(S("pool_passed"), 1)
                        for k in range(HALF):
                            slot = HALF * h + k
                            nc.gpsimd.indirect_dma_start(
                                out=ring[:, slot, :], out_offset=None, in_=xg[:, :],
                                in_offset=bass.IndirectOffsetOnAxis(ap=idx[:, h, k:k + 1], axis=0)).then_inc(gathered[slot], 16)
                    pool.reg_add(n, n, 1)

            with pool.Fori(0, W1.U) as u:
                for sl in range(2):
                    for ch, (n0, n1) in enumerate(CH):
                        g = (bass.ds(2 * u + sl, 1), slice(n0, n1))
                        pool.wait_ge(S("phi"), 6 * u + (3 * sl + ch + 1))
                        nc.gpsimd.tensor_tensor(gl[:, g[0], g[1]].rearrange("p o n -> p (o n)"), tmpA[(3 * sl + ch) % 2][:, 0:n1 - n0],
                                         f32(gh[:, g[0], g[1]]).rearrange("p o n -> p (o n)"), ALU.subtract).then_inc(S("plo"), 1)
            pool.wait_ge(S("b2_loaded"), 16)
            pool.wait_ge(S("x1c_ps"), T)
            for t in range(T):
                nc.gpsimd.tensor_tensor(xn[:, t, :], xn[:, t, :], b2[:, :], ALU.add).then_inc(S("b2_added"), 1)
            for pr in range(C):
                pool.wait_ge(S("attn_hi"), pr + 1)
                nc.gpsimd.tensor_tensor(x1l[:, pr, :], qT[:, pr, :], f32(x1h[:, pr, :]), ALU.subtract).then_inc(S("attn_lo"), 1)
            pool.wait_ge(S("bias2_loaded"), 48)
            nc.gpsimd.tensor_tensor(bcast2["bp"][:, :], bcast2["bp"][:, :], bcast2["ln2_b"][:, :], ALU.add).then_inc(S("bias_sum"), 1)
            pool.wait_ge(S("bias_sum"), 1)

            def quantised(p, u, sl):
                pool.wait_ge(S("quant_step"), quant_at(p, u, sl, QSTEPS))
                w, wq = p.raw[sl][:, 0:p.K * P], p.q[sl][:, 0:p.K * P]
                nc.gpsimd.tensor_tensor(wq, wq, w, ALU.add).then_inc(p.s("quant", sl), 1)

            for t in range(T):
                pool.wait_ge(S("ln2_scaled"), t + 1)
                nc.gpsimd.tensor_tensor(xn[:, t, :], xn[:, t, :], bcast2["bp"][:, :], ALU.add).then_inc(S("ln2_ready"), 1)
            pool.wait_ge(S("x_again"), 32)
            pool.wait_ge(S("ln2_ready"), T)
            nc.gpsimd.tensor_tensor(yx[:, :, D // 2:D], yx[:, :, D // 2:D], xn[:, :, D // 2:D], ALU.add).then_inc(S("ln2_done"), 1)
            quantised(GU, 0, 0)
            quantised(GU, 0, 1)

            def gateup(u, last):
                if not last:
                    quantised(GU, u + 1, 0)
                    quantised(GU, u + 1, 1)
                else:
                    quantised(WD, 0, 0)
                for ch, (n0, n1) in enumerate(CH):
                    pool.wait_ge(S("sil"), 3 * u + (ch + 1))
                    nc.gpsimd.tensor_tensor(hl[:, bass.ds(u, 1), n0:n1].rearrange("p o n -> p (o n)"), sg[ch][:, 0:n1 - n0],
                                     f32(hh[:, bass.ds(u, 1), n0:n1]).rearrange("p o n -> p (o n)"), ALU.subtract).then_inc(S("plo"), 1)

            with pool.Fori(0, GU.U - 1) as u:
                gateup(u, False)
            gateup(GU.U - 1, True)
            quantised(WD, 0, 1)
            for u in range(1, WD.U):
                for sl in range(2):
                    quantised(WD, u, sl)

        @block.scalar
        def _(act):
            start_credit(act, ["xs_ready", "xT_ready", "q_exp", "k_exp", "qT_saved", "S_saved", "ST_saved", "sd_ready"])
            pass_credit(act, ["whi", "outT", "used"])
            act.wait_ge(S("ln0_stats"), T + 1)
            nc.scalar.activation(lnsd[:, :], lnmv[:, :, 1], ACT.Sqrt, bias=epsc[0:NT, 0:1]).then_inc(S("ln0_sd"), 1)

            def save_w(n, c):
                act.wait_ge(S("wT_ps"), n * C + c + 1)
                nc.scalar.copy(wqkvh[:, c, n, :], bank[(n * C + c) % 4][:, :]).then_inc(S("wT_saved"), 1)

            for c in range(C):
                save_w(0, c)
            for t in range(T):
                act.wait_ge(S("xn_rows"), t + 1)
                nc.scalar.activation(xgst[:, t, 0:D], xn[:, t, :], ACT.Identity, scale=XSCALE).then_inc(S("xhi_ready"), 1)
            for n in range(1, 3):
                for c in range(C):
                    save_w(n, c)

            def copy_rows(t):
                nc.scalar.copy(xs[:, :], xn[:, bass.ds(t, 1), :].rearrange("p o f -> p (o f)")).then_inc(S("xs_ready"), 1)

            def tail_sd(i):
                act.wait_ge(S("var_ready"), cur("var_ready", i))
                nc.scalar.activation(sd[:, :], mv[:, 1:2], ACT.Sqrt, bias=epsc[0:NT, 0:1]).then_inc(S("sd_ready"), 1)

            def tile(i, first):
                def save_S(j):
                    act.wait_ge(S("group_done"), cur("group_done", i, j + 1))
                    if j == 0:
                        act.wait_ge(S("cnt_ready"), prev("cnt_ready", i))
                    nc.scalar.copy(cntb[:, j:j + 1], CNT).then_inc(S("S_saved"), 1)
                    nc.scalar.activation(S_sb[:, j % 2, :], SPS[:, :], ACT.Copy, scale=1.0 / XSCALE).then_inc(S("S_saved"), 1)

                def save_ST(j):
                    act.wait_ge(S("ST_ps"), cur("ST_ps", i, j + 1))
                    nc.scalar.copy(ST[:, :, :, GW * j:GW * (j + 1)],
                                   SUMT[j][:, :].rearrange("p (c t d) -> p c t d", c=C, t=R)).then_inc(S("ST_saved"), 1)

                save_S(0)
                save_S(1)
                act.wait_ge(S("xnT_ps"), cur("xnT_ps", i))
                act.wait_ge(S("self_ps"), prev("self_ps", i))
                act.wait_ge(S("xTl_ready"), prev("xTl_ready", i))
                nc.scalar.copy(xT[:, :, :], bview(TP, C, NT)).then_inc(S("xT_ready"), 1)
                act.wait_ge(S("v_ps"), prev("v_ps", i))
                act.wait_ge(S("xT_ready"), cur("xT_ready", i, 1))
                nc.scalar.copy(xTh[:, :, :], xT[:, :, :]).then_inc(S("xT_ready"), 1)
                if not first:
                    act.wait_ge(S("rel_done"), cur("rel_done", i - 1))
                save_ST(0)
                save_ST(1)
                if not first:
                    tail_sd(i - 1)
                save_S(2)
                act.wait_ge(S("q_shift"), cur("q_shift", i))
                nc.scalar.activation(qf[:, :], qf[:, :], ACT.Exp).then_inc(S("q_exp"), 1)
                act.wait_ge(S("k_shift"), cur("k_shift", i))
                nc.scalar.activation(kf[:, :], kf[:, :], ACT.Exp).then_inc(S("k_exp"), 1)
                save_ST(2)
                save_S(3)
                act.wait_ge(S("qT_ps"), cur("qT_ps", i))
                nc.scalar.copy(qT[:, :, bass.ds(i * NT, NT)], bview(TP, C, NT)).then_inc(S("qT_saved"), 1)
                save_ST(3)

            copy_rows(0)
            tile(0, True)
            with act.Fori(1, T) as i:
                copy_rows(i)
                tile(i, False)
            tail_sd(T - 1)

            act.wait_ge(S("x1_ready"), cur("x1_ready", T - 1))
            act.wait_ge(S("rel_done"), cur("rel_done", T - 1))
            def weights_hi(p, u, sl):
                for ci, (k0, k1) in enumerate(p.chunks):
                    if p.transposed:
                        act.wait_ge(p.s("wT", sl), p.cur("wT", u, ci + 1))
                        source = TB[tb_of(p, sl, ci)][:, 0:(k1 - k0) * P]
                    else:
                        act.wait_ge(p.s("loaded", sl), p.cur("loaded", u))
                        source = p.raw[sl][:, 0:p.K * P]
                    if ci == 0:
                        act.wait_ge(p.s("mm", sl), p.prev("mm", u))
                    nc.scalar.copy(p.h[sl][:, k0 * P:k1 * P], source).then_inc(p.s("whi", sl), 1)

            def results(p, u, sl):
                for ch, (n0, n1) in enumerate(CH):
                    w = n1 - n0
                    if p.mode == "gelu":
                        act.wait_ge(p.s("mm", sl), p.cur("mm", u, ch + 1))
                        b = (3 * sl + ch) % 2
                        act.wait_ge(S("plo"), 6 * u + 3 * sl + ch + 1 )
                        act.sem_inc(S("act_passed"), 1)
                        nc.scalar.activation(tmpA[b][:, 0:w], MB[sl][ch][:, 0:w], ACT.Gelu,
                                             bias=b1c[:, bass.ds(2 * u + sl, 1)]).then_inc(p.s("used", sl), 1)
                        act.wait_ge(p.s("used", sl), p.cur("used", u, ch + 1))
                        nc.scalar.copy(gh[:, bass.ds(2 * u + sl, 1), n0:n1].rearrange("p o n -> p (o n)"), tmpA[b][:, 0:w]).then_inc(S("phi"), 1)
                    elif p.mode == "gateup":
                        if sl == 0:
                            act.wait_ge(p.s("mm", 0), p.cur("mm", u, ch + 1))
                            act.wait_ge(S("plo"), 3 * u + (PLO_W1 - 2 + ch))
                            nc.scalar.activation(sg[ch][:, 0:w], MB[0][ch][:, 0:w], ACT.Silu).then_inc(p.s("used", 0), 1)
                        else:
                            act.wait_ge(p.s("used", 1), p.cur("used", u, ch + 1))
                            nc.scalar.copy(hh[:, bass.ds(u, 1), n0:n1].rearrange("p o n -> p (o n)"), sg[ch][:, 0:w]).then_inc(S("sil"), 1)
                    else:
                        act.wait_ge(p.s("mm", sl), p.cur("mm", u, ch + 1))
                        if ch == 0:
                            if sl == 0:
                                act.wait_ge(p.s("backT", 1), p.prev("backT", u))
                            else:
                                act.wait_ge(p.s("backT", 0), p.cur("backT", u))
                        nc.scalar.copy(p.outT[:, n0:n1], MB[sl][ch][:, 0:w]).then_inc(p.s("outT", sl), 1)

            def no_work(p, u, sl):
                pass

            def run(p, following, behind=None):
                def body(u, last):
                    weights_hi(p, u, 1)
                    results(p, u, 0)
                    weights_hi(*(following if last else (p, u + 1, 0)))
                    results(p, u, 1)
                    if behind and not last:
                        behind(u + 1)
                with act.Fori(0, p.U - 1) as u:
                    body(u, False)
                body(p.U - 1, True)

            def chain(tiles, following=None, ahead=no_work, beside=no_work):
                for tile_, nxt in zip(tiles, tiles[1:] + [following]):
                    if nxt:
                        weights_hi(*nxt)
                    ahead(*tile_)
                    results(*tile_)
                    beside(*tile_)

            def pair_operands(u):
                act.wait_ge(S("attn_ps"), 3 * u + 3)
                nc.scalar.copy(pair[:, 0, :], ksumbd[:, bass.ds(u, 1), :].rearrange("p o f -> p (o f)"))
                nc.scalar.copy(pair[:, 1, :], ctxbd[:, bass.ds(u, 1), :].rearrange("p o f -> p (o f)")).then_inc(S("pair_ready"), 1)

            def attention_hi(u, sl):
                if (u, sl) == (0, 0):
                    act.wait_ge(S("attn_full"), 3 * C + 1)
                    for k in range(2):
                        act.wait_ge(W1.s("mm", k), W1.cur("mm", W1.U - 1))
                nc.scalar.copy(x1h[:, 2 * u + sl, :], qT[:, 2 * u + sl, :]).then_inc(S("attn_hi"), 1)

            def ahead_chain(p, u, sl):
                if p is W2:
                    attention_hi(u, sl)
                elif (u, sl) == (0, 0):
                    act.wait_ge(S("ln2_stats"), T)
                    nc.scalar.activation(lnsd[:, :], lnmv[:, :, 1], ACT.Sqrt, bias=epsc[0:NT, 0:1]).then_inc(S("ln2_sd"), 1)

            def beside_chain(p, u, sl):
                if p is WP and (u, sl) == (0, 0):
                    act.wait_ge(S("ln2_rs"), 1)
                    for t in range(T):
                        nc.scalar.activation(xn[:, t, :], xn[:, t, :], ACT.Copy, scale=lnrs[:, t:t + 1]).then_inc(S("ln2_scaled"), 1)

            weights_hi(W1, 0, 0)
            for t in range(T):
                if t == 4:
                    act.wait_ge(S("ctx_bd_ready"), 1)
                    pair_operands(0)
                act.wait_ge(S("x1c_ps"), t + 1)
                nc.scalar.copy(x1h[:, :, t * NT:(t + 1) * NT], bview(XB[t % 3], C, NT)).then_inc(S("x1c_hi"), 1)
            act.wait_ge(S("biases_loaded"), 16 * 11)
            run(W1, (W2, 0, 0), pair_operands)
            chain(CHAIN, (GU, 0, 0), ahead_chain, beside_chain)
            act.wait_ge(S("ln3_stats"), T)
            nc.scalar.activation(lnsd[:, :], lnmv[:, :, 1], ACT.Sqrt, bias=epsc[0:NT, 0:1]).then_inc(S("ln3_sd"), 1)
            for t in range(T):
                act.wait_ge(S("n3c_ps"), t + 1)
                nc.scalar.copy(nh[:, :, t * NT:(t + 1) * NT], bview(XB[t % 3], C, NT)).then_inc(S("n3c_hi"), 1)
            run(GU, (WD, 0, 0))
            chain(DOWN)

        @block.tensor
        def _(pe):
            pe.sem_inc(S("attn_ps"), 3)
            start_credit(pe, ["xnT_ps", "q_ps", "k_ps", "v_ps", "self_ps", "qT_ps", "ctx_done", "group_done", "ST_ps", "rel_done"])
            pe.sem_inc(S("slots_used"), ROUND)
            pass_credit(pe, ["mm", "wT", "backT"])
            pe.wait_ge(S("consts_iota"), 1)

            def weights_T(n):
                pe.wait_ge(S(f"w{'qkv'[n]}_loaded"), 16)
                for c in range(C):
                    k = n * C + c
                    if k >= 4:
                        pe.wait_ge(S("wT_saved"), k - 3)
                        pe.wait_ge(S("wTl_saved"), k - 3)
                    transposes(bank[k % 4], lambda b: wstage[:, n, b, c * P:(c + 1) * P], C, P, P, P).then_inc(S("wT_ps"), 1)

            weights_T(0)
            pe.wait_ge(S("edge_prep"), 2)
            transposes(bank[4], lambda b: ekey[:, b, :], EB, P, P, P)
            transposes(bank[5], lambda b: esrc[:, b, :], EB, P, P, P).then_inc(S("edge_T"), 1)
            pe.wait_ge(S("bound_val"), N_BOUND)
            W2G = 2 * (G + 1)
            transposes(bank[6], lambda b: gv[:, b, :, :].rearrange("p a g -> p (a g)"), EB, P, W2G, P).then_inc(S("bound_T"), 1)
            pe.wait_ge(S("bound_max"), 1)
            nc.tensor.transpose(bank[7][0:1, 0:W2G], gm[:, 0:1], ident[0:W2G, 0:W2G]).then_inc(S("bound_T"), 1)
            weights_T(1)
            weights_T(2)
            pe.wait_ge(S("consts_vec"), N_CONSTS)
            pe.wait_ge(S("bound_int"), 1)
            for b in CTX:
                nc.tensor.matmul(b[:, :], zero16[:, 0:P], zero16[:, :], start=True, stop=True, skip_group_check=True)
            pe.wait_ge(S("edge_out"), 2)
            pe.wait_ge(S("wT_saved"), 3 * C)
            pe.wait_ge(S("wTl_saved"), 3 * C)

            n = pe.alloc_register("agg_round")
            pe.reg_mov(n, 0)
            def relations(i, r0, r1):
                for r in range(r0, r1):
                    for c in range(C):
                        nc.tensor.matmul(AGG[0:NT, :], ST[:, c, r, 0:NT], relW[:, r * C + c, :], start=r + c == 0, stop=False)

            def relation_biases(i):
                pe.wait_ge(S("A_ready"), cur("A_ready", i))
                av = A[:, :, :].rearrange("p g d -> p (g d)")[:, 0:NT]
                nc.tensor.matmul(AGG[0:NT, :], av, relb[:, :], start=False, stop=True)
                nc.tensor.matmul(DEG, av, ones[:, :], start=True, stop=True, skip_group_check=True).then_inc(S("rel_done"), 1)

            def tile(i, first):
                def neighbours(j):
                    lo = pe.value_load(bounds[0:1, bass.ds(i * 4 + j, 1)], min_val=0, max_val=ETILES)
                    hi = pe.value_load(bounds[0:1, bass.ds(i * 4 + (j + G + 1), 1)], min_val=0, max_val=ETILES)
                    pe.wait_ge(S("S_saved"), 2 * (i * 4 + j) + 8)
                    nc.tensor.matmul(SPS[:, :], zero16[:, 0:P], zero16[:, :], start=True, stop=False, skip_group_check=True)
                    if j == 0:
                        pe.wait_ge(S("qT_saved"), prev("qT_saved", i))
                    if j == 2:
                        pe.wait_ge(S("xT_ready"), cur("xT_ready", i, 1))
                        if not first:
                            pe.wait_ge(S("y_ready"), cur("y_ready", i - 1))
                    nc.tensor.matmul(CNT, zero16[:, 0:P], zero16[:, 0:1], start=True, stop=False, skip_group_check=True)
                    with pe.Fori(lo, hi, ROUND) as tb:
                        m = pe.snap(n, min_val=0, max_val=G * 33)
                        for h in range(2):
                            pe.wait_ge(S("oh_ready"), m * 2 + (h + 3))
                            for k in range(HALF):
                                slot = HALF * h + k
                                pe.wait_ge(gathered[slot], m * 16 + 16)
                                nc.tensor.matmul(SPS[:, :], oh[:, h, k, :], ring[:, slot, 0:D], start=False, stop=False, skip_group_check=True)
                                nc.tensor.matmul(SPS[:, :], oh[:, h, k, :], ring[:, slot, D:2 * D], start=False, stop=False, skip_group_check=True)
                                nc.tensor.matmul(CNT, oh[:, h, k, :], one16[:, 0:1], start=False, stop=False,
                                                 skip_group_check=True).then_inc(S("slots_used"), 1)
                        pe.reg_add(n, n, 1)
                    nc.tensor.matmul(MARK, zero16[:, 0:P], zero16[:, 0:1], start=False, stop=True,
                                     skip_group_check=True).then_inc(S("group_done"), 1)

                def sums_T(j):
                    pe.wait_ge(S("S_saved"), 2 * (i * 4 + j) + 10)
                    transposes(SUMT[j], lambda c: S_sb[:, j % 2, c * P:(c + 1) * P], C, P, P, P).then_inc(S("ST_ps"), 1)

                def project(b, n, name):
                    for c in range(C):
                        for k, (xp, w) in enumerate(((xTh, wqkvh[:, c, n, :]), (xTl, wqkvh[:, c, n, :]), (xTh, wqkvl[c][:, n, :]))):
                            last = nc.tensor.matmul(b[0:NT, :], xp[:, c, :], w, start=c + k == 0, stop=c == C - 1 and k == 2)
                    last.then_inc(S(name), 1)

                def project_self(b):
                    for c in range(C):
                        last = nc.tensor.matmul(b[0:NT, :], xT[:, c, :], selfW[:, c, :], start=c == 0, stop=c == C - 1)
                    last.then_inc(S("self_ps"), 1)

                neighbours(0)
                if not first:
                    pe.wait_ge(S("ST_saved"), prev("ST_saved", i))
                    relations(i - 1, 0, R // 2)
                neighbours(1)
                pe.wait_ge(S("S_saved"), 2 * (i * 4 + 1) + 10)
                pe.wait_ge(S("xs_ready"), cur("xs_ready", i))
                transposes(TP, lambda c: xs[:, c * P:(c + 1) * P], C, NT, P, NT).then_inc(S("xnT_ps"), 1)
                if not first:
                    relations(i - 1, R // 2, R)
                    pe.wait_ge(S("xT_ready"), cur("xT_ready", i, 1))
                    relation_biases(i - 1)
                pe.wait_ge(S("ST_saved"), prev("ST_saved", i))
                sums_T(0)
                pe.wait_ge(S("self_added"), prev("self_added", i))
                sums_T(1)
                neighbours(2)
                pe.wait_ge(S("xT_ready"), cur("xT_ready", i, 2))
                pe.wait_ge(S("xTl_ready"), cur("xTl_ready", i))
                pe.wait_ge(S("v_biased"), prev("v_biased", i))
                project(QK[0], 0, "q_ps")
                pe.wait_ge(S("ST_saved"), cur("ST_saved", i, 2))
                project(QK[1], 1, "k_ps")
                sums_T(2)
                neighbours(3)
                pe.wait_ge(S("q_biased"), cur("q_biased", i))
                project(QK[0], 2, "v_ps")
                pe.wait_ge(S("q_soft"), cur("q_soft", i))
                pe.wait_ge(S("S_saved"), 2 * (i * 4 + 3) + 10)
                transposes(TP, lambda c: qf[:, c * P:(c + 1) * P], C, NT, P, NT).then_inc(S("qT_ps"), 1)
                pe.wait_ge(S("k_biased"), cur("k_biased", i))
                project_self(QK[1])
                pe.wait_ge(S("k_soft"), cur("k_soft", i))
                pe.wait_ge(S("v_biased"), cur("v_biased", i))
                for pr in range(4):
                    last = nc.tensor.matmul(CTX[pr // 2][:, 130 * (pr % 2):130 * (pr % 2) + 130], kf[:, pr * P:(pr + 1) * P], vf[:, pr, :],
                                            start=False, stop=True, skip_group_check=True)
                last.then_inc(S("ctx_done"), 1)
                pe.wait_ge(S("ST_saved"), cur("ST_saved", i, 3))
                sums_T(3)

            pe.wait_ge(S("selfW_loaded"), 16)
            tile(0, True)
            pe.wait_ge(S("relW_loaded"), 16 * R)
            pe.wait_ge(S("biases_loaded"), 16 * 11)
            with pe.Fori(1, T) as i:
                tile(i, False)
            pe.wait_ge(S("ST_saved"), cur("ST_saved", T - 1, 4))
            relations(T - 1, 0, R)
            relation_biases(T - 1)

            def to_columns(name, ready, ch):
                done = [-(-n1 // NT) for n0, n1 in CH]
                ahead = [min(T, t + len(XB)) for t in done]
                for t in range(ahead[ch - 1] if ch else 0, ahead[ch]):
                    ready(t)
                    if t >= 3:
                        pe.wait_ge(S(name + "_hi"), t - 2)
                        pe.wait_ge(S(name + "_lo"), t - 2)
                    transposes(XB[t % 3], lambda c: xn[:, t, c * P:(c + 1) * P], C, NT, P, NT).then_inc(S(name + "_ps"), 1)
                for part in ("_hi", "_lo"):
                    pe.wait_ge(S(name + part), done[ch])

            def weights_T2(p, u, sl, part, before=None):
                if not p.transposed:
                    return
                w = p.q if p.q else p.raw
                pe.wait_ge(p.s("quant", sl), p.cur("quant", u)) if p.q else pe.wait_ge(p.s("loaded", sl), p.cur("loaded", u))
                total = len(p.chunks)
                for ci, (k0, k1) in list(enumerate(p.chunks))[2 * part:2 * part + 2]:
                    b = sl * total + ci
                    back = b - 2
                    if back >= 0:
                        osl, oci, ou = back // total, back % total, u
                        pe.wait_ge(p.s("whi", osl), p.cur("whi", ou, oci + 1))
                        pe.wait_ge(p.s("wlo", osl), p.cur("wlo", ou, oci + 1))
                    else:
                        osl, oci = (back + 2 * total) // total, (back + 2 * total) % total
                        pe.wait_ge(p.s("whi", osl), p.cur("whi", u, oci + 1 - total))
                        pe.wait_ge(p.s("wlo", osl), p.cur("wlo", u, oci + 1 - total))
                    if before:
                        bp_, bu, bsl = before
                        pe.wait_ge(bp_.s("backed", bsl), bp_.cur("backed", bu))
                    last = transposes(TB[b % 2], lambda c: w[sl][:, (k0 + c) * P:(k0 + c + 1) * P], k1 - k0, P, P, P)
                    last.then_inc(p.s("wT", sl), 1)

            def attention(u, ch):
                n0, n1 = CH[ch]
                if ch == 0:
                    pe.wait_ge(S("pair_ready"), u + 1)
                pe.wait_ge(S("attn_nd"), 3 * u + (ch + 1))
                q = qT[:, bass.ds(u, 1), n0:n1].rearrange("p o n -> p (o n)")
                nc.tensor.matmul(TB[0][:, 0:n1 - n0], pair[:, 0, :], q, start=True, stop=True)
                nc.tensor.matmul(TB[1][:, 0:n1 - n0], pair[:, 1, :], q, start=True, stop=True).then_inc(S("attn_ps"), 1)

            def nothing(*_):
                pass

            def products(p, u, sl, before=nothing, amid=nothing, after=nothing):
                for ch, (n0, n1) in enumerate(CH):
                    before(ch)
                    w = n1 - n0
                    if ch == 0:
                        pe.wait_ge(p.s("whi", sl), p.cur("whi", u))
                        pe.wait_ge(p.s("wlo", sl), p.cur("wlo", u))
                    done = "outT" if p.back else "used"
                    pe.wait_ge(p.s(done, sl), p.cur(done, u, ch - 2))
                    k = 0
                    for kc in range(p.K):
                        ws = slice(kc * P, (kc + 1) * P)
                        for wgt, mov in ((p.h, p.act[0]), (p.h, p.act[1]), (p.l, p.act[0])):
                            last = nc.tensor.matmul(MB[sl][ch][:, 0:w], wgt[sl][:, ws], mov[:, kc, n0:n1],
                                                    start=k == 0, stop=k == 3 * p.K - 1)
                            k += 1
                        if kc == p.K // 2:
                            amid(ch)
                    last.then_inc(p.s("mm", sl), 1)
                    if p.mode == "gelu" and (sl, ch) in ATTN_AT:
                        attention(u, ATTN_AT.index((sl, ch)))
                    after(ch)

            def back(p, u, sl, part, weights):
                if part == 0:
                    pe.wait_ge(p.s("outT", sl), p.cur("outT", u))
                    if weights and weights[0].transposed:
                        wp_, wu, wsl = weights
                        pe.wait_ge(wp_.s("whi", wsl), wp_.cur("whi", wu))
                        pe.wait_ge(wp_.s("wlo", wsl), wp_.cur("wlo", wu))
                    if sl == 0:
                        pe.wait_ge(p.s("backed", 1), p.prev("backed", u))
                    else:
                        pe.wait_ge(p.s("backed", 0), p.cur("backed", u))
                else:
                    pe.wait_ge(p.s("backed", sl), p.cur("backed", u, 1))
                for q, (t0, t1_) in list(enumerate(BACK))[2 * part:2 * part + 2]:
                    for t in range(t0, t1_):
                        last = nc.tensor.transpose(TB[q % 2][0:NT, (t - t0) * P:(t - t0 + 1) * P],
                                                   p.outT[:, t * NT:(t + 1) * NT], ident[:, :])
                    last.then_inc(p.s("backT", sl), 1)

            def run(p, following, before):
                def weights_at(*tile_):
                    return dict(after=lambda ch: weights_T2(*tile_, 0) if ch == 1 else None,
                                amid=lambda ch: weights_T2(*tile_, 1) if ch == 2 else None)

                def body(u, last, before=nothing):
                    products(p, u, 0, before, **weights_at(p, u, 1))
                    products(p, u, 1, **weights_at(*(following if last else (p, u + 1, 0))))
                body(0, False, before)
                with pe.Fori(1, p.U - 1) as u:
                    body(u, False)
                body(p.U - 1, True)

            def chain(tiles, before, following=None):
                for i, tile_ in enumerate(tiles):
                    last_tile = tiles[i - 1] if i else None
                    nxt = tiles[i + 1] if i + 1 < len(tiles) else following

                    def amid(ch):
                        if ch == 1 and last_tile:
                            back(*last_tile, 1, tile_)
                        if ch == 2 and nxt:
                            weights_T2(*nxt, 1, last_tile)

                    def after(ch):
                        if ch == 0 and last_tile:
                            back(*last_tile, 0, tile_)
                        if ch == 1 and nxt:
                            weights_T2(*nxt, 0, last_tile)

                    products(*tile_, before[tile_[0]] if tile_[1:] == (0, 0) else nothing, amid, after)
                for part in range(2):
                    back(*tiles[-1], part, following)

            def before_w1(ch):
                to_columns("x1c", x1_tile_ready, ch)
                if ch == 1:
                    pe.wait_ge(S("ctx_bd_ready"), 1)

            def x1_tile_ready(t):
                pe.wait_ge(S("x1_ready"), cur("x1_ready", t))
                if t == 2:
                    pe.wait_ge(S("y_ready"), cur("y_ready", T - 1))

            def before_w2(ch):
                if ch == 2:
                    pe.wait_ge(S("attn_nd"), 3 * C + 1)
                pe.wait_ge(S("phi"), 3 * 2 * W1.U - 2 + ch)
                pe.wait_ge(S("plo"), PLO_W1 - 2 + ch)

            def before_wp(ch):
                if ch == 0:
                    pe.wait_ge(S("attn_hi"), C)
                    pe.wait_ge(S("attn_lo"), C)

            def before_gu(ch):
                to_columns("n3c", lambda t: pe.wait_ge(S("n3_rows"), t + 1), ch)

            def before_wd(ch):
                missing = 2 if ch == 0 else 0
                pe.wait_ge(S("sil"), 3 * GU.U - missing)
                pe.wait_ge(S("plo"), PLO_W1 + 3 * GU.U - missing)

            pe.wait_ge(S("v_biased"), cur("v_biased", T - 1))
            pe.wait_ge(S("self_added"), cur("self_added", T - 1))
            run(W1, (W2, 0, 0), before_w1)
            chain(CHAIN, {W2: before_w2, WP: before_wp}, (GU, 0, 0))
            run(GU, (WD, 0, 0), before_gu)
            chain(DOWN, {WD: before_wd})

        @block.vector
        def _(dve):
            V = nc.vector
            start_credit(dve, ["xTl_ready", "q_biased", "k_biased", "v_biased", "self_added", "q_shift", "k_shift", "q_soft", "k_soft",
                               "cnt_ready", "A_ready", "y_ready", "var_ready", "x1_ready", "soft_step", "tail_step"])
            dve.sem_inc(S("oh_ready"), 2)
            dve.sem_inc(S("attn_nd"), 1)
            dve.sem_inc(S("attn_full"), 1)
            dve.sem_inc(S("quant_step"), QSTEPS)
            pass_credit(dve, ["wlo", "backed"])

            V.memset(ei[:, 0, EB - 1, :], 0)
            V.memset(ei[:, 2, EB - 1, :], 0)
            V.memset(ei[:, 1, EB - 1, :], int(NO_DST)).then_inc(S("epad"), 1)

            V.memset(epsc[:, :], EPS)

            def const(ins):
                ins.then_inc(S("consts_vec"), 1)

            const(V.memset(zero16[:, :], 0.0))
            const(V.memset(one16[:, :], 1.0))
            const(V.memset(ones[:, :], 1.0))
            const(V.memset(cntb[:, :], 0.0))
            dve.wait_ge(S("consts_iota"), 6)
            const(V.tensor_copy(gb[:, :], gbi[:, :]))
            const(V.tensor_copy(iotaK[:, :], ikey[:, :]))
            const(V.tensor_copy(gmask[:, :, :], gmi[:, :, :]))
            dve.wait_ge(S("consts_vec"), 7)
            for q in range(4):
                quad = gmask[GW * q:GW * (q + 1), :, :]
                last = V.tensor_scalar(quad, quad, float(GW * q), None, ALU.is_equal)
            const(last)
            dve.wait_ge(S("consts_mem"), 2)
            V.memset(bmask[0:DH, 0:DH], 1.0)
            const(V.memset(bmask[DH:P, DH:P], 1.0))

            for t in range(T):
                if t % (T // 2) == 0:
                    dve.wait_ge(S(f"x_loaded{t // (T // 2)}"), 32)
                V.bn_stats(lnst[:, t, :], xn[:, t, :]).then_inc(S("ln0_stats"), 1)
            dve.wait_ge(S("ln0_stats"), T)
            for t in range(T):
                last = V.bn_aggr(lnmv[:, t, :], lnst[:, t, :])
            last.then_inc(S("ln0_stats"), 1)

            dve.wait_ge(S("edges_loaded"), 16 * 9)
            V.scalar_tensor_tensor(ekey[:, :, :], ei[:, 2, :, :], float(KEY), ei[:, 1, :, :], ALU.mult, ALU.add).then_inc(S("edge_prep"), 1)
            V.tensor_copy(esrc[:, :, :], ei[:, 0, :, :]).then_inc(S("edge_prep"), 1)
            bv = [0]

            def bound(ins, wait=True):
                bv[0] += 1
                ins.then_inc(S("bound_val"), 1)
                if wait:
                    dve.wait_ge(S("bound_val"), bv[0])

            bound(V.tensor_reduce(emin[:, :], ei[:, 1, :, :], AX.X, ALU.min), False)
            bound(V.tensor_reduce(emax[:, :], ei[:, 1, :, :], AX.X, ALU.max), False)
            bound(V.tensor_copy(tn[:, :], tni[:, :]))
            bound(V.tensor_scalar(emin[:, :], emin[:, :], 1.0 - GW, None, ALU.add), False)
            bound(V.tensor_scalar(tnr[:, :], tn[:, :], -1.0, 400.0, ALU.mult, ALU.add))
            for b in range(EB):
                bound(V.tensor_scalar(ga[:, :], gb[:, :], emin[:, b:b + 1], None, ALU.is_ge))
                bound(V.scalar_tensor_tensor(ga[:, :], gb[:, :], emax[:, b:b + 1], ga[:, :], ALU.is_le, ALU.mult))
                bound(V.tensor_scalar(gv[:, b, 0, :], ga[:, :], tnr[:, b:b + 1], None, ALU.mult), False)
                bound(V.scalar_tensor_tensor(gv[:, b, 1, :], ga[:, :], tn[:, b:b + 1], ga[:, :], ALU.mult, ALU.add))
            assert bv[0] == N_BOUND
            dve.wait_ge(S("ln0_sd"), 1)
            V.reciprocal(lnrs[:, :], lnsd[:, :]).then_inc(S("ln0_rs"), 1)
            dve.wait_ge(S("ln0_rs"), 1)
            for t in range(T):
                V.tensor_scalar(xn[:, t, :], xn[:, t, :], lnmv[:, t, 0:1], lnrs[:, t:t + 1], ALU.subtract, ALU.mult).then_inc(S("xn_rows"), 1)
            dve.wait_ge(S("edge_T"), 1)
            V.tensor_copy(keyT[:, :], bank[4][:, 0:EB * P]).then_inc(S("edge_out"), 1)
            V.tensor_copy(srcT[:, :], bank[5][:, 0:EB * P]).then_inc(S("edge_out"), 1)
            dve.wait_ge(S("bound_T"), 1)
            V.reduce_max(gm[:, :], bank[6][0:2 * (G + 1), 0:EB * P], AX.X).then_inc(S("bound_max"), 1)
            dve.wait_ge(S("bound_T"), 2)
            V.tensor_scalar(gr[:, :], bank[7][0:1, 0:2 * (G + 1)], -1.0, 400.0, ALU.mult, ALU.add).then_inc(S("bound_row"), 1)
            dve.wait_ge(S("bound_row"), 1)
            V.tensor_scalar(bounds[:, 0:G + 1], gr[:, 0:G + 1], float(ETILES - 1), None, ALU.min)
            V.tensor_copy(bounds[:, G + 1:], bank[7][0:1, G + 1:2 * (G + 1)]).then_inc(S("bound_int"), 1)
            for t in range(T):
                dve.wait_ge(S("xhi_ready"), t + 1)
                V.scalar_tensor_tensor(xgst[:, t, D:2 * D], xn[:, t, :], XSCALE, xgst[:, t, 0:D],
                                       ALU.mult, ALU.subtract).then_inc(S("xlo_ready"), 1)

            for n in range(3):
                for c in range(C):
                    dve.wait_ge(S("wT_saved"), n * C + c + 1)
                    V.tensor_tensor(wqkvl[c][:, n, :], bank[(n * C + c) % 4][:, :], f32(wqkvh[:, c, n, :]),
                                    ALU.subtract).then_inc(S("wTl_saved"), 1)

            n = dve.alloc_register("onehot_round")
            dve.reg_mov(n, 0)

            def onehots(g):
                lo = dve.value_load(bounds[0:1, bass.ds(g, 1)], min_val=0, max_val=ETILES)
                hi = dve.value_load(bounds[0:1, bass.ds(g + (G + 1), 1)], min_val=0, max_val=ETILES)
                m = dve.snap(n, min_val=0, max_val=G * 33)
                dve.wait_ge(S("oh_ready"), m * 2 + 2)
                V.tensor_scalar(iotaG[:, :], iotaK[:, :], gb[:, bass.ds(g, 1)], None, ALU.add).then_inc(S("iotaG_ready"), 1)
                with dve.Fori(lo, hi, ROUND) as tb:
                    m = dve.snap(n, min_val=0, max_val=G * 33)
                    for h in range(2):
                        dve.wait_ge(S("slots_used"), m * ROUND + HALF * (h + 1))
                        dve.wait_ge(S("iotaG_ready"), g + 1)
                        V.tensor_tensor(oh[:, h, :, :], iotaG[:, :].rearrange("p (o c) -> p o c", o=1).broadcast_to([P, HALF, P]),
                                        keyT[:, bass.ds(tb + HALF * h, HALF)].rearrange("p (k o) -> p k o", o=1).broadcast_to([P, HALF, P]),
                                        ALU.is_equal).then_inc(S("oh_ready"), 1)
                    dve.reg_add(n, n, 1)

            dve.wait_ge(S("edge_out"), 2)
            dve.wait_ge(S("bound_int"), 1)
            for k in range(2):
                dve.wait_ge(xg_stored[k], 16)
            dve.wait_ge(S("wT_ps"), 3 * C)
            dve.wait_ge(S("biases_loaded"), 16 * 11)
            V.memset(vf[:, :, P:130], 1.0)
            onehots(0)

            def heads(v):
                return v[:, :].rearrange("p (h e) -> p h e", h=HEADS)

            def over(v):
                return v[:, :].rearrange("p (h o) -> p h o", o=1).broadcast_to([NT, HEADS, DH])

            def tail(i):
                dve.wait_ge(S("rel_done"), cur("rel_done", i))
                V.tensor_scalar(rdeg[:, :], DEG[:, 0:1], 1.0, None, ALU.max).then_inc(S("tail_step"), 1)
                dve.wait_ge(S("tail_step"), cur("tail_step", i, 2))
                V.reciprocal(rdeg[:, :], rdeg[:, :]).then_inc(S("tail_step"), 1)
                dve.wait_ge(S("tail_step"), cur("tail_step", i, 3))
                V.scalar_tensor_tensor(t1[:, :], AGG[0:NT, :], rdeg[:, 0:1], t1[:, :], ALU.mult, ALU.add).then_inc(S("y_ready"), 1)
                dve.wait_ge(S("y_ready"), cur("y_ready", i))
                V.bn_stats(st6[:, :], t1[:, :]).then_inc(S("tail_step"), 1)
                dve.wait_ge(S("tail_step"), cur("tail_step", i, 4))
                dve.sem_inc(S("dve_passed"), 1)
                V.bn_aggr(mv[:, :], st6[:, :]).then_inc(S("var_ready"), 1)
                dve.wait_ge(S("sd_ready"), cur("sd_ready", i))
                V.reciprocal(rs[:, :], sd[:, :]).then_inc(S("tail_step"), 1)
                dve.wait_ge(S("tail_step"), cur("tail_step", i, 5))
                V.tensor_scalar(t1[:, :], t1[:, :], mv[:, 0:1], rs[:, 0:1], ALU.subtract, ALU.mult).then_inc(S("tail_step"), 1)
                dve.wait_ge(S("tail_step"), cur("tail_step", i, 6))
                V.tensor_tensor(t1[:, :], t1[:, :], bcast["ln1_w"][:, :], ALU.mult).then_inc(S("tail_step"), 1)
                dve.wait_ge(S("tail_step"), cur("tail_step", i, 7))
                V.tensor_tensor(xn[:, bass.ds(i, 1), :].rearrange("p o f -> p (o f)"), t1[:, :], bcast["ln1_b"][:, :],
                                ALU.add).then_inc(S("x1_ready"), 1)

            def tile(i, first):
                def shifted(b, name, z, mx, k):
                    dve.wait_ge(S(name + "_ps"), cur(name + "_ps", i))
                    V.tensor_tensor(z[:, :], b[0:NT, :], bcast["b" + name][:, :], ALU.add).then_inc(S(name + "_biased"), 1)
                    dve.wait_ge(S(name + "_biased"), cur(name + "_biased", i))
                    V.reduce_max(mx[:, :], heads(z), AX.X).then_inc(S("soft_step"), 1)
                    dve.wait_ge(S("soft_step"), cur("soft_step", i, k))
                    V.tensor_tensor(heads(z), heads(z), over(mx), ALU.subtract).then_inc(S(name + "_shift"), 1)

                def normed(name, z, sm, k):
                    dve.wait_ge(S(name + "_exp"), cur(name + "_exp", i))
                    V.reduce_sum(sm[:, :], heads(z), AX.X).then_inc(S("soft_step"), 1)
                    dve.wait_ge(S("soft_step"), cur("soft_step", i, k))
                    V.reciprocal(sm[:, :], sm[:, :]).then_inc(S("soft_step"), 1)
                    dve.wait_ge(S("soft_step"), cur("soft_step", i, k + 1))
                    V.tensor_tensor(heads(z), heads(z), over(sm), ALU.mult).then_inc(S(name + "_soft"), 1)

                onehots(i * 4 + 1)
                onehots(i * 4 + 2)
                if not first:
                    tail(i - 1)
                dve.wait_ge(S("v_ps"), prev("v_ps", i))
                dve.wait_ge(S("xT_ready"), cur("xT_ready", i, 2))
                V.tensor_tensor(xTl[:, :, :], xT[:, :, :], f32(xTh[:, :, :]), ALU.subtract).then_inc(S("xTl_ready"), 1)
                onehots(i * 4 + 3)
                dve.wait_ge(S("qT_ps"), prev("qT_ps", i))
                shifted(QK[0], "q", qf, mxq, 1)
                dve.wait_ge(S("ctx_done"), prev("ctx_done", i))
                shifted(QK[1], "k", kf, mxk, 2)
                normed("q", qf, smq, 3)
                normed("k", kf, smk, 5)
                onehots(i * 4 + 4)
                dve.wait_ge(S("v_ps"), cur("v_ps", i))
                V.tensor_tensor(vf[:, :, 0:P], QK[0][0:NT, :].rearrange("p (a b) -> p a b", a=4),
                                bcast["bv"][:, :].rearrange("p (a b) -> p a b", a=4), ALU.add).then_inc(S("v_biased"), 1)
                dve.wait_ge(S("self_ps"), cur("self_ps", i))
                if not first:
                    dve.wait_ge(S("x1_ready"), cur("x1_ready", i - 1))
                V.tensor_tensor(t1[:, :], QK[1][0:NT, :], bcast["self_b"][:, :], ALU.add).then_inc(S("self_added"), 1)
                dve.wait_ge(S("self_added"), cur("self_added", i))
                V.tensor_tensor(t1[:, :], t1[:, :], xn[:, bass.ds(i, 1), :].rearrange("p o f -> p (o f)"), ALU.add).then_inc(S("tail_step"), 1)
                dve.wait_ge(S("S_saved"), cur("S_saved", i, 8))
                V.transpose(cntT[:, :], cntb[:, :]).then_inc(S("cnt_ready"), 1)
                dve.wait_ge(S("cnt_ready"), cur("cnt_ready", i))
                V.tensor_tensor(A[:, :, :], gmask[:, :, :], cntT[:, :].rearrange("p (o d) -> p o d", o=1).broadcast_to([P, 4, GW]),
                                ALU.mult).then_inc(S("A_ready"), 1)

            tile(0, True)
            with dve.Fori(1, T) as i:
                tile(i, False)
            tail(T - 1)

            def columns_lo(name, hi, lo, t):
                dve.wait_ge(S(name + "_hi"), t + 1)
                nodes = slice(t * NT, (t + 1) * NT)
                V.tensor_tensor(lo[:, :, nodes], bview(XB[t % 3], C, NT), f32(hi[:, :, nodes]), ALU.subtract).then_inc(S(name + "_lo"), 1)

            def weights_lo(p, u, sl):
                for ci, (k0, k1) in enumerate(p.chunks):
                    dve.wait_ge(p.s("whi", sl), p.cur("whi", u, ci + 1))
                    source = TB[tb_of(p, sl, ci)][:, 0:(k1 - k0) * P] if p.transposed else p.raw[sl][:, 0:p.K * P]
                    V.tensor_tensor(p.l[sl][:, k0 * P:k1 * P], source, f32(p.h[sl][:, k0 * P:k1 * P]), ALU.subtract).then_inc(p.s("wlo", sl), 1)

            def quantise(p, u, sl, stages=(0, 1, 2)):
                step = S("quant_step")
                at_step = lambda k: quant_at(p, u, sl, k)
                w, wq, K = p.raw[sl], p.q[sl], p.K
                groups = [(k, slice(k * P, (k + 1) * P)) for k in range(K)]
                if 0 in stages:
                    scales_and_sign(p, u, sl)
                if 1 in stages:
                    dve.wait_ge(step, at_step(6))
                    for k, g in groups:
                        last = V.scalar_tensor_tensor(wq[:, g], w[:, g], qs[:, 3, k:k + 1], wq[:, g], ALU.is_lt, ALU.subtract)
                    last.then_inc(step, 1)
                if 2 in stages:
                    dve.wait_ge(step, at_step(7))
                    for k, g in groups:
                        last = V.scalar_tensor_tensor(wq[:, g], wq[:, g], qs[:, 4, k:k + 1], w[:, g], ALU.mult, ALU.subtract)
                    last.then_inc(step, 1)

            def scales_and_sign(p, u, sl):
                step = S("quant_step")
                at_step = lambda k: quant_at(p, u, sl, k)
                w, wq, K = p.raw[sl], p.q[sl], p.K
                groups = [(k, slice(k * P, (k + 1) * P)) for k in range(K)]
                dve.wait_ge(p.s("loaded", sl), p.cur("loaded", u))
                if not (isinstance(u, int) and u == 0):
                    dve.wait_ge(p.s("wT", sl), p.prev("wT", u))
                dve.wait_ge(step, at_step(0))
                V.tensor_reduce(qs[:, 0, 0:K], w[:, 0:K * P].rearrange("p (k f) -> p k f", k=K), AX.X, ALU.add,
                                apply_absolute_value=True).then_inc(step, 1)
                dve.wait_ge(step, at_step(1))
                V.tensor_scalar(qs[:, 1, 0:K], qs[:, 0, 0:K], 1.0 / P, EPS, ALU.mult, ALU.add).then_inc(step, 1)
                dve.wait_ge(step, at_step(2))
                for n, m in enumerate((0.5, -0.5, -1.0)):
                    V.tensor_scalar(qs[:, 2 + n, 0:K], qs[:, 1, 0:K], m, None, ALU.mult).then_inc(step, 1)
                dve.wait_ge(step, at_step(5))
                for k, g in groups:
                    last = V.tensor_scalar(wq[:, g], w[:, g], qs[:, 2, k:k + 1], None, ALU.is_gt)
                last.then_inc(step, 1)

            def attention(u, ch):
                n0, n1 = CH[ch]
                w = n1 - n0
                dve.wait_ge(S("attn_ps"), 3 * u + (3 + ch + 1))
                dve.wait_ge(S("attn_full"), 3 * u + (ch + 1))
                V.reciprocal(at[:, 0:w], TB[0][:, 0:w]).then_inc(S("attn_rd"), 1)
                dve.wait_ge(S("attn_rd"), 3 * u + (ch + 1))
                V.tensor_tensor(at[:, 0:w], TB[1][:, 0:w], at[:, 0:w], ALU.mult).then_inc(S("attn_nd"), 1)
                dve.wait_ge(S("attn_nd"), 3 * u + (ch + 2))
                q = qT[:, bass.ds(u, 1), n0:n1].rearrange("p o n -> p (o n)")
                V.tensor_tensor(q, q, at[:, 0:n1 - n0], ALU.add).then_inc(S("attn_full"), 1)

            def results(p, u, sl):
                if p.mode == "gelu":
                    for ch in ((0,), (1, 2))[sl]:
                        attention(u, ch)
                elif p.mode == "gateup":
                    if sl == 0:
                        return
                    for ch, (n0, n1) in enumerate(CH):
                        w = n1 - n0
                        dve.wait_ge(p.s("used", 0), p.cur("used", u, ch + 1))
                        dve.wait_ge(p.s("mm", 1), p.cur("mm", u, ch + 1))
                        V.tensor_tensor(sg[ch][:, 0:w], MB[1][ch][:, 0:w], sg[ch][:, 0:w], ALU.mult).then_inc(p.s("used", 1), 1)
                else:
                    rows = xn if p.mode == "w2" else yx
                    for q, (t0, t1_) in enumerate(BACK):
                        dve.wait_ge(p.s("backT", sl), p.cur("backT", u, q + 1))
                        r = rows[:, t0:t1_, bass.ds((2 * u + sl) * P, P)]
                        V.tensor_tensor(r, r, TB[q % 2][0:NT, 0:(t1_ - t0) * P].rearrange("p (t f) -> p t f", f=P),
                                        ALU.add).then_inc(p.s("backed", sl), 1)

            def no_work(p, u, sl):
                pass

            def run(p, following):
                def body(u, last):
                    if p.q:
                        quantise(*following, (1,)) if last else quantise(p, u + 1, 0)
                    weights_lo(p, u, 1)
                    results(p, u, 0)
                    if p.q:
                        quantise(*following, (2,)) if last else quantise(p, u + 1, 1)
                    weights_lo(*(following if last else (p, u + 1, 0)))
                    results(p, u, 1)
                with dve.Fori(0, p.U - 1) as u:
                    body(u, False)
                if p.q:
                    quantise(*following, (0,))
                body(p.U - 1, True)

            def chain(tiles, following=None, ahead=no_work, beside=no_work):
                for tile_, nxt in zip(tiles, tiles[1:] + [following]):
                    if nxt:
                        weights_lo(*nxt)
                    ahead(*tile_)
                    results(*tile_)
                    beside(*tile_)

            lc = [0]

            def step(ins, wait=False):
                lc[0] += 1
                ins.then_inc(S("ln2_step"), 1)
                if wait:
                    dve.wait_ge(S("ln2_step"), lc[0])

            def chunk_stats(p, u, sl, rows):
                c = 2 * u + sl
                dve.wait_ge(p.s("backed", sl), p.cur("backed", u))
                for t in range(T):
                    step(V.bn_stats(lnst4[:, t, c, :], rows[:, t, c * P:(c + 1) * P]), c == C - 1 and t == T - 1)

            def aggregate(name):
                for t in range(T):
                    V.bn_aggr(lnmv[:, t, :], lnst4[:, t, :, :]).then_inc(S(name), 1)

            def ahead_chain(p, u, sl):
                if p is WP and (u, sl) == (0, 0):
                    dve.wait_ge(S("bias2_loaded"), 48)
                    dve.wait_ge(S("ln2_stats"), T)
                    for t in range(T):
                        V.scalar_tensor_tensor(xn[:, t, :], xn[:, t, :], lnmv[:, t, 0:1], bcast2["ln2_w"][:, :],
                                               ALU.subtract, ALU.mult).then_inc(S("ln2_weighted"), 1)
                    dve.wait_ge(S("ln2_sd"), 1)
                    dve.wait_ge(S("ln2_weighted"), T)
                    V.reciprocal(lnrs[:, :], lnsd[:, :]).then_inc(S("ln2_rs"), 1)
                    dve.wait_ge(S("x_again"), 32)

            def beside_chain(p, u, sl):
                if p is W2:
                    chunk_stats(W2, u, sl, xn)
                    if (u, sl) == (W2.U - 1, 1):
                        aggregate("ln2_stats")
                elif (u, sl) == (0, 0):
                    quantise(GU, 0, 0)
                    quantise(GU, 0, 1)
                elif (u, sl) == (0, 1):
                    for k in range(2):
                        dve.wait_ge(WP.s("backed", k), WP.cur("backed", 0))
                    dve.wait_ge(S("ln2_ready"), T)
                    V.tensor_tensor(yx[:, :, 0:D // 2], yx[:, :, 0:D // 2], xn[:, :, 0:D // 2], ALU.add).then_inc(S("ln2_done"), 1)
                    dve.wait_ge(S("ln2_done"), 2)
                    chunk_stats(WP, 0, 0, yx)
                elif (u, sl) == (1, 0):
                    for c in range(1, C - 1):
                        chunk_stats(WP, c // 2, c % 2, yx)
                else:
                    chunk_stats(WP, u, sl, yx)

            dve.wait_ge(S("x1_ready"), cur("x1_ready", T - 1))
            weights_lo(W1, 0, 0)
            for t in range(4):
                columns_lo("x1c", x1h, x1l, t)
            dve.wait_ge(S("ctx_done"), cur("ctx_done", T - 1))
            for pr in range(4):
                o = 130 * (pr % 2)
                V.tensor_tensor(ctxbd[:, pr, :], CTX[pr // 2][:, o:o + P], bmask[:, :], ALU.mult)
                last = V.tensor_scalar(ksumbd[:, pr, :], bmask[:, :], CTX[pr // 2][:, o + P:o + P + 1], None, ALU.mult)
            last.then_inc(S("ctx_bd_ready"), 1)
            for t in range(4, T):
                columns_lo("x1c", x1h, x1l, t)
            run(W1, (W2, 0, 0))
            dve.wait_ge(S("b2_added"), T)
            chain(CHAIN, (GU, 0, 0), ahead_chain, beside_chain)

            aggregate("ln3_stats")
            dve.wait_ge(S("ln3_sd"), 1)
            step(V.reciprocal(lnrs[:, :], lnsd[:, :]), True)

            def n3_rows(t):
                V.tensor_scalar(xn[:, t, :], yx[:, t, :], lnmv[:, t, 0:1], lnrs[:, t:t + 1],
                                ALU.subtract, ALU.mult).then_inc(S("n3_rows"), 1)

            for t in range(3):
                n3_rows(t)
            for t in range(T):
                if t + 3 < T:
                    n3_rows(t + 3)
                columns_lo("n3c", nh, nl, t)
            run(GU, (WD, 0, 0))
            for sl in range(2):
                dve.wait_ge(GU.s("mm", sl), GU.cur("mm", GU.U - 1))
            quantise(WD, 0, 1)
            chain(DOWN, ahead=lambda p, u, sl: quantise(p, u + 1, sl) if u + 1 < p.U else None)


INPUTS = ("x", "src", "dst", "edge_type_4", "L0_gnn_self_W", "L0_gnn_self_b", "L0_gnn_rel_W", "L0_gnn_rel_b", "L0_gnn_ln1_w",
          "L0_gnn_ln1_b", "L0_gnn_W1", "L0_gnn_b1", "L0_gnn_W2", "L0_gnn_b2", "L0_gnn_ln2_w", "L0_gnn_ln2_b", "L0_mix_Wq",
          "L0_mix_bq", "L0_mix_Wk", "L0_mix_bk", "L0_mix_Wv", "L0_mix_bv", "L0_mix_Wp", "L0_mix_bp", "L0_ffn_w_gate",
          "L0_ffn_w_up", "L0_ffn_w_down")


def kernel(**inputs):
    import concourse.bacc as bacc
    from concourse.bass_utils import run_bass_kernel_spmd

    nc = bacc.Bacc("TRN2", target_bir_lowering=False, num_devices=1)
    arrays, aps = {}, {}
    for name in INPUTS:
        v = np.ascontiguousarray(inputs[name])
        arrays[name] = v
        aps[name] = nc.dram_tensor(name, v.shape, mybir.dt.from_np(v.dtype), kind="ExternalInput").ap()
    out = nc.dram_tensor("out", (N, D), F32, kind="ExternalOutput").ap()
    program(nc, aps, out)
    r = run_bass_kernel_spmd(nc, [arrays], core_ids=[0])
    return r.results[0]["out"]
```
